# Optimizing a Trainium2 kernel written in Bass

```python
import numpy as np
import jax
import jax.numpy as jnp

def _softmax(x, axis=-1):
    return jax.nn.softmax(x, axis=axis)

def _gelu(x):
    return jax.nn.gelu(x, approximate=True)

def _silu(x):
    return jax.nn.silu(x)

def _sigmoid(x):
    return jax.nn.sigmoid(x)

def _layernorm(x, axis=-1, eps=1e-05):
    m = jnp.mean(x, axis=axis, keepdims=True)
    v = jnp.var(x, axis=axis, keepdims=True)
    return (x - m) / jnp.sqrt(v + eps)

def _scatter_add(tgt, idx, src, axis=0):
    return tgt.at[idx].add(src)

def _segment_sum(src, seg, n):
    return jax.ops.segment_sum(src, seg, n)
kernel_name = 'mk_seq_preln_d2_jaxref_r8_bae24b'

def setup_inputs(seed: int=0):
    np.random.seed(seed)
    _w = jnp.asarray

    def _L0_attn_setup():
        import jax, jax.numpy as jnp
        import numpy as np
        D_MODEL = 128
        NUM_HEADS = 16
        D_K = D_MODEL // NUM_HEADS
        BATCH, SEQ = (2, 256)
        key = jax.random.key(seed)
        k = jax.random.split(key, 5)
        std = np.sqrt(2.0 / (D_MODEL + D_MODEL)).astype(np.float32)
        return {'x': jax.random.normal(k[0], (BATCH, SEQ, D_MODEL), dtype=jnp.float32), 'WQ': jax.random.normal(k[1], (D_MODEL, D_MODEL), dtype=jnp.float32) * std, 'WK': jax.random.normal(k[2], (D_MODEL, D_MODEL), dtype=jnp.float32) * std, 'WV': jax.random.normal(k[3], (D_MODEL, D_MODEL), dtype=jnp.float32) * std, 'WO': jax.random.normal(k[4], (D_MODEL, D_MODEL), dtype=jnp.float32) * std}
    _L0_attn_in = _L0_attn_setup()

    def _L0_ffn_setup():
        import jax, jax.numpy as jnp
        import numpy as np
        DIM = 128
        N_EXPERTS = 8
        TOPK = 2
        CAPACITY_FACTOR = 1.25
        B, S = (2, 256)

        def _moe(x, Wr, W1, b1, W2, b2):
            Bsz, Sl, D = x.shape
            E = Wr.shape[1]
            T = Bsz * Sl
            capacity = max(1, int(T * CAPACITY_FACTOR / E))
            xt = x.reshape(T, D)
            probs_full = jax.nn.softmax(xt @ Wr, axis=-1)
            topv, topi = jax.lax.top_k(probs_full, TOPK)
            topv = topv / jnp.sum(topv, axis=-1, keepdims=True)
            onehot = jax.nn.one_hot(topi, E, dtype=x.dtype)
            rank = jnp.cumsum(onehot, axis=0)
            keep = (rank <= capacity).astype(x.dtype) * onehot
            w = jnp.einsum('tk,tke->te', topv, keep)
            h = jax.nn.gelu(jnp.einsum('td,edf->etf', xt, W1) + b1[:, None, :], approximate=False)
            y = jnp.einsum('etf,efd->etd', h, W2) + b2[:, None, :]
            out = jnp.einsum('te,etd->td', w, y)
            return out.reshape(Bsz, Sl, D)
        key = jax.random.key(seed)
        ks = jax.random.split(key, 6)
        D, E, F = (DIM, N_EXPERTS, 4 * DIM)
        x = jax.random.normal(ks[0], (B, S, D), dtype=jnp.float32)
        Wr = jax.random.normal(ks[1], (D, E), dtype=jnp.float32) * (1.0 / np.sqrt(D))
        W1 = jax.random.normal(ks[2], (E, D, F), dtype=jnp.float32) * (1.0 / np.sqrt(D))
        b1 = jnp.zeros((E, F), dtype=jnp.float32)
        W2 = jax.random.normal(ks[3], (E, F, D), dtype=jnp.float32) * (1.0 / np.sqrt(F))
        b2 = jnp.zeros((E, D), dtype=jnp.float32)
        return {'x': x, 'Wr': Wr, 'W1': W1, 'b1': b1, 'W2': W2, 'b2': b2}
    _L0_ffn_in = _L0_ffn_setup()

    def _L1_attn_setup():
        import jax, jax.numpy as jnp
        import numpy as np
        D_MODEL = 128
        H = 16
        DH = 64
        EPS = 1e-05

        def _layernorm(x, g, b):
            mu = jnp.mean(x, axis=-1, keepdims=True)
            var = jnp.var(x, axis=-1, keepdims=True)
            return (x - mu) * jax.lax.rsqrt(var + EPS) * g + b
        key = jax.random.key(seed)
        ks = jax.random.split(key, 16)
        B, L = (4, 512)
        s = 0.02
        inp = {'x': jax.random.normal(ks[0], (B, L, D_MODEL), jnp.float32), 'ln1_g': jnp.ones((D_MODEL,), jnp.float32), 'ln1_b': jnp.zeros((D_MODEL,), jnp.float32), 'Wq': jax.random.normal(ks[1], (D_MODEL, H * DH), jnp.float32) * s, 'bq': jnp.zeros((H * DH,), jnp.float32), 'Wk': jax.random.normal(ks[2], (D_MODEL, H * DH), jnp.float32) * s, 'bk': jnp.zeros((H * DH,), jnp.float32), 'Wv': jax.random.normal(ks[3], (D_MODEL, H * DH), jnp.float32) * s, 'bv': jnp.zeros((H * DH,), jnp.float32), 'Wg': jax.random.normal(ks[4], (D_MODEL, H * DH), jnp.float32) * s, 'bg': jnp.zeros((H * DH,), jnp.float32), 'decay_logit': jnp.zeros((H,), jnp.float32), 'Wo': jax.random.normal(ks[5], (H * DH, D_MODEL), jnp.float32) * s, 'bo': jnp.zeros((D_MODEL,), jnp.float32), 'ln2_g': jnp.ones((D_MODEL,), jnp.float32), 'ln2_b': jnp.zeros((D_MODEL,), jnp.float32), 'W1': jax.random.normal(ks[6], (D_MODEL, 4 * D_MODEL), jnp.float32) * s, 'b1': jnp.zeros((4 * D_MODEL,), jnp.float32), 'W2': jax.random.normal(ks[7], (4 * D_MODEL, D_MODEL), jnp.float32) * s, 'b2': jnp.zeros((D_MODEL,), jnp.float32)}
        return inp
    _L1_attn_in = _L1_attn_setup()

    def _L1_ffn_setup():
        import jax, jax.numpy as jnp
        import numpy as np
        D_IN, D_HID = (128, 512)

        def _ternary(key, shape):
            return jax.random.randint(key, shape, -1, 2).astype(jnp.float32)

        def _tlin(x, w, s):
            return jnp.einsum('bsi,oi->bso', x, w) * s
        key = jax.random.key(seed)
        ks = jax.random.split(key, 12)
        inv = lambda fan: 1.0 / np.sqrt(fan).astype(np.float32)
        return {'x': jax.random.normal(ks[0], (4, 256, D_IN), dtype=jnp.float32), 'w1_w': _ternary(ks[1], (D_HID, D_IN)), 'w1_s': jax.random.uniform(ks[2], (D_HID,), dtype=jnp.float32) * inv(D_IN), 'w2_w': _ternary(ks[3], (D_HID, D_IN)), 'w2_s': jax.random.uniform(ks[4], (D_HID,), dtype=jnp.float32) * inv(D_IN), 'h1_w': _ternary(ks[5], (D_HID, D_HID)), 'h1_s': jax.random.uniform(ks[6], (D_HID,), dtype=jnp.float32) * inv(D_HID), 'h2_w': _ternary(ks[7], (D_HID, D_HID)), 'h2_s': jax.random.uniform(ks[8], (D_HID,), dtype=jnp.float32) * inv(D_HID), 'w3_w': _ternary(ks[9], (D_IN, D_HID)), 'w3_s': jax.random.uniform(ks[10], (D_IN,), dtype=jnp.float32) * inv(D_HID)}
    _L1_ffn_in = _L1_ffn_setup()
    _d = {'L0_attn_x': _L0_attn_in['x'], 'L0_attn_WQ': _L0_attn_in['WQ'], 'L0_attn_WK': _L0_attn_in['WK'], 'L0_attn_WV': _L0_attn_in['WV'], 'L0_attn_WO': _L0_attn_in['WO'], 'L0_ffn_Wr': _L0_ffn_in['Wr'], 'L0_ffn_W1': _L0_ffn_in['W1'], 'L0_ffn_b1': _L0_ffn_in['b1'], 'L0_ffn_W2': _L0_ffn_in['W2'], 'L0_ffn_b2': _L0_ffn_in['b2'], 'L1_attn_ln1_g': _L1_attn_in['ln1_g'], 'L1_attn_ln1_b': _L1_attn_in['ln1_b'], 'L1_attn_Wq': _L1_attn_in['Wq'], 'L1_attn_bq': _L1_attn_in['bq'], 'L1_attn_Wk': _L1_attn_in['Wk'], 'L1_attn_bk': _L1_attn_in['bk'], 'L1_attn_Wv': _L1_attn_in['Wv'], 'L1_attn_bv': _L1_attn_in['bv'], 'L1_attn_Wg': _L1_attn_in['Wg'], 'L1_attn_bg': _L1_attn_in['bg'], 'L1_attn_decay_logit': _L1_attn_in['decay_logit'], 'L1_attn_Wo': _L1_attn_in['Wo'], 'L1_attn_bo': _L1_attn_in['bo'], 'L1_attn_ln2_g': _L1_attn_in['ln2_g'], 'L1_attn_ln2_b': _L1_attn_in['ln2_b'], 'L1_attn_W1': _L1_attn_in['W1'], 'L1_attn_b1': _L1_attn_in['b1'], 'L1_attn_W2': _L1_attn_in['W2'], 'L1_attn_b2': _L1_attn_in['b2'], 'L1_ffn_w1_w': _L1_ffn_in['w1_w'], 'L1_ffn_w1_s': _L1_ffn_in['w1_s'], 'L1_ffn_w2_w': _L1_ffn_in['w2_w'], 'L1_ffn_w2_s': _L1_ffn_in['w2_s'], 'L1_ffn_h1_w': _L1_ffn_in['h1_w'], 'L1_ffn_h1_s': _L1_ffn_in['h1_s'], 'L1_ffn_h2_w': _L1_ffn_in['h2_w'], 'L1_ffn_h2_s': _L1_ffn_in['h2_s'], 'L1_ffn_w3_w': _L1_ffn_in['w3_w'], 'L1_ffn_w3_s': _L1_ffn_in['w3_s']}
    _x0 = _d['L0_attn_x']
    _d['L0_attn_x'] = jax.random.normal(jax.random.fold_in(jax.random.key(seed), 1), (4, 512, 128), dtype=_x0.dtype)
    del _x0
    return _d

def reference(L0_attn_x, L0_attn_WQ, L0_attn_WK, L0_attn_WV, L0_attn_WO, L0_ffn_Wr, L0_ffn_W1, L0_ffn_b1, L0_ffn_W2, L0_ffn_b2, L1_attn_ln1_g, L1_attn_ln1_b, L1_attn_Wq, L1_attn_bq, L1_attn_Wk, L1_attn_bk, L1_attn_Wv, L1_attn_bv, L1_attn_Wg, L1_attn_bg, L1_attn_decay_logit, L1_attn_Wo, L1_attn_bo, L1_attn_ln2_g, L1_attn_ln2_b, L1_attn_W1, L1_attn_b1, L1_attn_W2, L1_attn_b2, L1_ffn_w1_w, L1_ffn_w1_s, L1_ffn_w2_w, L1_ffn_w2_s, L1_ffn_h1_w, L1_ffn_h1_s, L1_ffn_h2_w, L1_ffn_h2_s, L1_ffn_w3_w, L1_ffn_w3_s):

    def _L0_attn_ref(x, WQ, WK, WV, WO):
        import jax, jax.numpy as jnp
        import numpy as np
        D_MODEL = 128
        NUM_HEADS = 16
        D_K = D_MODEL // NUM_HEADS
        BATCH, SEQ = (2, 256)
        B, S, E = x.shape
        mask = jnp.where(jnp.triu(jnp.ones((S, S), dtype=bool), k=1), -jnp.inf, 0.0).astype(x.dtype)

        def heads(W):
            return (x @ W).reshape(B, S, NUM_HEADS, D_K).transpose(0, 2, 1, 3)
        Q, K, V = (heads(WQ), heads(WK), heads(WV))
        score = jnp.einsum('bhqd,bhkd->bhqk', Q, K) / jnp.sqrt(jnp.asarray(D_K, x.dtype))
        score = score + mask
        score = score - jnp.max(score, axis=-1, keepdims=True)
        score = jnp.exp(score)
        score = score / jnp.sum(score, axis=-1, keepdims=True)
        out = jnp.einsum('bhqk,bhkd->bhqd', score, V)
        out = out.transpose(0, 2, 1, 3).reshape(B, S, E)
        return out @ WO

    def _L0_ffn_ref(x, Wr, W1, b1, W2, b2):
        import jax, jax.numpy as jnp
        import numpy as np
        DIM = 128
        N_EXPERTS = 8
        TOPK = 2
        CAPACITY_FACTOR = 1.25
        B, S = (2, 256)

        def _moe(x, Wr, W1, b1, W2, b2):
            Bsz, Sl, D = x.shape
            E = Wr.shape[1]
            T = Bsz * Sl
            capacity = max(1, int(T * CAPACITY_FACTOR / E))
            xt = x.reshape(T, D)
            probs_full = jax.nn.softmax(xt @ Wr, axis=-1)
            topv, topi = jax.lax.top_k(probs_full, TOPK)
            topv = topv / jnp.sum(topv, axis=-1, keepdims=True)
            onehot = jax.nn.one_hot(topi, E, dtype=x.dtype)
            rank = jnp.cumsum(onehot, axis=0)
            keep = (rank <= capacity).astype(x.dtype) * onehot
            w = jnp.einsum('tk,tke->te', topv, keep)
            h = jax.nn.gelu(jnp.einsum('td,edf->etf', xt, W1) + b1[:, None, :], approximate=False)
            y = jnp.einsum('etf,efd->etd', h, W2) + b2[:, None, :]
            out = jnp.einsum('te,etd->td', w, y)
            return out.reshape(Bsz, Sl, D)
        return _moe(x, Wr, W1, b1, W2, b2)

    def _L1_attn_ref(x, ln1_g, ln1_b, Wq, bq, Wk, bk, Wv, bv, Wg, bg, decay_logit, Wo, bo, ln2_g, ln2_b, W1, b1, W2, b2):
        import jax, jax.numpy as jnp
        import numpy as np
        D_MODEL = 128
        H = 16
        DH = 64
        EPS = 1e-05

        def _layernorm(x, g, b):
            mu = jnp.mean(x, axis=-1, keepdims=True)
            var = jnp.var(x, axis=-1, keepdims=True)
            return (x - mu) * jax.lax.rsqrt(var + EPS) * g + b
        B, L, _ = x.shape
        y = _layernorm(x, ln1_g, ln1_b)

        def proj(W, b):
            return (y @ W + b).reshape(B, L, H, DH).transpose(1, 0, 2, 3)
        q = proj(Wq, bq)
        k = proj(Wk, bk)
        v = proj(Wv, bv)
        g = jax.nn.sigmoid(y @ Wg + bg).reshape(B, L, H, DH).transpose(1, 0, 2, 3)
        decay = jax.nn.sigmoid(decay_logit)[None, :, None]
        scale = DH ** (-0.5)

        def step(state, qkvg):
            q_t, k_t, v_t, g_t = qkvg
            state = decay * state + k_t * v_t
            out_t = g_t * q_t * state * scale
            return (state, out_t)
        state0 = jnp.zeros((B, H, DH), x.dtype)
        _, outs = jax.lax.scan(step, state0, (q, k, v, g))
        o = outs.transpose(1, 0, 2, 3).reshape(B, L, H * DH) @ Wo + bo
        x2 = x + o
        h = _layernorm(x2, ln2_g, ln2_b)
        ff = jax.nn.gelu(h @ W1 + b1, approximate=False) @ W2 + b2
        return x2 + ff

    def _L1_ffn_ref(x, w1_w, w1_s, w2_w, w2_s, h1_w, h1_s, h2_w, h2_s, w3_w, w3_s):
        import jax, jax.numpy as jnp
        import numpy as np
        D_IN, D_HID = (128, 512)

        def _ternary(key, shape):
            return jax.random.randint(key, shape, -1, 2).astype(jnp.float32)

        def _tlin(x, w, s):
            return jnp.einsum('bsi,oi->bso', x, w) * s
        h = jax.nn.silu(_tlin(x, w1_w, w1_s)) * _tlin(x, w2_w, w2_s)
        h = jax.nn.gelu(_tlin(h, h1_w, h1_s), approximate=False)
        h = jax.nn.gelu(_tlin(h, h2_w, h2_s), approximate=False)
        return _tlin(h, w3_w, w3_s)
    x = L0_attn_x
    x = x + _L0_attn_ref(_layernorm(x, axis=-1), L0_attn_WQ, L0_attn_WK, L0_attn_WV, L0_attn_WO)
    x = x + _L0_ffn_ref(_layernorm(x, axis=-1), L0_ffn_Wr, L0_ffn_W1, L0_ffn_b1, L0_ffn_W2, L0_ffn_b2)
    x = x + _L1_attn_ref(_layernorm(x, axis=-1), L1_attn_ln1_g, L1_attn_ln1_b, L1_attn_Wq, L1_attn_bq, L1_attn_Wk, L1_attn_bk, L1_attn_Wv, L1_attn_bv, L1_attn_Wg, L1_attn_bg, L1_attn_decay_logit, L1_attn_Wo, L1_attn_bo, L1_attn_ln2_g, L1_attn_ln2_b, L1_attn_W1, L1_attn_b1, L1_attn_W2, L1_attn_b2)
    x = x + _L1_ffn_ref(_layernorm(x, axis=-1), L1_ffn_w1_w, L1_ffn_w1_s, L1_ffn_w2_w, L1_ffn_w2_s, L1_ffn_h1_w, L1_ffn_h1_s, L1_ffn_h2_w, L1_ffn_h2_s, L1_ffn_w3_w, L1_ffn_w3_s)
    return x

_drawn_inputs = setup_inputs


def setup_inputs(seed=0):
    import zlib

    import numpy as np

    out = dict(_drawn_inputs(seed))
    spreads = {'L0_ffn_b1': (0.0, 0.1),
     'L0_ffn_b2': (0.0, 0.1),
     'L1_attn_ln1_g': (1.0, 0.2),
     'L1_attn_ln1_b': (0.0, 0.1),
     'L1_attn_bq': (0.0, 0.1),
     'L1_attn_bk': (0.0, 0.1),
     'L1_attn_bv': (0.0, 0.1),
     'L1_attn_bg': (0.0, 0.1),
     'L1_attn_decay_logit': (0.0, 0.1),
     'L1_attn_bo': (0.0, 0.1),
     'L1_attn_ln2_g': (1.0, 0.2),
     'L1_attn_ln2_b': (0.0, 0.1),
     'L1_attn_b1': (0.0, 0.1),
     'L1_attn_b2': (0.0, 0.1)}
    factors = {}
    for name, (base, spread) in spreads.items():
        noise = np.random.default_rng([zlib.crc32(name.encode()), seed]).standard_normal(out[name].shape)
        drawn = base * np.exp(spread * noise) if base else spread * noise
        out[name] = jnp.asarray(drawn.astype(out[name].dtype))
    for name, factor in factors.items():
        out[name] = (out[name] * factor).astype(out[name].dtype)
    return out
```

```python
from contextlib import ExitStack

import concourse.bass as bass
from concourse import mybir

ALU = mybir.AluOpType
ACT = mybir.ActivationFunctionType
AXX = mybir.AxisListType.X
F32 = mybir.dt.float32
F32R = mybir.dt.float32r
BF16 = mybir.dt.bfloat16
U32 = mybir.dt.uint32

P = 128
NB = 4
TB = 4
SEQ = TB * P
NT = NB * TB
H = 16
DK = P // H
NG = 4
E = 8
TOPK = 2
CAP = int(NB * SEQ * 1.25 / E)
SLOTS = TOPK * CAP
ST = SLOTS // P
HALF = SLOTS // 2
FF = 4
LF = 8
EPS = 1e-5
DUMP = E * SLOTS
NEG = -1e30
NM = 2 * NG
MXU = (0, 1, 3, 5)
OU = (2, 4, 6, 7)
RSU = 1 + 2 * TB
N_CONST = 4 * P + 16 + 2 * NT + 8 + 3

COLS = [("ln1_g", 1), ("ln1_b", 1), ("ln2_g", 1), ("ln2_b", 1), ("bq", LF), ("bk", LF), ("bv", LF), ("bg", LF),
        ("decay_logit", LF), ("b1", FF), ("w1_s", FF), ("w2_s", FF), ("h1_s", FF), ("h2_s", FF), ("eb1", E * FF)]
COL = {}
_at = 0
for _name, _n in COLS:
    COL[_name] = _at
    _at += _n
N_COLS = _at
ROWS = ["bo", "b2", "w3_s"] + [f"eb2_{e}" for e in range(E)]
ROW = {n: i for i, n in enumerate(ROWS)}


def build(nc, d):
    ctx = ExitStack()
    with ctx:
        def sb(name, shape, dt=F32):
            return ctx.enter_context(nc.sbuf_tensor(name, shape, dt))

        def sem(name):
            return ctx.enter_context(nc.semaphore(name))

        ps = ctx.enter_context(nc.psum_tensor("ps", [P, 8, 512], F32))

        X = sb("X", [P, NT, P])
        const = sb("const", [P, N_CONST])
        cols = sb("cols", [P, N_COLS])
        rows = sb("rows", [P, len(ROWS), P])
        ident = const[:, 0:P]
        tri_f = const[:, 3 * P:4 * P]
        slot_base = const[:, 4 * P:4 * P + 16]
        dump_row = const[:, 4 * P + 16:4 * P + 16 + 2 * NT]
        iota8 = const[:, 4 * P + 16 + 2 * NT:4 * P + 24 + 2 * NT]
        c0 = 4 * P + 24 + 2 * NT
        q_part, k_part, k_one = const[:, c0:c0 + 1], const[:, c0 + 1:c0 + 2], const[:, c0 + 2:c0 + 3]
        identb = sb("identb", [P, P], BF16)
        maskb = sb("maskb", [P, P], BF16)
        maskTb = sb("maskTb", [P, P], BF16)
        trib = sb("trib", [P, P], BF16)
        onesb = sb("onesb", [P, P], BF16)
        mhalf = sb("mhalf", [P, 4])
        decay = sb("decay", [P, LF])

        wq = sb("wq", [P, P])
        wk = sb("wk", [P, P])
        wv = sb("wv", [P, P])
        wo = sb("wo", [P, P])
        WQS = sb("WQS", [P, H, 4, DK])
        WKS = sb("WKS", [P, H, 4, DK])
        xnT = sb("xnT", [P, NB * SEQ])
        V = sb("V", [P, TB * H, 32])
        rq = sb("rq", [P, SEQ], F32R)
        rk = sb("rk", [P, SEQ], F32R)
        QS = sb("QS", [P, 2, SEQ], F32R)
        KS = sb("KS", [P, 2, SEQ], F32R)
        QM = sb("QM", [P, 2, SEQ], F32R)
        mx = sb("mx", [P, TB, 4])
        MX = sb("MX", [P, TB, 4, 32], F32R)
        PT = sb("PT", [P, 4, TB, SEQ])
        rden = sb("rden", [P, TB * 4])
        O = sb("O", [P, TB, P])
        VR = sb("VR", [P, NT, P])
        OG = sb("OG", [P, SEQ])
        OT = sb("OT", [P, SEQ])

        stats = sb("stats", [P, 4, 6])
        mv = sb("mv", [P, 4, 2])
        veps = sb("veps", [P, 4])
        rstd = sb("rstd", [P, 4])
        xn = sb("xn", [P, TB, P])

        wr = sb("wr", [P, E])
        xn2T = sb("xn2T", [P, SEQ])
        lg = sb("lg", [P, TB, E])
        top = sb("top", [P, TB, 8])
        topi = sb("topi", [P, TB, 8], U32)
        topf = sb("topf", [P, 8])
        oh = sb("oh", [P, 8, 8])
        ohb = sb("ohb", [P, 8, 8], BF16)
        seen = sb("seen", [P, TB + 1, 16])
        seenb = sb("seenb", [P, TB, 16], BF16)
        rank = sb("rank", [P, 8, 8])
        sel = sb("sel", [P, 8, 8])
        keep = sb("keep", [P, 8])
        pos = sb("pos", [P, 8])
        pos2 = sb("pos2", [P, 8])
        posS = sb("posS", [P, 8], U32)
        posG = sb("posG", [P, 2 * NT], U32)
        dl = sb("dl", [P, TB])
        ex = sb("ex", [P, TB])
        w1t = sb("w1t", [P, TB])
        wts = sb("wts", [P, 2 * NT])

        zero = sb("zero", [P, 10 * P])
        W1 = sb("W1", [P, 2, FF * P])
        W2 = sb("W2", [P, 2, FF, P])
        XS = sb("XS", [P, 2, ST, P])
        XST = sb("XST", [P, 2, SLOTS])
        HT = sb("HT", [P, 2, FF, SLOTS])
        YS = zero[:, :].rearrange("p (s j n) -> p s j n", s=2, n=P)
        G = HT[:, :, :, :].rearrange("p s f n -> p (s f n)")[:, 0:2 * NT * P].rearrange("p (n c) -> p n c", c=P)

        lw = {n: sb("lw_" + n, [P, LF * P]) for n in ("Wq", "Wk", "Wv", "Wg")}
        lwo = sb("lwo", [P, LF, P])
        lw1 = sb("lw1", [P, FF * P])
        lw2 = sb("lw2", [P, FF, P])
        fw1 = sb("fw1", [P, FF * P])
        fw2 = sb("fw2", [P, FF * P])
        fh1 = sb("fh1", [P, FF, FF * P])
        fh2 = sb("fh2", [P, FF, FF * P])
        fw3 = sb("fw3", [P, FF, P])
        u = VR[:, 0 * TB:1 * TB, :]
        ubo = VR[:, 1 * TB:2 * TB, :]
        r = VR[:, 2 * TB:3 * TB, :]
        rx = VR[:, 3 * TB:4 * TB, :]
        aT = sb("aT", [P, SEQ])
        vs = xnT[:, 0:0 + 2 * SEQ].rearrange("p (a n) -> p a n", a=2)
        gs = xnT[:, 2 * SEQ:2 * SEQ + 2 * SEQ].rearrange("p (a n) -> p a n", a=2)
        Vflat = V[:, :, :].rearrange("p n k -> p (n k)")
        kv = OG[:, :]
        st = Vflat[:, 0:0 + 2 * SEQ].rearrange("p (a n) -> p a n", a=2)
        qg = Vflat[:, 2 * SEQ:2 * SEQ + 2 * SEQ].rearrange("p (a n) -> p a n", a=2)
        oT = PT[:, 0:2, :, :].rearrange("p i j n -> p (i j) n")
        hA = PT[:, 2, :, :]
        hB = PT[:, 3, :, :]
        yo = sb("yo", [P, TB, P])

        xs_dram = nc.dram_tensor("xs_dram", [DUMP + TOPK * NB * SEQ, P], F32, kind="Internal").ap()
        ys_dram = nc.dram_tensor("ys_dram", [DUMP, P], F32, kind="Internal").ap()

        x_in = [sem(f"x_in{b}") for b in range(NB)]
        par_in = sem("par_in")
        w0_in = sem("w0_in")
        w1_in = sem("w1_in")
        setup = sem("setup")
        bfc = sem("bfc")
        dve0 = sem("dve0")
        var0, rs0, xn0, tp0, tc0, vp0, vc0 = (sem(n) for n in ("var0", "rs0", "xn0", "tp0", "tc0", "vp0", "vc0"))
        l0 = sem("l0")
        lA = sem("lA")
        rs_full, rs_free = sem("rs_full"), sem("rs_free")
        parts = sem("parts")
        mx_done = sem("mx_done")
        m_full, m_done = sem("m_full"), sem("m_done")
        ts_full, exp_done = sem("ts_full"), sem("exp_done")
        pv_done, v_ready = sem("pv_done"), sem("v_ready")
        varA, rsA, xnA = sem("varA"), sem("rsA"), sem("xnA")
        og_done, lT = sem("og_done"), sem("lT")
        e_full, e_done = sem("e_full"), sem("e_done")
        oh_done, dl_done, ex_done, pos_done = sem("oh_done"), sem("dl_done"), sem("ex_done"), sem("pos_done")
        zeroed, scattered = sem("zeroed"), sem("scattered")
        ew_in = [sem(f"ew_in{s}") for s in range(2)]
        xs_in = [sem(f"xs_in{s}") for s in range(2)]
        xt_full, xt_done = sem("xt_full"), sem("xt_done")
        h_full, h_done = sem("h_full"), sem("h_done")
        y_full, y_done = sem("y_full"), sem("y_done")
        ys_out = [sem(f"ys_out{s}") for s in range(2)]
        gathered, rows_here = sem("gathered"), sem("rows_here")
        lC = sem("lC")
        v_paced, g_paced = sem("v_paced"), sem("g_paced")
        varC, rsC, lnC = sem("varC"), sem("rsC"), sem("lnC")
        t_full, t_done = sem("t_full"), sem("t_done")
        qkvg = sem("qkvg")
        v_done, k_done, g_done, q_done = sem("v_done"), sem("k_done"), sem("g_done"), sem("q_done")
        o_ready = sem("o_ready")
        row_full = sem("row_full")
        add_in, add_done = sem("add_in"), sem("add_done")
        hid_full, hid_done = sem("hid_full"), sem("hid_done")
        a_full, sl_done, a_done = sem("a_full"), sem("sl_done"), sem("a_done")
        y_out, out_done = sem("y_out"), sem("out_done")

        bank = [ps[:, i, :] for i in range(8)]
        tp_bank = bank[7]

        def tiles(ap):
            return ap.rearrange("p (t n) -> p t n", n=P)

        block = ctx.enter_context(nc.Block())

        @block.sync
        def _(sp):
            x_v = d["x"].rearrange("(b t p) n -> b p t n", t=TB, p=P)
            for b in range(NB):
                sp.dma_start(X[:, b * TB:(b + 1) * TB, :], x_v[b]).then_inc(x_in[b], 16)
                if b == 0:
                    sp.dma_start(const[:, :], d["const"]).then_inc(par_in, 16)
                    sp.dma_start(cols[:, :], d["cols"]).then_inc(par_in, 16)
                    for t, n in ((wq, "WQ"), (wk, "WK"), (wv, "WV"), (wo, "WO"), (wr, "Wr")):
                        sp.dma_start(t[:, :], d[n]).then_inc(w0_in, 16)
            for i, n in enumerate(("bo", "b2", "w3_s")):
                sp.dma_start(rows[:, i, :], d[n].partition_broadcast(P)).then_inc(w1_in, 16)
            for e in range(E):
                sp.dma_start(rows[:, 3 + e, :], d["eb2"][e].partition_broadcast(P)).then_inc(w1_in, 16)
            sp.wait_ge(setup, 3)
            zv = xs_dram[0:DUMP, :].rearrange("(p r) n -> p (r n)", p=P)
            for i in range(4):
                sp.dma_start(zv[:, i * 10 * P:(i + 1) * 10 * P], zero[:, :]).then_inc(zeroed, 16)
            for n in ("Wq", "Wk", "Wv", "Wg"):
                sp.dma_start(lw[n][:, :], d[n]).then_inc(w1_in, 16)
            sp.dma_start(lwo[:, :, :], d["Wo"].rearrange("(f p) n -> p f n", p=P)).then_inc(w1_in, 16)
            for t, n in ((lw1, "W1"), (fw1, "w1_w"), (fw2, "w2_w")):
                sp.dma_start(t[:, :], d[n]).then_inc(w1_in, 16)
            for t, n in ((lw2, "W2"), (fh1, "h1_w"), (fh2, "h2_w"), (fw3, "w3_w")):
                sp.dma_start(t[:, :, :], d[n].rearrange("(f p) n -> p f n", p=P)).then_inc(w1_in, 16)

            with sp.Fori(0, E // 2) as it:
                for s in range(2):
                    x = it * 2 + s
                    sp.wait_ge(y_full, x + 1)
                    sp.dma_start(W1[:, s, :], d["eW1"][bass.ts(x, P), :]).then_inc(ew_in[s], 16)
                    sp.dma_start(W2[:, s, :, :], d["eW2"][bass.ts(x, FF * P), :]
                                 .rearrange("(f p) n -> p f n", p=P)).then_inc(ew_in[s], 16)
                    sp.wait_ge(scattered, 16 * TOPK * NT)
                    sp.wait_ge(xt_full, x + 1)
                    sp.dma_start(XS[:, s, :, :], xs_dram[bass.ts(x, SLOTS), :]
                                 .rearrange("(j p) n -> p j n", p=P)).then_inc(xs_in[s], 16)
            with sp.Fori(0, NB) as b:
                sp.wait_ge(y_out, b + 1)
                sp.dma_start(d["out"][bass.ts(b, SEQ), :].rearrange("(t p) n -> p t n", p=P),
                             yo[:, :, :]).then_inc(out_done, 16)
            sp.wait_ge(out_done, 16 * NB)

        @block.gpsimd
        def _(g):
            g.memset(zero[:, :], 0.0).then_inc(setup, 1)
            g.memset(mhalf[:, :], -0.5).then_inc(setup, 1)
            g.memset(V[:, :, :], 0.0).then_inc(setup, 1)
            g.memset(WQS[:, :, 3:4, :], 0.0).then_inc(setup, 1)
            g.memset(WKS[:, :, 3:4, :], 0.0).then_inc(setup, 1)
            g.memset(onesb[:, :], 1.0).then_inc(setup, 1)
            g.memset(seen[:, TB, :], 0.0).then_inc(setup, 1)
            g.wait_ge(w0_in, 80)
            for c in range(3):
                g.tensor_copy(WQS[:, :, c, :], wq[:, :].rearrange("p (h k) -> p h k", k=DK)).then_inc(setup, 1)
                g.tensor_copy(WKS[:, :, c, :], wk[:, :].rearrange("p (h k) -> p h k", k=DK)).then_inc(setup, 1)

            g.wait_ge(setup, 13)
            g.memset(V[:, :, DK:DK + 1], 1.0).then_inc(setup, 1)
            g.wait_ge(setup, 14)

            def rsqrt(seen_sem, done_sem, value):
                g.wait_ge(seen_sem, value)
                g.tensor_tensor(rstd[:, :], veps[:, :], mhalf[:, :], ALU.pow).then_inc(done_sem, 1)

            for b in range(NB):
                rsqrt(var0, rs0, b + 1)
            g.wait_ge(zeroed, 64)
            with g.Fori(0, NB) as b:
                rsqrt(varA, rsA, b + 1)
                g.wait_ge(pos_done, b + 1)
                g.sem_inc(g_paced, 1)
                for t in range(TB):
                    for k in range(TOPK):
                        g.indirect_dma_start(
                            out=xs_dram, out_offset=bass.IndirectOffsetOnAxis(ap=posS[:, 2 * t + k:2 * t + k + 1], axis=0),
                            in_=xn[:, t, :], in_offset=None).then_inc(scattered, 16)
            g.wait_ge(ys_out[0], 16 * E // 2)
            g.wait_ge(ys_out[1], 16 * E // 2)

            def gather(b):
                for i in range(2 * TB):
                    c = b * 2 * TB + i
                    g.indirect_dma_start(
                        out=G[:, c, :], out_offset=None, in_=ys_dram,
                        in_offset=bass.IndirectOffsetOnAxis(ap=posG[:, c:c + 1], axis=0)).then_inc(gathered, 16)

            def gather_end(b):
                g.wait_ge(gathered, 16 * 2 * TB * (b + 1))
                g.sem_inc(rows_here, 1)

            gather(0)
            gather_end(0)
            for b in range(NB):
                rsqrt(varC, rsC, b * 4 + 1)
                rsqrt(varC, rsC, b * 4 + 2)
                g.wait_ge(add_in, b * 2 + 1)
                g.tensor_tensor(ubo[:, :, :], u[:, :, :],
                                rows[:, ROW["bo"]:ROW["bo"] + 1, :].to_broadcast([P, TB, P]), ALU.add).then_inc(add_done, 1)
                if b < NB - 1:
                    gather(b + 1)
                rsqrt(varC, rsC, b * 4 + 3)
                g.wait_ge(add_in, b * 2 + 2)
                g.tensor_tensor(rx[:, :, :], u[:, :, :],
                                rows[:, ROW["b2"]:ROW["b2"] + 1, :].to_broadcast([P, TB, P]), ALU.add).then_inc(add_done, 1)
                if b < NB - 1:
                    gather_end(b + 1)
                rsqrt(varC, rsC, b * 4 + 4)

        @block.scalar
        def _(act):
            act.wait_ge(par_in, 32)
            act.activation(identb[:, :], const[:, 0:P], ACT.Copy).then_inc(bfc, 1)
            act.activation(maskb[:, :], const[:, P:2 * P], ACT.Copy).then_inc(bfc, 1)
            act.activation(maskTb[:, :], const[:, 2 * P:3 * P], ACT.Copy).then_inc(bfc, 1)
            act.activation(trib[:, :], tri_f, ACT.Copy).then_inc(bfc, 1)
            act.activation(decay[:, :], cols[:, COL["decay_logit"]:COL["decay_logit"] + LF], ACT.Sigmoid).then_inc(bfc, 1)
            act.wait_ge(setup, 14)
            for b in range(NB):
                act.wait_ge(tp0, b + 1)
                act.activation(xnT[:, b * SEQ:(b + 1) * SEQ], bank[b % 2], ACT.Copy).then_inc(tc0, 1)
                act.wait_ge(vp0, b + 1)
                act.activation(VR[:, b * TB:(b + 1) * TB, :], tiles(bank[2 + b % 2]), ACT.Copy).then_inc(vc0, 1)

            def round_parts(b, g):
                slot = (g * RSU) % 2
                act.wait_ge(rs_full, b * NG * RSU + g * RSU + 1)
                act.activation(rq[:, :], ps[:, 2 * slot, :], ACT.Identity).then_inc(parts, 1)
                act.activation(rk[:, :], ps[:, 2 * slot + 1, :], ACT.Identity, bias=k_one).then_inc(parts, 1)

            def gate_exp(tb):
                act.wait_ge(dl_done, tb + 1)
                act.activation(ex[:, :], dl[:, :], ACT.Exp).then_inc(ex_done, 1)

            def store_sums(b, g):
                act.wait_ge(pv_done, b * 2 * NG + 2 * g + 4)
                act.activation(OG[:, :], bank[6], ACT.Identity).then_inc(og_done, 1)

            def attention(b, tail, following):
                act.activation(V[:, :, 0:DK], VR[:, bass.ts(b, TB), :].rearrange("p t (h k) -> p (t h) k", k=DK),
                               ACT.Identity).then_inc(v_ready, 1)
                for g in range(NG):
                    if g < NG - 1:
                        round_parts(b, g + 1)
                    elif following:
                        round_parts(b + 1, 0)
                    for i in range(4):
                        hh = g * 4 + i
                        if i % 2 == 0:
                            act.wait_ge(pv_done, b * 2 * NG + hh // 2 + 1)
                        for j in range(TB):
                            n = hh * TB + j
                            act.wait_ge(ts_full, b * H * TB + n + 1)
                            act.activation(PT[:, i, j, j * P:SEQ], ps[:, 4 + n % 2, 0:SEQ - j * P], ACT.Exp,
                                           scale=float(DK) ** -0.5).then_inc(exp_done, 1)
                        if g and i == 1:
                            store_sums(b, g - 1)
                    if tail and g == 1:
                        gate_exp(b - 1)
                store_sums(b, NG - 1)

            act.wait_ge(vc0, NB)
            round_parts(0, 0)
            attention(0, False, True)
            with act.Fori(1, NB - 1) as b:
                attention(b, True, True)
            attention(NB - 1, True, False)
            gate_exp(NB - 1)

            with act.Fori(0, E // 2) as it:
                for s in range(2):
                    x = it * 2 + s
                    for f in range(FF):
                        act.wait_ge(h_full, x * FF + f + 1)
                        act.activation(HT[:, s, f, :].rearrange("p (a n) -> p a n", a=2),
                                       ps[:, 2 * (f % 2):2 * (f % 2) + 2, 0:HALF], ACT.Gelu,
                                       bias=cols[:, bass.ds(x * FF + (COL["eb1"] + f), 1)]).then_inc(h_done, 1)
                    act.wait_ge(y_done, x + 2)
                    act.dma_start(ys_dram[bass.ts(x, SLOTS), :].rearrange("(j p) n -> p j n", p=P),
                                  YS[:, s, :, :]).then_inc(ys_out[s], 16)

            def col(name, f=0):
                return cols[:, COL[name] + f:COL[name] + f + 1]

            with act.Fori(0, NB) as b:
                act.wait_ge(t_full, b * 3 + 1)
                act.activation(aT[:, :], bank[4], ACT.Identity, scale=col("ln1_g"), bias=col("ln1_b")).then_inc(t_done, 1)
                for f in range(LF):
                    if f >= 2:
                        act.wait_ge(k_done, b * LF + f - 1)
                        act.wait_ge(q_done, b * LF + f - 1)
                    act.wait_ge(qkvg, b * 4 * LF + 4 * f + 1)
                    act.activation(vs[:, f % 2, :], bank[0], ACT.Identity, bias=col("bv", f)).then_inc(v_done, 1)
                    act.wait_ge(qkvg, b * 4 * LF + 4 * f + 3)
                    act.activation(gs[:, f % 2, :], bank[2], ACT.Sigmoid, bias=col("bg", f)).then_inc(g_done, 1)
                act.wait_ge(t_full, b * 3 + 2)
                act.activation(aT[:, :], bank[4], ACT.Identity, scale=col("ln2_g"), bias=col("ln2_b")).then_inc(t_done, 1)
                for f in range(FF):
                    act.wait_ge(hid_full, b * 12 + f + 1)
                    act.activation(hA[:, f, :], bank[6 + f % 2], ACT.Gelu, bias=col("b1", f)).then_inc(hid_done, 1)
                act.wait_ge(t_full, b * 3 + 3)
                act.activation(aT[:, :], bank[4], ACT.Identity).then_inc(t_done, 1)
                for f in range(FF):
                    act.wait_ge(a_full, b * 2 * FF + 2 * f + 1)
                    if f >= 2:
                        act.wait_ge(a_done, b * FF + f - 1)
                    act.activation(vs[:, f % 2, :], bank[f % 2], ACT.Silu, scale=col("w1_s", f)).then_inc(sl_done, 1)
                for m, (dst, name) in enumerate(((hB, "h1_s"), (hA, "h2_s"))):
                    for f in range(FF):
                        act.wait_ge(hid_full, b * 12 + 4 + 4 * m + f + 1)
                        act.activation(dst[:, f, :], bank[6 + f % 2], ACT.Gelu, scale=col(name, f)).then_inc(hid_done, 1)

        @block.vector
        def _(v):
            v.sem_inc(rs_free, 2)
            v.sem_inc(exp_done, 2)
            v.sem_inc(pv_done, 2)
            v.sem_inc(xt_done, 1)
            v.sem_inc(h_done, 2)
            v.sem_inc(y_done, 1)
            v.sem_inc(y_full, 2)
            v.sem_inc(xt_full, 2)

            class Order:

                def __init__(self, s, n, it):
                    self.s, self.n, self.it, self.k = s, n, it, 0

                def __call__(self, ins):
                    self.k += 1
                    ins.then_inc(self.s, 1)
                    v.wait_ge(self.s, self.it * self.n + self.k)

            def ln_stats(src, link, var_s):
                v.sem_inc(v_paced, 1)
                for t in range(TB):
                    ins = v.bn_stats(stats[:, t, :], src(t))
                link(ins)
                v.sem_inc(v_paced, 1)
                for t in range(TB):
                    ins = v.bn_aggr(mv[:, t, :], stats[:, t, :])
                link(ins)
                v.tensor_scalar(veps[:, :], mv[:, :, 1], EPS, None, ALU.add).then_inc(var_s, 1)

            def ln_apply(src, dst, rs_s, value, done):
                v.wait_ge(rs_s, value)
                for t in range(TB):
                    ins = v.tensor_scalar(dst(t), src(t), mv[:, t, 0:1], rstd[:, t:t + 1], ALU.subtract, ALU.mult)
                ins.then_inc(done, 1)

            def layernorm(src, dst, link, var_s, rs_s, value, done):
                ln_stats(src, link, var_s)
                ln_apply(src, dst, rs_s, value, done)

            o0 = Order(l0, 0, 0)
            for b in range(NB):
                v.wait_ge(x_in[b], 16)
                if b:
                    v.wait_ge(tp0, b)
                layernorm(lambda t: X[:, b * TB + t, :], lambda t: xn[:, t, :], o0, var0, rs0, b + 1, xn0)
            v.wait_ge(setup, 14)
            v.wait_ge(par_in, 32)
            v.memset(MX[:, :, :, :].bitcast(F32), 0.0).then_inc(l0, 1)
            v.wait_ge(l0, 2 * NB + 1)

            NLA = 2 * NG
            NLT = 22

            def make_parts(b, g):
                u0 = g * RSU
                slot = u0 % 2
                v.wait_ge(parts, b * 2 * NG + 2 * g + 2)
                v.scalar_tensor_tensor(out=QS[:, g % 2, :], in0=rq[:, :].bitcast(F32), scalar=q_part,
                                       in1=ps[:, 2 * slot, :], op0=ALU.mult, op1=ALU.add)
                v.scalar_tensor_tensor(out=KS[:, g % 2, :], in0=rk[:, :].bitcast(F32), scalar=k_part,
                                       in1=ps[:, 2 * slot + 1, :], op0=ALU.mult, op1=ALU.add).then_inc(rs_free, 1)

            def row_max(b, g, n):
                t, hp = n // 2, n % 2
                use = g * RSU + 1 + n
                slot = use % 2
                v.wait_ge(rs_full, b * NG * RSU + use + 1)
                v.tensor_reduce(mx[:, t, 2 * hp:2 * hp + 2], ps[:, 2 * slot:2 * slot + 2, 0:(t + 1) * P],
                                AXX, ALU.max).then_inc(rs_free, 1)

            def minus_max(b, g, link):
                v.wait_ge(rs_free, b * NG * RSU + (g + 1) * RSU + 2)
                link(v.tensor_scalar(MX[:, :, :, 24], mx[:, :, :], -1.0, None, ALU.mult))
                v.scalar_tensor_tensor(out=MX[:, :, :, 25], in0=mx[:, :, :], scalar=-1.0,
                                       in1=MX[:, :, :, 24].bitcast(F32), op0=ALU.mult,
                                       op1=ALU.subtract).then_inc(mx_done, 1)

            def add_max(b, g):
                v.wait_ge(m_full, b * NM + MXU[g] + 1)
                v.tensor_tensor(QM[:, g % 2, :], QS[:, g % 2, :].bitcast(F32), tp_bank, ALU.add).then_inc(m_done, 1)

            def attention(b, tail, following):
                link = Order(lA, NLA, b)

                def normalise(g):
                    v.wait_ge(m_full, b * NM + OU[g] + 1)
                    o = tp_bank.rearrange("p (t i k) -> p t i k", t=TB, i=4)
                    rd = rden[:, :].rearrange("p (t i) -> p t i", t=TB)
                    link(v.reciprocal(rd, o[:, :, :, DK]))
                    for t in range(TB):
                        ins = v.tensor_tensor(
                            O[:, t, g * 32:(g + 1) * 32].rearrange("p (i k) -> p i k", k=DK), o[:, t, :, 0:DK],
                            rd[:, t, :].rearrange("p (i a) -> p i a", a=1).to_broadcast([P, 4, DK]), ALU.mult)
                    ins.then_inc(m_done, 1)

                for g in range(NG):
                    minus_max(b, g, link)
                    add_max(b, g)
                    unit = (b, g + 1) if g < NG - 1 else (b + 1, 0) if following else None
                    if unit:
                        make_parts(*unit)
                    for n in range(8):
                        if unit:
                            row_max(*unit, n)
                        if n == 5 and g:
                            normalise(g - 1)
                        if tail and (g, n) in TAIL_AT:
                            tail(TAIL_AT[g, n])
                normalise(NG - 1)
                assert link.k == NLA, link.k

            TAIL_AT = {(0, 1): "turn", (0, 5): "stats", (0, 6): "norm", (1, 1): "turn2", (1, 5): "choose", (2, 1): "place"}

            def tail_of(b):
                link = Order(lT, NLT, b)

                def xt(t):
                    return X[:, bass.ds(b * TB + t, 1), :].rearrange("p a n -> p (a n)")

                def piece(name):
                    parts_of[name]()

                def turn():
                    v.wait_ge(e_full, b * 5 + 1)
                    v.tensor_copy(OT[:, :], tp_bank).then_inc(e_done, 1)

                def stats_():
                    v.wait_ge(e_full, b * 5 + 2)
                    xb = X[:, bass.ts(b, TB), :]
                    v.tensor_tensor(xb, tiles(tp_bank), xb, ALU.add).then_inc(e_done, 1)
                    v.wait_ge(e_done, b * 5 + 2)
                    ln_stats(xt, link, varA)

                def norm():
                    v.wait_ge(scattered, b * 16 * TOPK * TB)
                    ln_apply(xt, lambda t: xn[:, t, :], rsA, b + 1, xnA)

                def turn2():
                    v.wait_ge(e_full, b * 5 + 3)
                    v.tensor_copy(xn2T[:, :], tp_bank).then_inc(e_done, 1)

                def choose():
                    v.wait_ge(e_full, b * 5 + 4)
                    v.tensor_copy(lg[:, :, :], tp_bank[:, 0:TB * E].rearrange("p (t e) -> p t e", e=E)).then_inc(e_done, 1)
                    v.wait_ge(e_done, b * 5 + 4)
                    v.sem_inc(v_paced, 1)
                    for t in range(TB):
                        ins = v.max(top[:, t, :], lg[:, t, :])
                    link(ins)
                    v.sem_inc(v_paced, 1)
                    for t in range(TB):
                        ins = v.max_index(topi[:, t, :], top[:, t, :], lg[:, t, :])
                    link(ins)
                    v.tensor_tensor(dl[:, :], top[:, :, 1], top[:, :, 0], ALU.subtract).then_inc(dl_done, 1)
                    link(v.tensor_copy(topf[:, :].rearrange("p (t k) -> p t k", k=2), topi[:, :, 0:2]))
                    link(v.tensor_tensor(oh[:, :, :],
                                         iota8.rearrange("p (a e) -> p a e", a=1).to_broadcast([P, 8, 8]),
                                         topf[:, :].rearrange("p (n a) -> p n a", a=1).to_broadcast([P, 8, 8]),
                                         ALU.is_equal))
                    ohv = oh[:, :, :].rearrange("p (t k) e -> p t (k e)", k=2)
                    v.tensor_copy(ohb[:, :, :], oh[:, :, :])
                    link(v.tensor_copy(seen[:, 0, :], seen[:, TB, :]))
                    for t in range(TB):
                        link(v.tensor_tensor(seen[:, t + 1, :], seen[:, t, :], ohv[:, t, :], ALU.add))
                    v.tensor_copy(seenb[:, :, :], seen[:, 0:TB, :]).then_inc(oh_done, 1)

                def place():
                    v.wait_ge(e_full, b * 5 + 5)
                    link(v.tensor_copy(rank[:, :, :], tp_bank[:, 0:64].rearrange("p (n e) -> p n e", e=8)))
                    link(v.scalar_tensor_tensor(out=sel[:, :, :], in0=rank[:, :, :], scalar=float(CAP),
                                                in1=oh[:, :, :], op0=ALU.is_le, op1=ALU.mult))
                    link(v.tensor_reduce(keep[:, :], sel[:, :, :], AXX, ALU.add))
                    rv = rank[:, :, :].rearrange("p (t k) e -> p t (k e)", k=2)
                    link(v.tensor_tensor(rv, rv, slot_base.rearrange("p (a n) -> p a n", a=1).to_broadcast([P, TB, 16]), ALU.add))
                    link(v.tensor_tensor(rank[:, :, :], rank[:, :, :], oh[:, :, :], ALU.mult))
                    link(v.tensor_reduce(pos[:, :], rank[:, :, :], AXX, ALU.add))
                    db = dump_row[:, bass.ts(b, 2 * TB)]
                    v.tensor_tensor(posG[:, bass.ts(b, 2 * TB)], pos[:, :], keep[:, :], ALU.mult)
                    link(v.tensor_tensor(pos2[:, :], pos[:, :], db, ALU.subtract))
                    link(v.tensor_tensor(pos2[:, :], pos2[:, :], keep[:, :], ALU.mult))
                    v.tensor_tensor(posS[:, :], pos2[:, :], db, ALU.add).then_inc(pos_done, 1)
                    v.wait_ge(ex_done, b + 1)
                    link(v.tensor_scalar(w1t[:, :], ex[:, :], 1.0, None, ALU.add))
                    link(v.reciprocal(w1t[:, :], w1t[:, :]))
                    wb = wts[:, bass.ts(b, 2 * TB)].rearrange("p (t k) -> p t k", k=2)
                    kb = keep[:, :].rearrange("p (t k) -> p t k", k=2)
                    v.tensor_tensor(wb[:, :, 0], w1t[:, :], kb[:, :, 0], ALU.mult)
                    link(v.tensor_tensor(w1t[:, :], w1t[:, :], ex[:, :], ALU.mult))
                    v.tensor_tensor(wb[:, :, 1], w1t[:, :], kb[:, :, 1], ALU.mult).then_inc(e_done, 1)
                    assert link.k == NLT, link.k

                parts_of = {"turn": turn, "stats": stats_, "norm": norm, "turn2": turn2, "choose": choose, "place": place}
                return piece

            make_parts(0, 0)
            for n in range(8):
                row_max(0, 0, n)
            attention(0, None, True)
            with v.Fori(1, NB - 1) as b:
                attention(b, tail_of(b - 1), True)
            attention(NB - 1, tail_of(NB - 2), False)
            last = tail_of(NB - 1)
            for name in TAIL_AT.values():
                last(name)

            v.wait_ge(w1_in, 16 * 23)
            with v.Fori(0, E // 2) as it:
                for s in range(2):
                    x = it * 2 + s
                    v.wait_ge(xt_full, x + 3)
                    v.tensor_copy(XST[:, s, 0:512], bank[6])
                    v.tensor_copy(XST[:, s, 512:SLOTS], bank[7][:, 0:P]).then_inc(xt_done, 1)
                    v.wait_ge(y_full, x + 3)
                    v.wait_ge(ys_out[s], it * 16)
                    b2 = rows[:, bass.ds(x + ROW["eb2_0"], 1), :]
                    v.tensor_tensor(YS[:, s, 0:4, :], tiles(bank[4]), b2.to_broadcast([P, 4, P]), ALU.add)
                    v.tensor_tensor(YS[:, s, 4:5, :], tiles(bank[5][:, 0:P]), b2, ALU.add).then_inc(y_done, 1)

            NLC = 8 + 4 + LF + 7
            with v.Fori(0, NB) as b:
                link = Order(lC, NLC, b)
                v.wait_ge(rows_here, b + 1)
                for k in range(2):
                    for t in range(TB):
                        xt = X[:, bass.ds(b * TB + t, 1), :].rearrange("p a n -> p (a n)")
                        gt = G[:, bass.ds(b * 2 * TB + (2 * t + k), 1), :].rearrange("p a n -> p (a n)")
                        wt = wts[:, bass.ds(b * 2 * TB + (2 * t + k), 1)]
                        link(v.scalar_tensor_tensor(out=xt, in0=gt, scalar=wt, in1=xt, op0=ALU.mult, op1=ALU.add))

                def tile_x(t):
                    return X[:, bass.ds(b * TB + t, 1), :].rearrange("p a n -> p (a n)")

                layernorm(tile_x, lambda t: u[:, t, :], link, varC, rsC, b * 4 + 1, add_in)
                v.wait_ge(add_in, b * 2 + 1)
                layernorm(lambda t: u[:, t, :], lambda t: xn[:, t, :], link, varC, rsC, b * 4 + 2, lnC)
                for f in range(LF):
                    fb = f % 2
                    c = COL["decay_logit"]
                    v.wait_ge(qkvg, b * 4 * LF + 4 * f + 2)
                    v.wait_ge(v_done, b * LF + f + 1)
                    v.scalar_tensor_tensor(out=kv[:, :], in0=bank[1], scalar=cols[:, COL["bk"] + f:COL["bk"] + f + 1],
                                           in1=vs[:, fb, :], op0=ALU.add, op1=ALU.mult).then_inc(k_done, 1)
                    v.wait_ge(k_done, b * LF + f + 1)
                    link(v.tensor_tensor_scan(st[:, fb, :], decay[:, f:f + 1].to_broadcast([P, SEQ]), kv[:, :], 0.0,
                                              ALU.mult, ALU.add))
                    v.wait_ge(qkvg, b * 4 * LF + 4 * f + 4)
                    v.wait_ge(g_done, b * LF + f + 1)
                    v.scalar_tensor_tensor(out=qg[:, fb, :], in0=bank[3], scalar=cols[:, COL["bq"] + f:COL["bq"] + f + 1],
                                           in1=gs[:, fb, :], op0=ALU.add, op1=ALU.mult).then_inc(q_done, 1)
                    v.wait_ge(q_done, b * LF + f + 1)
                    v.scalar_tensor_tensor(out=oT[:, f, :], in0=qg[:, fb, :], scalar=0.125, in1=st[:, fb, :],
                                           op0=ALU.mult, op1=ALU.mult).then_inc(o_ready, 1)
                v.wait_ge(row_full, b * 3 + 1)
                v.wait_ge(add_done, b * 2 + 1)
                link(v.tensor_tensor(r[:, :, :], tiles(bank[5]), ubo[:, :, :], ALU.add))
                layernorm(lambda t: r[:, t, :], lambda t: xn[:, t, :], link, varC, rsC, b * 4 + 3, lnC)
                xb = X[:, bass.ts(b, TB), :]
                v.tensor_tensor(u[:, :, :], r[:, :, :], xb, ALU.add).then_inc(add_in, 1)
                v.wait_ge(row_full, b * 3 + 2)
                v.wait_ge(lnC, b * 3 + 2)
                v.wait_ge(add_done, b * 2 + 2)
                link(v.tensor_tensor(r[:, :, :], tiles(bank[5]), rx[:, :, :], ALU.add))
                layernorm(lambda t: r[:, t, :], lambda t: xn[:, t, :], link, varC, rsC, b * 4 + 4, lnC)
                for f in range(FF):
                    v.wait_ge(a_full, b * 2 * FF + 2 * f + 2)
                    v.wait_ge(sl_done, b * FF + f + 1)
                    v.scalar_tensor_tensor(out=hA[:, f, :], in0=bank[2 + f % 2],
                                           scalar=cols[:, COL["w2_s"] + f:COL["w2_s"] + f + 1],
                                           in1=vs[:, f % 2, :], op0=ALU.mult, op1=ALU.mult).then_inc(a_done, 1)
                v.wait_ge(row_full, b * 3 + 3)
                v.wait_ge(out_done, b * 16)
                link(v.tensor_tensor(yo[:, :, :], tiles(bank[5]),
                                     rows[:, ROW["w3_s"]:ROW["w3_s"] + 1, :].to_broadcast([P, TB, P]), ALU.mult))
                v.tensor_tensor(yo[:, :, :], yo[:, :, :], r[:, :, :], ALU.add).then_inc(y_out, 1)
                assert link.k == NLC, link.k

        @block.tensor
        def _(pe):
            pe.wait_ge(par_in, 32)
            pe.wait_ge(w0_in, 80)
            for b in range(NB):
                pe.wait_ge(xn0, b + 1)
                if b >= 2:
                    pe.wait_ge(tc0, b - 1)
                for t in range(TB):
                    mm = pe.transpose(bank[b % 2][:, t * P:(t + 1) * P], xn[:, t, :], ident)
                mm.then_inc(tp0, 1)
                pe.wait_ge(tc0, b + 1)
                if b >= 2:
                    pe.wait_ge(vc0, b - 1)
                for t in range(TB):
                    c = (b * TB + t) * P
                    mm = pe.matmul(bank[2 + b % 2][:, t * P:(t + 1) * P], xnT[:, c:c + P], wv[:, :], start=True, stop=True)
                mm.then_inc(vp0, 1)
            pe.wait_ge(setup, 14)
            pe.wait_ge(bfc, 4)
            pe.wait_ge(vc0, NB)

            def tail_of(b):
                def piece(name):
                    if name == "turn":
                        for t in range(TB):
                            mm = pe.transpose(tp_bank[:, t * P:(t + 1) * P], O[:, t, :], ident)
                    elif name == "wo":
                        pe.wait_ge(e_done, b * 5 + 1)
                        for t in range(TB):
                            mm = pe.matmul(tp_bank[:, t * P:(t + 1) * P], OT[:, t * P:(t + 1) * P], wo[:, :],
                                           start=True, stop=True)
                    elif name == "turn2":
                        pe.wait_ge(xnA, b + 1)
                        for t in range(TB):
                            mm = pe.transpose(tp_bank[:, t * P:(t + 1) * P], xn[:, t, :], ident)
                    elif name == "logits":
                        pe.wait_ge(e_done, b * 5 + 3)
                        for t in range(TB):
                            mm = pe.matmul(tp_bank[:, t * E:(t + 1) * E], xn2T[:, t * P:(t + 1) * P], wr[:, :],
                                           start=True, stop=True)
                    else:
                        pe.wait_ge(oh_done, b + 1)
                        pe.wait_ge(e_done, b * 5 + 4)
                        for t in range(TB):
                            c = slice(t * 16, (t + 1) * 16)
                            pe.matmul(tp_bank[:, c], trib[:, :], ohb[:, 2 * t:2 * t + 2, :].rearrange("p k e -> p (k e)"),
                                      start=True, stop=False)
                            mm = pe.matmul(tp_bank[:, c], onesb[:, :], seenb[:, t, :], start=False, stop=True)
                    mm.then_inc(e_full, 1)
                return piece

            def slot_of(b, use):
                pe.wait_ge(rs_free, b * NG * RSU + use + 1)
                return use % 2

            def project(b, g):
                s = slot_of(b, g * RSU)
                x = xnT[:, bass.ts(b, SEQ)]
                pe.matmul(ps[:, 2 * s, :], WQS[:, 4 * g:4 * g + 4, :, :].rearrange("p h c k -> p (h c k)"), x,
                          start=True, stop=True)
                pe.matmul(ps[:, 2 * s + 1, :], WKS[:, 4 * g:4 * g + 4, :, :].rearrange("p h c k -> p (h c k)"), x,
                          start=True, stop=True).then_inc(rs_full, 1)

            def row_scores(b, g, n):
                t, hp = n // 2, n % 2
                s = slot_of(b, g * RSU + 1 + n)
                if n == 0:
                    pe.wait_ge(rs_free, b * NG * RSU + g * RSU + 3)
                for a in range(2):
                    i = 2 * hp + a
                    pe.matmul(ps[:, 2 * s + a, 0:(t + 1) * P], QS[32 * i:32 * i + 32, g % 2, t * P:(t + 1) * P],
                              KS[32 * i:32 * i + 32, g % 2, 0:(t + 1) * P], start=True, stop=False)
                    mm = pe.matmul(ps[:, 2 * s + a, t * P:(t + 1) * P], identb[:, :], maskb[:, :],
                                   start=False, stop=True)
                mm.then_inc(rs_full, 1)

            def attention(b, tail, following):
                def claim(m, e):
                    pe.wait_ge(m_done, b * NM + m)
                    if tail:
                        pe.wait_ge(e_done, (b - 1) * 5 + e)

                def turn_max(g):
                    claim(MXU[g], (0, 2, 4, 5)[g])
                    pe.wait_ge(mx_done, b * NG + g + 1)
                    for t in range(TB):
                        mm = pe.transpose(tp_bank[:, t * P:(t + 1) * P],
                                          MX[:, t, :, :].rearrange("p i c -> p (i c)").bitcast(F32), ident)
                    mm.then_inc(m_full, 1)

                def key_scores(g, i, js):
                    for j in js:
                        n = (g * 4 + i) * TB + j
                        pe.wait_ge(exp_done, b * H * TB + n + 1)
                        pe.matmul(ps[:, 4 + n % 2, 0:SEQ - j * P], KS[32 * i:32 * i + 32, g % 2, j * P:(j + 1) * P],
                                  QM[32 * i:32 * i + 32, g % 2, j * P:SEQ], start=True, stop=False)
                        pe.matmul(ps[:, 4 + n % 2, 0:P], identb[:, :], maskTb[:, :],
                                  start=False, stop=True).then_inc(ts_full, 1)

                def values(g, p, js):
                    if 0 in js:
                        pe.wait_ge(exp_done, b * H * TB + (4 * g + 2 * p + 2) * TB + 2)
                        if p == 0:
                            pe.wait_ge(v_ready, b + 1)
                            pe.wait_ge(og_done, b * NG + g)
                    for j in js:
                        for i in (2 * p, 2 * p + 1):
                            mm = pe.matmul(bank[6][32 * i:32 * i + 32, j * P:SEQ], V[:, j * H + g * 4 + i, :],
                                           PT[:, i, j, j * P:SEQ], start=(j == 0), stop=(j == TB - 1),
                                           skip_group_check=True)
                    if TB - 1 in js:
                        mm.then_inc(pv_done, 1)

                def turn_out(g):
                    claim(OU[g], (3, 5, 5, 5)[g])
                    pe.wait_ge(og_done, b * NG + g + 1)
                    for t in range(TB):
                        mm = pe.transpose(tp_bank[:, t * P:(t + 1) * P], OG[:, t * P:(t + 1) * P], ident)
                    mm.then_inc(m_full, 1)

                def piece(m, e, name):
                    if tail:
                        claim(m, e)
                        tail(name)

                for g in range(NG):
                    unit = (b, g + 1) if g < NG - 1 else (b + 1, 0) if following else None
                    if unit:
                        project(*unit)
                    turn_max(g)
                    pe.wait_ge(m_done, b * NM + MXU[g] + 1)
                    for i in range(4):
                        before = (g, 0) if i >= 2 else (g - 1, 1) if g else None
                        if i == 1 and g < 3:
                            piece((1, 2, 4)[g], (0, 2, 4)[g], ("turn", "turn2", "ranks")[g])
                        if i == 3:
                            if g:
                                turn_out(g - 1)
                            if g < 2:
                                piece((1, 3)[g], (1, 3)[g], ("wo", "logits")[g])
                        for half in range(2):
                            key_scores(g, i, (2 * half, 2 * half + 1))
                            if unit:
                                row_scores(*unit, 2 * i + half)
                        if before:
                            values(*before, (0,) if i % 2 == 0 else (1, 2, 3))
                values(NG - 1, 1, range(TB))
                turn_out(NG - 1)

            project(0, 0)
            for n in range(8):
                row_scores(0, 0, n)
            attention(0, None, True)
            with pe.Fori(1, NB - 1) as b:
                attention(b, tail_of(b - 1), True)
            attention(NB - 1, tail_of(NB - 2), False)
            last = tail_of(NB - 1)
            pe.wait_ge(m_done, NB * NM)
            for name in ("turn", "wo", "turn2", "logits", "ranks"):
                last(name)

            pe.wait_ge(m_done, NB * NM)
            pe.wait_ge(e_done, NB * 5)
            with pe.Fori(0, E // 2) as it:
                for s in range(2):
                    x = it * 2 + s
                    pe.wait_ge(xs_in[s], it * 16 + 16)
                    pe.wait_ge(xt_done, x + 1)
                    for j in range(ST):
                        mm = pe.transpose(bank[6 + j // 4][:, (j % 4) * P:(j % 4 + 1) * P], XS[:, s, j, :], ident)
                    mm.then_inc(xt_full, 1)
                    pe.wait_ge(xt_done, x + 2)
                    pe.wait_ge(ew_in[s], it * 32 + 32)
                    for f in range(FF):
                        pe.wait_ge(h_done, x * FF + f + 1)
                        for a in range(2):
                            mm = pe.matmul(ps[:, 2 * (f % 2) + a, 0:HALF], W1[:, s, f * P:(f + 1) * P],
                                           XST[:, s, a * HALF:(a + 1) * HALF], start=True, stop=True)
                        mm.then_inc(h_full, 1)
                    pe.wait_ge(h_done, x * FF + FF + 2)
                    pe.wait_ge(y_done, x + 1)
                    for j in range(ST):
                        for f in range(FF):
                            mm = pe.matmul(bank[4 + j // 4][:, (j % 4) * P:(j % 4 + 1) * P], HT[:, s, f, j * P:(j + 1) * P],
                                           W2[:, s, f, :], start=(f == 0), stop=(f == FF - 1))
                    mm.then_inc(y_full, 1)

            pe.wait_ge(w1_in, 16 * 23)
            pe.wait_ge(y_done, E + 1)
            with pe.Fori(0, NB) as b:
                def turn(k):
                    pe.wait_ge(lnC, b * 3 + k + 1)
                    for t in range(TB):
                        mm = pe.transpose(bank[4][:, t * P:(t + 1) * P], xn[:, t, :], ident)
                    mm.then_inc(t_full, 1)
                    pe.wait_ge(t_done, b * 3 + k + 1)

                def to_rows(src, w, n):
                    for t in range(TB):
                        for f in range(n):
                            mm = pe.matmul(bank[5][:, t * P:(t + 1) * P], src[:, f, t * P:(t + 1) * P], w[:, f, :],
                                           start=(f == 0), stop=(f == n - 1))
                    mm.then_inc(row_full, 1)

                turn(0)
                for f in range(LF):
                    for m, (n, done) in enumerate((("Wv", v_done), ("Wk", k_done), ("Wg", g_done), ("Wq", q_done))):
                        pe.wait_ge(done, b * LF + f)
                        pe.matmul(bank[m], lw[n][:, f * P:(f + 1) * P], aT[:, :], start=True, stop=True).then_inc(qkvg, 1)
                pe.wait_ge(o_ready, b * LF + LF)
                to_rows(oT, lwo, LF)
                turn(1)
                for f in range(FF):
                    if f >= 2:
                        pe.wait_ge(hid_done, b * 12 + f - 1)
                    pe.matmul(bank[6 + f % 2], lw1[:, f * P:(f + 1) * P], aT[:, :], start=True, stop=True).then_inc(hid_full, 1)
                pe.wait_ge(hid_done, b * 12 + 4)
                to_rows(hA, lw2, FF)
                turn(2)
                for f in range(FF):
                    if f >= 2:
                        pe.wait_ge(sl_done, b * FF + f - 1)
                        pe.wait_ge(a_done, b * FF + f - 1)
                    pe.matmul(bank[f % 2], fw1[:, f * P:(f + 1) * P], aT[:, :], start=True, stop=True).then_inc(a_full, 1)
                    pe.matmul(bank[2 + f % 2], fw2[:, f * P:(f + 1) * P], aT[:, :], start=True, stop=True).then_inc(a_full, 1)
                pe.wait_ge(a_done, b * FF + FF)
                for m, (src, w) in enumerate(((hA, fh1), (hB, fh2))):
                    if m:
                        pe.wait_ge(hid_done, b * 12 + 8)
                    for f in range(FF):
                        n = 4 + 4 * m + f
                        pe.wait_ge(hid_done, b * 12 + n - 1)
                        for c in range(FF):
                            mm = pe.matmul(bank[6 + f % 2], w[:, c, f * P:(f + 1) * P], src[:, c, :],
                                           start=(c == 0), stop=(c == FF - 1))
                        mm.then_inc(hid_full, 1)
                pe.wait_ge(hid_done, b * 12 + 12)
                to_rows(hA, fw3, FF)


def shape_constants():
    import numpy as np
    i = np.arange(P)
    later = i[None, :] > i[:, None]
    c = np.zeros((P, N_CONST), np.float32)
    c[:, 0:P] = np.eye(P)
    c[:, P:2 * P] = np.where(later, NEG, 0.0)
    c[:, 2 * P:3 * P] = np.where(later.T, NEG, 0.0)
    c[:, 3 * P:4 * P] = i[:, None] <= i[None, :]
    at = 4 * P
    for k in range(TOPK):
        for e in range(E):
            c[:, at + k * E + e] = e * SLOTS + k * CAP - 1
    at += 16
    for t in range(NT):
        for k in range(TOPK):
            c[:, at + 2 * t + k] = DUMP + k * NT * P + t * P + i
    at += 2 * NT
    c[:, at:at + 8] = np.arange(8)
    at += 8
    part = (i % 32) // 8
    c[:, at] = np.where(part == 2, -1.0, 0.0)
    c[:, at + 1] = np.where(part == 1, -1.0, np.where(part == 3, 1.0, 0.0))
    c[:, at + 2] = np.where(part == 3, 1.0, 0.0)
    return c


def kernel(**inputs):
    import numpy as np
    import concourse.bacc as _bacc
    from concourse.bass_utils import run_bass_kernel_spmd as _run

    a = {k: np.asarray(v) for k, v in inputs.items()}
    col = lambda x: x.reshape(-1, P).T
    dec = np.repeat(a["L1_attn_decay_logit"], LF * P // H)
    parts = [a["L1_attn_ln1_g"], a["L1_attn_ln1_b"], a["L1_attn_ln2_g"], a["L1_attn_ln2_b"], a["L1_attn_bq"],
             a["L1_attn_bk"], a["L1_attn_bv"], a["L1_attn_bg"], dec, a["L1_attn_b1"], a["L1_ffn_w1_s"],
             a["L1_ffn_w2_s"], a["L1_ffn_h1_s"], a["L1_ffn_h2_s"], a["L0_ffn_b1"]]
    arrays = {
        "x": a["L0_attn_x"].reshape(NT * P, P),
        "const": shape_constants(),
        "cols": np.concatenate([col(p) for p in parts], axis=1),
        "WQ": a["L0_attn_WQ"], "WK": a["L0_attn_WK"], "WV": a["L0_attn_WV"], "WO": a["L0_attn_WO"],
        "Wr": a["L0_ffn_Wr"], "eW1": a["L0_ffn_W1"].reshape(E * P, FF * P), "eW2": a["L0_ffn_W2"].reshape(E * FF * P, P),
        "eb2": a["L0_ffn_b2"], "bo": a["L1_attn_bo"], "b2": a["L1_attn_b2"], "w3_s": a["L1_ffn_w3_s"],
        "Wq": a["L1_attn_Wq"], "Wk": a["L1_attn_Wk"], "Wv": a["L1_attn_Wv"], "Wg": a["L1_attn_Wg"],
        "Wo": a["L1_attn_Wo"], "W1": a["L1_attn_W1"], "W2": a["L1_attn_W2"],
        "w1_w": a["L1_ffn_w1_w"].T, "w2_w": a["L1_ffn_w2_w"].T, "h1_w": a["L1_ffn_h1_w"].T,
        "h2_w": a["L1_ffn_h2_w"].T, "w3_w": a["L1_ffn_w3_w"].T,
    }
    arrays = {f"in_{k}": np.ascontiguousarray(v) for k, v in arrays.items()}
    nc = _bacc.Bacc("TRN2", target_bir_lowering=False, num_devices=1)
    d = {k[3:]: nc.dram_tensor(k, v.shape, mybir.dt.from_np(v.dtype), kind="ExternalInput").ap() for k, v in arrays.items()}
    d["out"] = nc.dram_tensor("out_dram", (NT * P, P), F32, kind="ExternalOutput").ap()
    build(nc, d)
    res = _run(nc, [arrays], core_ids=[0])
    return res.results[0]["out_dram"].reshape(NB, SEQ, P)
```

```python
from contextlib import ExitStack

import concourse.bass as bass
from concourse import mybir

ALU = mybir.AluOpType
ACT = mybir.ActivationFunctionType
AXX = mybir.AxisListType.X
F32 = mybir.dt.float32
F32R = mybir.dt.float32r
BF16 = mybir.dt.bfloat16
U32 = mybir.dt.uint32

P = 128
NB = 4
TB = 4
SEQ = TB * P
NT = NB * TB
H = 16
DK = P // H
NG = 4
E = 8
TOPK = 2
CAP = int(NB * SEQ * 1.25 / E)
SLOTS = TOPK * CAP
ST = SLOTS // P
HALF = SLOTS // 2
FF = 4
LF = 8
EPS = 1e-5
DUMP = E * SLOTS
NEG = -1e30
NM = 2 * NG
MXU = (0, 1, 3, 5)
OU = (2, 4, 6, 7)
RSU = 1 + 2 * TB
N_CONST = 4 * P + 16 + 2 * NT + 8 + 3

TURN2_AT = 5

COLS = [("ln1_g", 1), ("ln1_b", 1), ("ln2_g", 1), ("ln2_b", 1), ("bq", LF), ("bk", LF), ("bv", LF), ("bg", LF),
        ("decay_logit", LF), ("b1", FF), ("w1_s", FF), ("w2_s", FF), ("h1_s", FF), ("h2_s", FF), ("eb1", E * FF)]
COL = {}
_at = 0
for _name, _n in COLS:
    COL[_name] = _at
    _at += _n
N_COLS = _at
ROWS = ["bo", "b2", "w3_s"] + [f"eb2_{e}" for e in range(E)]
ROW = {n: i for i, n in enumerate(ROWS)}


def TURN(b):
    return b * 3 + 3 if isinstance(b, int) and b == NB - 1 else b * 3 + 4


def VAR(b):
    return b * 4 + 4 if isinstance(b, int) and b == NB - 1 else b * 4 + 6


def build(nc, d):
    ctx = ExitStack()
    with ctx:
        def sb(name, shape, dt=F32):
            return ctx.enter_context(nc.sbuf_tensor(name, shape, dt))

        def sem(name):
            return ctx.enter_context(nc.semaphore(name))

        ps = ctx.enter_context(nc.psum_tensor("ps", [P, 8, 512], F32))

        X = sb("X", [P, NT, P])
        const = sb("const", [P, N_CONST])
        cols = sb("cols", [P, N_COLS])
        rows = sb("rows", [P, len(ROWS), P])
        ident = const[:, 0:P]
        tri_f = const[:, 3 * P:4 * P]
        slot_base = const[:, 4 * P:4 * P + 16]
        dump_row = const[:, 4 * P + 16:4 * P + 16 + 2 * NT]
        iota8 = const[:, 4 * P + 16 + 2 * NT:4 * P + 24 + 2 * NT]
        c0 = 4 * P + 24 + 2 * NT
        q_part, k_part, k_one = const[:, c0:c0 + 1], const[:, c0 + 1:c0 + 2], const[:, c0 + 2:c0 + 3]
        identb = sb("identb", [P, P], BF16)
        maskb = sb("maskb", [P, P], BF16)
        maskTb = sb("maskTb", [P, P], BF16)
        trib = sb("trib", [P, P], BF16)
        onesb = sb("onesb", [P, P], BF16)
        mhalf = sb("mhalf", [P, NT])
        decay = sb("decay", [P, LF])

        wq = sb("wq", [P, P])
        wk = sb("wk", [P, P])
        wv = sb("wv", [P, P])
        wo = sb("wo", [P, P])
        WQS = sb("WQS", [P, H, 4, DK])
        WKS = sb("WKS", [P, H, 4, DK])
        xnT = sb("xnT", [P, NB * SEQ])
        V = sb("V", [P, TB * H, 32])
        rq = sb("rq", [P, SEQ], F32R)
        rk = sb("rk", [P, SEQ], F32R)
        QS = sb("QS", [P, 2, SEQ], F32R)
        KS = sb("KS", [P, 2, SEQ], F32R)
        QM = sb("QM", [P, 2, SEQ], F32R)
        KP = sb("KP", [P, 2, 4, SEQ], F32R)
        mx = sb("mx", [P, TB, 4])
        MX = sb("MX", [P, TB, 4, 32], F32R)
        PT = sb("PT", [P, 4, TB, SEQ])
        rden = sb("rden", [P, TB * 4])
        O = sb("O", [P, TB, P])
        VR = sb("VR", [P, NT, P])
        OG = sb("OG", [P, SEQ])
        OT = sb("OT", [P, SEQ])

        stats = sb("stats", [P, 4, 6])
        mv = sb("mv", [P, 4, 2])
        veps = sb("veps", [P, 4])
        rstd = sb("rstd", [P, 4])
        xn = sb("xn", [P, TB, P])

        stats0 = sb("stats0", [P, NT, 6])
        mv0 = sb("mv0", [P, NT, 2])
        veps0 = sb("veps0", [P, NT])
        rstd0 = sb("rstd0", [P, NT])

        wr = sb("wr", [P, E])
        xn2T = sb("xn2T", [P, SEQ])
        lg = sb("lg", [P, TB, E])
        top = sb("top", [P, TB, 8])
        topi = sb("topi", [P, TB, 8], U32)
        topf = sb("topf", [P, 8])
        oh = sb("oh", [P, 8, 8])
        ohb = sb("ohb", [P, 8, 8], BF16)
        seen = sb("seen", [P, TB + 1, 16])
        seenb = sb("seenb", [P, TB, 16], BF16)
        rank = sb("rank", [P, 8, 8])
        sel = sb("sel", [P, 8, 8])
        keep = sb("keep", [P, 8])
        pos = sb("pos", [P, 8])
        pos2 = sb("pos2", [P, 8])
        posS = sb("posS", [P, 8], U32)
        posG = sb("posG", [P, 2 * NT], U32)
        dl = sb("dl", [P, TB])
        ex = sb("ex", [P, TB])
        w1t = sb("w1t", [P, TB])
        wts = sb("wts", [P, 2 * NT])

        zero = sb("zero", [P, 10 * P])
        PTflat = PT[:, :, :, :].rearrange("p i j n -> p (i j n)")
        _w, _x = 2 * FF * P, 2 * SLOTS
        W1 = PTflat[:, 0:_w].rearrange("p (s n) -> p s n", s=2)
        W2 = PTflat[:, _w:2 * _w].rearrange("p (s f n) -> p s f n", s=2, f=FF)
        XS = PTflat[:, 2 * _w:2 * _w + _x].rearrange("p (s j n) -> p s j n", s=2, j=ST)
        XST = PTflat[:, 2 * _w + _x:2 * _w + 2 * _x].rearrange("p (s n) -> p s n", s=2)
        HT = sb("HT", [P, 2, FF, SLOTS])
        HTflat = HT[:, :, :, :].rearrange("p s f n -> p (s f n)")
        YS = zero[:, :].rearrange("p (s j n) -> p s j n", s=2, n=P)
        G = HTflat[:, 0:2 * NT * P].rearrange("p (n c) -> p n c", c=P)

        lw = {n: sb("lw_" + n, [P, LF * P]) for n in ("Wq", "Wk", "Wv", "Wg")}
        lwo = sb("lwo", [P, LF, P])
        lw1 = sb("lw1", [P, FF * P])
        lw2 = sb("lw2", [P, FF, P])
        fw1 = sb("fw1", [P, FF * P])
        fw2 = sb("fw2", [P, FF * P])
        fh1 = sb("fh1", [P, FF, FF * P])
        fh2 = sb("fh2", [P, FF, FF * P])
        fw3 = sb("fw3", [P, FF, P])
        u = VR[:, 0 * TB:1 * TB, :]
        ubo = VR[:, 1 * TB:2 * TB, :]
        r = VR[:, 2 * TB:3 * TB, :]
        rx = VR[:, 3 * TB:4 * TB, :]
        aT = sb("aT", [P, SEQ])
        vs = xnT[:, 0:0 + 2 * SEQ].rearrange("p (a n) -> p a n", a=2)
        gs = xnT[:, 2 * SEQ:2 * SEQ + 2 * SEQ].rearrange("p (a n) -> p a n", a=2)
        Vflat = V[:, :, :].rearrange("p n k -> p (n k)")
        kv = OG[:, :]
        st = Vflat[:, 0:0 + 2 * SEQ].rearrange("p (a n) -> p a n", a=2)
        qg = Vflat[:, 2 * SEQ:2 * SEQ + 2 * SEQ].rearrange("p (a n) -> p a n", a=2)
        xp = O[:, :, :]
        aT2 = xn2T[:, :]
        sl = HTflat[:, 2 * NT * P:2 * NT * P + 2 * SEQ].rearrange("p (a n) -> p a n", a=2)
        oT = PT[:, 0:2, :, :].rearrange("p i j n -> p (i j) n")
        hA = PT[:, 2, :, :]
        hB = PT[:, 3, :, :]
        yo = sb("yo", [P, TB, P])

        xs_dram = nc.dram_tensor("xs_dram", [DUMP + TOPK * NB * SEQ, P], F32, kind="Internal").ap()
        ys_dram = nc.dram_tensor("ys_dram", [DUMP, P], F32, kind="Internal").ap()

        x_in = [sem(f"x_in{b}") for b in range(NB)]
        par_in = sem("par_in")
        w0_in = sem("w0_in")
        w1_in = sem("w1_in")
        setup = sem("setup")
        bfc = sem("bfc")
        dve0 = sem("dve0")
        var0, rs0, xn0, tp0, tc0, vp0, vc0 = (sem(n) for n in ("var0", "rs0", "xn0", "tp0", "tc0", "vp0", "vc0"))
        l0 = sem("l0")
        lA = sem("lA")
        rs_full, rs_free = sem("rs_full"), sem("rs_free")
        parts = sem("parts")
        padded = sem("padded")
        mx_done = sem("mx_done")
        m_full, m_done = sem("m_full"), sem("m_done")
        ts_full, exp_done = sem("ts_full"), sem("exp_done")
        pv_done, v_ready = sem("pv_done"), sem("v_ready")
        varA, rsA, xnA = sem("varA"), sem("rsA"), sem("xnA")
        og_done, lT = sem("og_done"), sem("lT")
        e_full, e_done = sem("e_full"), sem("e_done")
        oh_done, dl_done, ex_done, pos_done = sem("oh_done"), sem("dl_done"), sem("ex_done"), sem("pos_done")
        zeroed, scattered = sem("zeroed"), sem("scattered")
        ew_in = [sem(f"ew_in{s}") for s in range(2)]
        xs_in = [sem(f"xs_in{s}") for s in range(2)]
        xt_full, xt_done = sem("xt_full"), sem("xt_done")
        h_full, h_done = sem("h_full"), sem("h_done")
        y_full, y_done = sem("y_full"), sem("y_done")
        ys_out = [sem(f"ys_out{s}") for s in range(2)]
        gathered, rows_here = sem("gathered"), sem("rows_here")
        lC = sem("lC")
        v_paced, g_paced = sem("v_paced"), sem("g_paced")
        varC, rsC, lnC = sem("varC"), sem("rsC"), sem("lnC")
        t_full, t_done = sem("t_full"), sem("t_done")
        qkvg = sem("qkvg")
        v_done, k_done, g_done, q_done = sem("v_done"), sem("k_done"), sem("g_done"), sem("q_done")
        o_ready = sem("o_ready")
        lP, lE = sem("lP"), sem("lE")
        row_full, row_done = sem("row_full"), sem("row_done")
        u_in, ubo_done, rx_in, rx_done = sem("u_in"), sem("ubo_done"), sem("rx_in"), sem("rx_done")
        hid_full, hid_done = sem("hid_full"), sem("hid_done")
        a_full, sl_done, a_done = sem("a_full"), sem("sl_done"), sem("a_done")
        y_out, out_done = sem("y_out"), sem("out_done")

        bank = [ps[:, i, :] for i in range(8)]
        tp_bank = bank[7]

        def tiles(ap):
            return ap.rearrange("p (t n) -> p t n", n=P)

        block = ctx.enter_context(nc.Block())

        @block.sync
        def _(sp):
            x_v = d["x"].rearrange("(b t p) n -> b p t n", t=TB, p=P)
            for b in range(NB):
                sp.dma_start(X[:, b * TB:(b + 1) * TB, :], x_v[b]).then_inc(x_in[b], 16)
                if b == 0:
                    sp.dma_start(const[:, :], d["const"]).then_inc(par_in, 16)
                    sp.dma_start(cols[:, :], d["cols"]).then_inc(par_in, 16)
                    for t, n in ((wq, "WQ"), (wk, "WK"), (wv, "WV"), (wo, "WO"), (wr, "Wr")):
                        sp.dma_start(t[:, :], d[n]).then_inc(w0_in, 16)
            for i, n in enumerate(("bo", "b2", "w3_s")):
                sp.dma_start(rows[:, i, :], d[n].partition_broadcast(P)).then_inc(w1_in, 16)
            for e in range(E):
                sp.dma_start(rows[:, 3 + e, :], d["eb2"][e].partition_broadcast(P)).then_inc(w1_in, 16)
            sp.wait_ge(setup, 3)
            zv = xs_dram[0:DUMP, :].rearrange("(p r) n -> p (r n)", p=P)
            for i in range(4):
                sp.dma_start(zv[:, i * 10 * P:(i + 1) * 10 * P], zero[:, :]).then_inc(zeroed, 16)
            for n in ("Wq", "Wk", "Wv", "Wg"):
                sp.dma_start(lw[n][:, :], d[n]).then_inc(w1_in, 16)
            sp.dma_start(lwo[:, :, :], d["Wo"].rearrange("(f p) n -> p f n", p=P)).then_inc(w1_in, 16)
            for t, n in ((lw1, "W1"), (fw1, "w1_w"), (fw2, "w2_w")):
                sp.dma_start(t[:, :], d[n]).then_inc(w1_in, 16)
            for t, n in ((lw2, "W2"), (fh1, "h1_w"), (fh2, "h2_w"), (fw3, "w3_w")):
                sp.dma_start(t[:, :, :], d[n].rearrange("(f p) n -> p f n", p=P)).then_inc(w1_in, 16)

            def load_weights(x, s):
                sp.wait_ge(y_full, x + 1)
                sp.dma_start(W1[:, s, :], d["eW1"][bass.ts(x, P), :]).then_inc(ew_in[s], 16)
                sp.dma_start(W2[:, s, :, :], d["eW2"][bass.ts(x, FF * P), :]
                             .rearrange("(f p) n -> p f n", p=P)).then_inc(ew_in[s], 16)

            def load_rows(x, s):
                sp.wait_ge(xt_full, x + 1)
                sp.dma_start(XS[:, s, :, :], xs_dram[bass.ts(x, SLOTS), :]
                             .rearrange("(j p) n -> p j n", p=P)).then_inc(xs_in[s], 16)

            def send(x, s):
                sp.wait_ge(y_done, x + 2)
                sp.dma_start(ys_dram[bass.ts(x, SLOTS), :].rearrange("(j p) n -> p j n", p=P),
                             YS[:, s, :, :]).then_inc(ys_out[s], 16)

            sp.wait_ge(pv_done, NB * 2 * NG + 2)
            load_weights(0, 0)
            load_weights(1, 1)
            sp.wait_ge(scattered, 16 * TOPK * NT)
            load_rows(0, 0)
            load_rows(1, 1)
            with sp.Fori(0, E // 2 - 1) as it:
                for s in range(2):
                    load_rows(it * 2 + (s + 2), s)
                    send(it * 2 + s, s)
                    load_weights(it * 2 + (s + 2), s)
            send(E - 2, 0)
            send(E - 1, 1)
            with sp.Fori(0, NB) as b:
                sp.wait_ge(y_out, b + 1)
                sp.dma_start(d["out"][bass.ts(b, SEQ), :].rearrange("(t p) n -> p t n", p=P),
                             yo[:, :, :]).then_inc(out_done, 16)
            sp.wait_ge(out_done, 16 * NB)

        @block.gpsimd
        def _(g):
            g.memset(zero[:, :], 0.0).then_inc(setup, 1)
            g.memset(mhalf[:, :], -0.5).then_inc(setup, 1)
            g.memset(V[:, :, :], 0.0).then_inc(setup, 1)
            g.memset(WQS[:, :, 3:4, :], 0.0).then_inc(setup, 1)
            g.memset(WKS[:, :, 3:4, :], 0.0).then_inc(setup, 1)
            g.memset(onesb[:, :], 1.0).then_inc(setup, 1)
            g.memset(seen[:, TB, :], 0.0).then_inc(setup, 1)
            g.wait_ge(setup, 7)
            def first_rsqrt(i, c):
                g.wait_ge(var0, i + 1)
                g.tensor_tensor(rstd0[:, c], veps0[:, c], mhalf[:, c], ALU.pow).then_inc(rs0, 1)

            first_rsqrt(0, slice(0, TB))
            g.wait_ge(w0_in, 80)
            for c in range(3):
                g.tensor_copy(WQS[:, :, c, :], wq[:, :].rearrange("p (h k) -> p h k", k=DK)).then_inc(setup, 1)
                g.tensor_copy(WKS[:, :, c, :], wk[:, :].rearrange("p (h k) -> p h k", k=DK)).then_inc(setup, 1)

            g.wait_ge(setup, 13)
            first_rsqrt(1, slice(TB, NT))
            g.memset(V[:, :, DK:DK + 1], 1.0).then_inc(setup, 1)
            g.wait_ge(setup, 14)

            def rsqrt(seen_sem, done_sem, value):
                g.wait_ge(seen_sem, value)
                g.tensor_tensor(rstd[:, :], veps[:, :], mhalf[:, 0:4], ALU.pow).then_inc(done_sem, 1)

            def scatter(b):
                g.wait_ge(pos_done, b + 1)
                g.sem_inc(g_paced, 1)
                for t in range(TB):
                    for k in range(TOPK):
                        g.indirect_dma_start(
                            out=xs_dram, out_offset=bass.IndirectOffsetOnAxis(ap=posS[:, 2 * t + k:2 * t + k + 1], axis=0),
                            in_=xn[:, t, :], in_offset=None).then_inc(scattered, 16)

            g.wait_ge(zeroed, 64)
            with g.Fori(0, NB) as b:
                rsqrt(varA, rsA, b + 1)
                scatter(b)
            g.wait_ge(ys_out[0], 16 * E // 2)
            g.wait_ge(ys_out[1], 16 * E // 2)

            def gather(b):
                for i in range(2 * TB):
                    c = b * 2 * TB + i
                    g.indirect_dma_start(
                        out=G[:, c, :], out_offset=None, in_=ys_dram,
                        in_offset=bass.IndirectOffsetOnAxis(ap=posG[:, c:c + 1], axis=0)).then_inc(gathered, 16)

            def gather_end(b):
                g.wait_ge(gathered, 16 * 2 * TB * (b + 1))
                g.sem_inc(rows_here, 1)

            def add_bo(c):
                g.wait_ge(u_in, c + 1)
                g.tensor_tensor(ubo[:, :, :], u[:, :, :],
                                rows[:, ROW["bo"]:ROW["bo"] + 1, :].to_broadcast([P, TB, P]), ALU.add).then_inc(ubo_done, 1)

            def add_b2(c):
                g.wait_ge(rx_in, c + 1)
                g.tensor_tensor(rx[:, :, :], rx[:, :, :],
                                rows[:, ROW["b2"]:ROW["b2"] + 1, :].to_broadcast([P, TB, P]), ALU.add).then_inc(rx_done, 1)

            gather(0)
            gather_end(0)
            rsqrt(varC, rsC, 1)
            rsqrt(varC, rsC, 2)
            add_bo(0)
            gather(1)
            gather_end(1)
            rsqrt(varC, rsC, 3)
            rsqrt(varC, rsC, 4)
            gather(2)
            rsqrt(varC, rsC, 5)
            add_b2(0)
            add_bo(1)
            gather_end(2)
            gather(3)
            gather_end(3)

            def layer1(b, attn, prep):
                rsqrt(varC, rsC, VAR(b))
                if attn:
                    rsqrt(varC, rsC, VAR(b) + 1)
                    add_b2(b + 1)
                if prep:
                    rsqrt(varC, rsC, VAR(b) + 2)
                    rsqrt(varC, rsC, VAR(b) + 3)
                    add_bo(b + 2)

            with g.Fori(0, NB - 2) as b:
                layer1(b, True, True)
            layer1(NB - 2, True, False)
            layer1(NB - 1, False, False)

        @block.scalar
        def _(act):
            act.wait_ge(par_in, 32)
            act.activation(identb[:, :], const[:, 0:P], ACT.Copy).then_inc(bfc, 1)
            act.activation(maskb[:, :], const[:, P:2 * P], ACT.Copy).then_inc(bfc, 1)
            act.activation(maskTb[:, :], const[:, 2 * P:3 * P], ACT.Copy).then_inc(bfc, 1)
            act.activation(trib[:, :], tri_f, ACT.Copy).then_inc(bfc, 1)
            act.activation(decay[:, :], cols[:, COL["decay_logit"]:COL["decay_logit"] + LF], ACT.Sigmoid).then_inc(bfc, 1)

            def keep_turned(b):
                act.wait_ge(tp0, b + 1)
                act.activation(xnT[:, b * SEQ:(b + 1) * SEQ], bank[4 + b % 2], ACT.Copy).then_inc(tc0, 1)
                act.wait_ge(vp0, b + 1)
                act.activation(VR[:, b * TB:(b + 1) * TB, :], tiles(bank[6 + b % 2]), ACT.Copy).then_inc(vc0, 1)


            def round_parts(b, g):
                slot = (g * RSU) % 2
                act.wait_ge(rs_full, b * NG * RSU + g * RSU + 1)
                act.activation(rq[:, :], ps[:, 2 * slot, :], ACT.Identity).then_inc(parts, 1)
                act.activation(rk[:, :], ps[:, 2 * slot + 1, :], ACT.Identity, bias=k_one).then_inc(parts, 1)

            def pad(b, g, heads):
                act.wait_ge(rs_free, b * NG * RSU + g * RSU + 3)
                for i in heads:
                    q = slice(32 * i, 32 * i + 32)
                    ins = act.activation(KP[q, g % 2, i, :], KS[q, g % 2, :], ACT.Identity)
                ins.then_inc(padded, 1)

            def gate_exp(tb):
                act.wait_ge(dl_done, tb + 1)
                act.activation(ex[:, :], dl[:, :], ACT.Exp).then_inc(ex_done, 1)

            def store_sums(b, g):
                act.wait_ge(pv_done, b * 2 * NG + 2 * g + 4)
                act.activation(OG[:, :], bank[6], ACT.Identity).then_inc(og_done, 1)

            def attention(b, tail, following):
                act.activation(V[:, :, 0:DK], VR[:, bass.ts(b, TB), :].rearrange("p t (h k) -> p (t h) k", k=DK),
                               ACT.Identity).then_inc(v_ready, 1)
                for g in range(NG):
                    unit = (b, g + 1) if g < NG - 1 else (b + 1, 0) if following else None
                    if unit:
                        round_parts(*unit)
                    for i in range(4):
                        hh = g * 4 + i
                        if i % 2 == 0:
                            act.wait_ge(pv_done, b * 2 * NG + hh // 2 + 1)
                        for j in range(TB):
                            n = hh * TB + j
                            act.wait_ge(ts_full, b * H * TB + n + 1)
                            act.activation(PT[:, i, j, j * P:SEQ], ps[:, 4 + n % 2, 0:SEQ - j * P], ACT.Exp,
                                           scale=float(DK) ** -0.5).then_inc(exp_done, 1)
                        if unit and i < 2:
                            pad(*unit, (2 * i, 2 * i + 1))
                        if g and i == 1:
                            store_sums(b, g - 1)
                    if tail and g == 1:
                        gate_exp(b - 1)
                store_sums(b, NG - 1)

            keep_turned(0)
            keep_turned(1)
            round_parts(0, 0)
            keep_turned(2)
            keep_turned(3)
            act.wait_ge(setup, 14)
            pad(0, 0, (0, 1))
            pad(0, 0, (2, 3))
            attention(0, False, True)
            with act.Fori(1, NB - 1) as b:
                attention(b, True, True)
            attention(NB - 1, True, False)
            gate_exp(NB - 1)

            with act.Fori(0, E // 2) as it:
                for s in range(2):
                    x = it * 2 + s
                    for f in range(FF):
                        act.wait_ge(h_full, x * FF + f + 1)
                        act.activation(HT[:, s, f, :].rearrange("p (a n) -> p a n", a=2),
                                       ps[:, 2 * (f % 2):2 * (f % 2) + 2, 0:HALF], ACT.Gelu,
                                       bias=cols[:, bass.ds(x * FF + (COL["eb1"] + f), 1)]).then_inc(h_done, 1)

            def col(name, f=0):
                return cols[:, COL[name] + f:COL[name] + f + 1]

            def turned(n, dst, **kw):
                act.wait_ge(t_full, n)
                act.activation(dst, bank[4], ACT.Identity, **kw).then_inc(t_done, 1)

            def attn_in(n):
                turned(n, aT[:, :], scale=col("ln1_g"), bias=col("ln1_b"))

            def ffn_in(n):
                turned(n, aT2, scale=col("ln2_g"), bias=col("ln2_b"))

            def vg(c, f):
                if f >= 2:
                    act.wait_ge(k_done, c * LF + f - 1)
                    act.wait_ge(q_done, c * LF + f - 1)
                act.wait_ge(qkvg, c * 4 * LF + 4 * f + 1)
                act.activation(vs[:, f % 2, :], bank[0], ACT.Identity, bias=col("bv", f)).then_inc(v_done, 1)
                act.wait_ge(qkvg, c * 4 * LF + 4 * f + 3)
                act.activation(gs[:, f % 2, :], bank[2], ACT.Sigmoid, bias=col("bg", f)).then_inc(g_done, 1)

            def layer1(b, attn, prep):
                def hidden(n, dst, **kw):
                    act.wait_ge(hid_full, b * 12 + n + 1)
                    act.activation(dst, bank[6 + n % 2], ACT.Gelu, **kw).then_inc(hid_done, 1)

                if attn:
                    vg(b + 1, 0)
                for f in range(FF):
                    hidden(f, hA[:, f, :], bias=col("b1", f))
                if attn:
                    for f in range(1, TURN2_AT):
                        vg(b + 1, f)
                turned(TURN(b), aT2)
                if attn:
                    for f in range(TURN2_AT, LF):
                        vg(b + 1, f)
                for f in range(FF):
                    act.wait_ge(a_full, b * 2 * FF + 2 * f + 1)
                    if f >= 2:
                        act.wait_ge(a_done, b * FF + f - 1)
                    act.activation(sl[:, f % 2, :], bank[f % 2], ACT.Silu, scale=col("w1_s", f)).then_inc(sl_done, 1)
                for f in range(FF):
                    hidden(4 + f, hB[:, f, :], scale=col("h1_s", f))
                if attn:
                    ffn_in(TURN(b) + 1)
                for f in range(FF):
                    hidden(8 + f, hA[:, f, :], scale=col("h2_s", f))
                if prep:
                    attn_in(TURN(b) + 2)

            attn_in(1)
            for f in range(LF):
                vg(0, f)
            attn_in(2)
            ffn_in(3)
            with act.Fori(0, NB - 2) as b:
                layer1(b, True, True)
            layer1(NB - 2, True, False)
            layer1(NB - 1, False, False)

        @block.vector
        def _(v):
            v.sem_inc(rs_free, 2)
            v.sem_inc(exp_done, 2)
            v.sem_inc(pv_done, 2)
            v.sem_inc(hid_done, 1)
            v.sem_inc(xt_done, 1)
            v.sem_inc(h_done, 2)
            v.sem_inc(y_done, 1)
            v.sem_inc(y_full, 2)
            v.sem_inc(xt_full, 2)

            class Order:

                def __init__(self, s, n, it):
                    self.s, self.n, self.it, self.k = s, n, it, 0

                def __call__(self, ins):
                    self.k += 1
                    ins.then_inc(self.s, 1)
                    v.wait_ge(self.s, self.it * self.n + self.k)

            def ln_stats(src, link, var_s):
                v.sem_inc(v_paced, 1)
                for t in range(TB):
                    ins = v.bn_stats(stats[:, t, :], src(t))
                link(ins)
                v.sem_inc(v_paced, 1)
                for t in range(TB):
                    ins = v.bn_aggr(mv[:, t, :], stats[:, t, :])
                link(ins)
                v.tensor_scalar(veps[:, :], mv[:, :, 1], EPS, None, ALU.add).then_inc(var_s, 1)

            def ln_apply(src, dst, rs_s, value, done):
                v.wait_ge(rs_s, value)
                for t in range(TB):
                    ins = v.tensor_scalar(dst(t), src(t), mv[:, t, 0:1], rstd[:, t:t + 1], ALU.subtract, ALU.mult)
                ins.then_inc(done, 1)

            def layernorm(src, dst, link, var_s, rs_s, value, done):
                ln_stats(src, link, var_s)
                ln_apply(src, dst, rs_s, value, done)

            o0 = Order(l0, 0, 0)
            v.wait_ge(setup, 1)
            for i in range(3):
                v.tensor_copy(KP[:, i // 4, i % 4, :], zero[:, 0:SEQ])
            def first_norm(b):
                dst = (xn, O)[b % 2]
                v.wait_ge(rs0, min(b, 1) + 1)
                if b >= 2:
                    v.wait_ge(tp0, b - 1)
                for t in range(b * TB, (b + 1) * TB):
                    ins = v.tensor_scalar(dst[:, t % TB, :], X[:, t, :], mv0[:, t, 0:1], rstd0[:, t:t + 1],
                                          ALU.subtract, ALU.mult)
                ins.then_inc(xn0, 1)

            for ts in (range(0, TB), range(TB, NT)):
                if ts[0]:
                    for i in range(3, 8):
                        v.tensor_copy(KP[:, i // 4, i % 4, :], zero[:, 0:SEQ])
                    v.memset(MX[:, :, :, :].bitcast(F32), 0.0)
                    first_norm(0)
                for t in ts:
                    if t % TB == 0:
                        v.wait_ge(x_in[t // TB], 16)
                        v.sem_inc(v_paced, 1)
                    ins = v.bn_stats(stats0[:, t, :], X[:, t, :])
                o0(ins)
                v.sem_inc(v_paced, 1)
                for t in ts:
                    ins = v.bn_aggr(mv0[:, t, :], stats0[:, t, :])
                o0(ins)
                c = slice(ts[0], ts[-1] + 1)
                v.tensor_scalar(veps0[:, c], mv0[:, c, 1], EPS, None, ALU.add).then_inc(var0, 1)

            NLA = 2 * NG
            NLT = 22

            def make_parts(b, g):
                u0 = g * RSU
                slot = u0 % 2
                v.wait_ge(parts, b * 2 * NG + 2 * g + 2)
                v.scalar_tensor_tensor(out=QS[:, g % 2, :], in0=rq[:, :].bitcast(F32), scalar=q_part,
                                       in1=ps[:, 2 * slot, :], op0=ALU.mult, op1=ALU.add)
                v.scalar_tensor_tensor(out=KS[:, g % 2, :], in0=rk[:, :].bitcast(F32), scalar=k_part,
                                       in1=ps[:, 2 * slot + 1, :], op0=ALU.mult, op1=ALU.add).then_inc(rs_free, 1)

            def row_max(b, g, n):
                t, hp = n // 2, n % 2
                use = g * RSU + 1 + n
                slot = use % 2
                v.wait_ge(rs_full, b * NG * RSU + use + 1)
                v.tensor_reduce(mx[:, t, 2 * hp:2 * hp + 2], ps[:, 2 * slot:2 * slot + 2, 0:(t + 1) * P],
                                AXX, ALU.max).then_inc(rs_free, 1)

            def minus_max(b, g, link):
                v.wait_ge(rs_free, b * NG * RSU + (g + 1) * RSU + 2)
                link(v.tensor_scalar(MX[:, :, :, 24], mx[:, :, :], -1.0, None, ALU.mult))
                v.scalar_tensor_tensor(out=MX[:, :, :, 25], in0=mx[:, :, :], scalar=-1.0,
                                       in1=MX[:, :, :, 24].bitcast(F32), op0=ALU.mult,
                                       op1=ALU.subtract).then_inc(mx_done, 1)

            def add_max(b, g):
                v.wait_ge(m_full, b * NM + MXU[g] + 1)
                v.tensor_tensor(QM[:, g % 2, :], QS[:, g % 2, :].bitcast(F32), tp_bank, ALU.add).then_inc(m_done, 1)

            def attention(b, tail, following):
                link = Order(lA, NLA, b)

                def normalise(g):
                    v.wait_ge(m_full, b * NM + OU[g] + 1)
                    o = tp_bank.rearrange("p (t i k) -> p t i k", t=TB, i=4)
                    rd = rden[:, :].rearrange("p (t i) -> p t i", t=TB)
                    link(v.reciprocal(rd, o[:, :, :, DK]))
                    for t in range(TB):
                        ins = v.tensor_tensor(
                            O[:, t, g * 32:(g + 1) * 32].rearrange("p (i k) -> p i k", k=DK), o[:, t, :, 0:DK],
                            rd[:, t, :].rearrange("p (i a) -> p i a", a=1).to_broadcast([P, 4, DK]), ALU.mult)
                    ins.then_inc(m_done, 1)

                for g in range(NG):
                    minus_max(b, g, link)
                    add_max(b, g)
                    unit = (b, g + 1) if g < NG - 1 else (b + 1, 0) if following else None
                    if unit:
                        make_parts(*unit)
                    for n in range(8):
                        if unit:
                            row_max(*unit, n)
                        if n == 5 and g:
                            normalise(g - 1)
                        if tail and (g, n) in TAIL_AT:
                            tail(TAIL_AT[g, n])
                normalise(NG - 1)
                assert link.k == NLA, link.k

            TAIL_AT = {(0, 1): "turn", (0, 5): "stats", (0, 6): "norm", (1, 1): "turn2", (1, 5): "choose", (2, 1): "place"}

            def tail_of(b):
                link = Order(lT, NLT, b)

                def xt(t):
                    return X[:, bass.ds(b * TB + t, 1), :].rearrange("p a n -> p (a n)")

                def piece(name):
                    parts_of[name]()

                def turn():
                    v.wait_ge(e_full, b * 5 + 1)
                    v.tensor_copy(OT[:, :], tp_bank).then_inc(e_done, 1)

                def stats_():
                    v.wait_ge(e_full, b * 5 + 2)
                    xb = X[:, bass.ts(b, TB), :]
                    v.tensor_tensor(xb, tiles(tp_bank), xb, ALU.add).then_inc(e_done, 1)
                    v.wait_ge(e_done, b * 5 + 2)
                    ln_stats(xt, link, varA)

                def norm():
                    v.wait_ge(scattered, b * 16 * TOPK * TB)
                    ln_apply(xt, lambda t: xn[:, t, :], rsA, b + 1, xnA)

                def turn2():
                    v.wait_ge(e_full, b * 5 + 3)
                    v.tensor_copy(xn2T[:, :], tp_bank).then_inc(e_done, 1)

                def choose():
                    v.wait_ge(e_full, b * 5 + 4)
                    v.tensor_copy(lg[:, :, :], tp_bank[:, 0:TB * E].rearrange("p (t e) -> p t e", e=E)).then_inc(e_done, 1)
                    v.wait_ge(e_done, b * 5 + 4)
                    v.sem_inc(v_paced, 1)
                    for t in range(TB):
                        ins = v.max(top[:, t, :], lg[:, t, :])
                    link(ins)
                    v.sem_inc(v_paced, 1)
                    for t in range(TB):
                        ins = v.max_index(topi[:, t, :], top[:, t, :], lg[:, t, :])
                    link(ins)
                    v.tensor_tensor(dl[:, :], top[:, :, 1], top[:, :, 0], ALU.subtract).then_inc(dl_done, 1)
                    link(v.tensor_copy(topf[:, :].rearrange("p (t k) -> p t k", k=2), topi[:, :, 0:2]))
                    link(v.tensor_tensor(oh[:, :, :],
                                         iota8.rearrange("p (a e) -> p a e", a=1).to_broadcast([P, 8, 8]),
                                         topf[:, :].rearrange("p (n a) -> p n a", a=1).to_broadcast([P, 8, 8]),
                                         ALU.is_equal))
                    ohv = oh[:, :, :].rearrange("p (t k) e -> p t (k e)", k=2)
                    v.tensor_copy(ohb[:, :, :], oh[:, :, :])
                    link(v.tensor_copy(seen[:, 0, :], seen[:, TB, :]))
                    for t in range(TB):
                        link(v.tensor_tensor(seen[:, t + 1, :], seen[:, t, :], ohv[:, t, :], ALU.add))
                    v.tensor_copy(seenb[:, :, :], seen[:, 0:TB, :]).then_inc(oh_done, 1)

                def place():
                    v.wait_ge(e_full, b * 5 + 5)
                    link(v.tensor_copy(rank[:, :, :], tp_bank[:, 0:64].rearrange("p (n e) -> p n e", e=8)))
                    link(v.scalar_tensor_tensor(out=sel[:, :, :], in0=rank[:, :, :], scalar=float(CAP),
                                                in1=oh[:, :, :], op0=ALU.is_le, op1=ALU.mult))
                    link(v.tensor_reduce(keep[:, :], sel[:, :, :], AXX, ALU.add))
                    rv = rank[:, :, :].rearrange("p (t k) e -> p t (k e)", k=2)
                    link(v.tensor_tensor(rv, rv, slot_base.rearrange("p (a n) -> p a n", a=1).to_broadcast([P, TB, 16]), ALU.add))
                    link(v.tensor_tensor(rank[:, :, :], rank[:, :, :], oh[:, :, :], ALU.mult))
                    link(v.tensor_reduce(pos[:, :], rank[:, :, :], AXX, ALU.add))
                    db = dump_row[:, bass.ts(b, 2 * TB)]
                    v.tensor_tensor(posG[:, bass.ts(b, 2 * TB)], pos[:, :], keep[:, :], ALU.mult)
                    link(v.tensor_tensor(pos2[:, :], pos[:, :], db, ALU.subtract))
                    link(v.tensor_tensor(pos2[:, :], pos2[:, :], keep[:, :], ALU.mult))
                    v.tensor_tensor(posS[:, :], pos2[:, :], db, ALU.add).then_inc(pos_done, 1)
                    v.wait_ge(ex_done, b + 1)
                    link(v.tensor_scalar(w1t[:, :], ex[:, :], 1.0, None, ALU.add))
                    link(v.reciprocal(w1t[:, :], w1t[:, :]))
                    wb = wts[:, bass.ts(b, 2 * TB)].rearrange("p (t k) -> p t k", k=2)
                    kb = keep[:, :].rearrange("p (t k) -> p t k", k=2)
                    v.tensor_tensor(wb[:, :, 0], w1t[:, :], kb[:, :, 0], ALU.mult)
                    link(v.tensor_tensor(w1t[:, :], w1t[:, :], ex[:, :], ALU.mult))
                    v.tensor_tensor(wb[:, :, 1], w1t[:, :], kb[:, :, 1], ALU.mult).then_inc(e_done, 1)
                    assert link.k == NLT, link.k

                parts_of = {"turn": turn, "stats": stats_, "norm": norm, "turn2": turn2, "choose": choose, "place": place}
                return piece

            first_norm(1)
            first_norm(2)
            v.wait_ge(par_in, 32)
            make_parts(0, 0)
            first_norm(3)
            for n in range(8):
                row_max(0, 0, n)
            attention(0, None, True)
            with v.Fori(1, NB - 1) as b:
                attention(b, tail_of(b - 1), True)
            attention(NB - 1, tail_of(NB - 2), False)
            last = tail_of(NB - 1)
            for name in TAIL_AT.values():
                last(name)

            v.wait_ge(w1_in, 16 * 23)

            def store_rows(x, s):
                v.wait_ge(xt_full, x + 3)
                v.tensor_copy(XST[:, s, 0:512], bank[6])
                v.tensor_copy(XST[:, s, 512:SLOTS], bank[7][:, 0:P]).then_inc(xt_done, 1)

            def add_b2(x, s, n):
                v.wait_ge(y_full, x + 3)
                v.wait_ge(ys_out[s], n * 16)
                b2 = rows[:, bass.ds(x + ROW["eb2_0"], 1), :]
                v.tensor_tensor(YS[:, s, 0:4, :], tiles(bank[4]), b2.to_broadcast([P, 4, P]), ALU.add)
                v.tensor_tensor(YS[:, s, 4:5, :], tiles(bank[5][:, 0:P]), b2, ALU.add).then_inc(y_done, 1)

            store_rows(0, 0)
            with v.Fori(0, E // 2 - 1) as it:
                store_rows(it * 2 + 1, 1)
                add_b2(it * 2, 0, it)
                store_rows(it * 2 + 2, 0)
                add_b2(it * 2 + 1, 1, it)
            store_rows(E - 1, 1)
            add_b2(E - 2, 0, E // 2 - 1)
            add_b2(E - 1, 1, E // 2 - 1)

            def prepare(c, ln, link):
                def tile_x(t):
                    return X[:, bass.ds(c * TB + t, 1), :].rearrange("p a n -> p (a n)")

                def combine():
                    v.wait_ge(rows_here, c + 1)
                    for k in range(2):
                        for t in range(TB):
                            xt = tile_x(t)
                            gt = G[:, bass.ds(c * 2 * TB + (2 * t + k), 1), :].rearrange("p a n -> p (a n)")
                            wt = wts[:, bass.ds(c * 2 * TB + (2 * t + k), 1)]
                            ins = v.scalar_tensor_tensor(out=xt, in0=gt, scalar=wt, in1=xt, op0=ALU.mult, op1=ALU.add)
                        link(ins)

                def stats1():
                    ln_stats(tile_x, link, varC)

                def apply1(first=isinstance(c, int) and c == 0):
                    if not first:
                        v.wait_ge(ubo_done, c)
                    ln_apply(tile_x, lambda t: u[:, t, :], rsC, ln + 1, u_in)

                def stats2():
                    v.wait_ge(u_in, c + 1)
                    ln_stats(lambda t: u[:, t, :], link, varC)

                def apply2():
                    ln_apply(lambda t: u[:, t, :], lambda t: xp[:, t, :], rsC, ln + 2, lnC)

                return [combine, stats1, apply1, stats2, apply2]

            def attend(c, f, link):
                fb = f % 2
                v.wait_ge(qkvg, c * 4 * LF + 4 * f + 2)
                v.wait_ge(v_done, c * LF + f + 1)
                v.scalar_tensor_tensor(out=kv[:, :], in0=bank[1], scalar=cols[:, COL["bk"] + f:COL["bk"] + f + 1],
                                       in1=vs[:, fb, :], op0=ALU.add, op1=ALU.mult).then_inc(k_done, 1)
                v.wait_ge(k_done, c * LF + f + 1)
                link(v.tensor_tensor_scan(st[:, fb, :], decay[:, f:f + 1].to_broadcast([P, SEQ]), kv[:, :], 0.0,
                                          ALU.mult, ALU.add))
                v.wait_ge(qkvg, c * 4 * LF + 4 * f + 4)
                v.wait_ge(g_done, c * LF + f + 1)
                v.scalar_tensor_tensor(out=qg[:, fb, :], in0=bank[3], scalar=cols[:, COL["bq"] + f:COL["bq"] + f + 1],
                                       in1=gs[:, fb, :], op0=ALU.add, op1=ALU.mult).then_inc(q_done, 1)
                v.wait_ge(q_done, c * LF + f + 1)
                v.scalar_tensor_tensor(out=oT[:, f, :], in0=qg[:, fb, :], scalar=0.125, in1=st[:, fb, :],
                                       op0=ALU.mult, op1=ALU.mult).then_inc(o_ready, 1)

            def residual(c, row, ln, link):
                v.wait_ge(row_full, row)
                v.wait_ge(ubo_done, c + 1)
                v.tensor_tensor(r[:, :, :], tiles(bank[5]), ubo[:, :, :], ALU.add).then_inc(row_done, 1)
                v.wait_ge(row_done, row)
                ln_stats(lambda t: r[:, t, :], link, varC)
                v.tensor_tensor(rx[:, :, :], r[:, :, :], X[:, bass.ts(c, TB), :], ALU.add).then_inc(rx_in, 1)
                ln_apply(lambda t: r[:, t, :], lambda t: xn[:, t, :], rsC, ln + 1, lnC)

            def layer1(b, attn, prep, link):
                xb = X[:, bass.ts(b, TB), :]

                def tile_x(t):
                    return X[:, bass.ds(b * TB + t, 1), :].rearrange("p a n -> p (a n)")

                def second():
                    v.wait_ge(row_full, b * 3 + 2)
                    v.wait_ge(rx_done, b + 1)
                    v.tensor_tensor(xb, tiles(bank[5]), rx[:, :, :], ALU.add).then_inc(row_done, 1)
                    v.wait_ge(row_done, b * 3 + 2)
                    ln_stats(tile_x, link, varC)

                def second_apply():
                    ln_apply(tile_x, lambda t: xn[:, t, :], rsC, VAR(b), lnC)

                if attn:
                    attend(b + 1, 0, link)
                    attend(b + 1, 1, link)
                second()
                if attn:
                    attend(b + 1, 2, link)
                second_apply()
                if attn:
                    for f in range(3, LF):
                        attend(b + 1, f, link)
                for f in range(FF):
                    v.wait_ge(a_full, b * 2 * FF + 2 * f + 2)
                    v.wait_ge(sl_done, b * FF + f + 1)
                    v.scalar_tensor_tensor(out=hA[:, f, :], in0=bank[2 + f % 2],
                                           scalar=cols[:, COL["w2_s"] + f:COL["w2_s"] + f + 1],
                                           in1=sl[:, f % 2, :], op0=ALU.mult, op1=ALU.mult).then_inc(a_done, 1)
                if attn:
                    residual(b + 1, b * 3 + 3, VAR(b), link)
                if prep:
                    for piece in prepare(b + 2, VAR(b) + 1, link):
                        piece()
                v.wait_ge(row_full, b * 3 + (4 if attn else 3))
                v.wait_ge(out_done, b * 16)
                v.tensor_tensor(yo[:, :, :], tiles(bank[5]),
                                rows[:, ROW["w3_s"]:ROW["w3_s"] + 1, :].to_broadcast([P, TB, P]),
                                ALU.mult).then_inc(row_done, 1)
                v.wait_ge(row_done, b * 3 + (4 if attn else 3))
                v.tensor_tensor(yo[:, :, :], yo[:, :, :], xb, ALU.add).then_inc(y_out, 1)

            link = Order(lP, 0, 0)
            for piece in prepare(0, 0, link):
                piece()
            pieces = prepare(1, 2, link)
            for f in range(LF):
                attend(0, f, link)
                if f >= 2 and pieces:
                    pieces.pop(0)()
            residual(0, 1, 4, link)
            NLC = LF + 2 + 2 + 2 + 4
            with v.Fori(0, NB - 2) as b:
                link = Order(lC, NLC, b)
                layer1(b, True, True, link)
                assert link.k == NLC, link.k
            link = Order(lE, 0, 0)
            layer1(NB - 2, True, False, link)
            layer1(NB - 1, False, False, link)

        @block.tensor
        def _(pe):
            pe.wait_ge(par_in, 32)
            pe.wait_ge(w0_in, 80)

            def first_turn(b):
                src = (xn, O)[b % 2]
                pe.wait_ge(xn0, b + 1)
                if b >= 2:
                    pe.wait_ge(tc0, b - 1)
                for t in range(TB):
                    mm = pe.transpose(bank[4 + b % 2][:, t * P:(t + 1) * P], src[:, t, :], ident)
                mm.then_inc(tp0, 1)
                pe.wait_ge(tc0, b + 1)
                if b >= 2:
                    pe.wait_ge(vc0, b - 1)
                for t in range(TB):
                    c = (b * TB + t) * P
                    mm = pe.matmul(bank[6 + b % 2][:, t * P:(t + 1) * P], xnT[:, c:c + P], wv[:, :], start=True, stop=True)
                mm.then_inc(vp0, 1)

            def tail_of(b):
                def piece(name):
                    if name == "turn":
                        for t in range(TB):
                            mm = pe.transpose(tp_bank[:, t * P:(t + 1) * P], O[:, t, :], ident)
                    elif name == "wo":
                        pe.wait_ge(e_done, b * 5 + 1)
                        for t in range(TB):
                            mm = pe.matmul(tp_bank[:, t * P:(t + 1) * P], OT[:, t * P:(t + 1) * P], wo[:, :],
                                           start=True, stop=True)
                    elif name == "turn2":
                        pe.wait_ge(xnA, b + 1)
                        for t in range(TB):
                            mm = pe.transpose(tp_bank[:, t * P:(t + 1) * P], xn[:, t, :], ident)
                    elif name == "logits":
                        pe.wait_ge(e_done, b * 5 + 3)
                        for t in range(TB):
                            mm = pe.matmul(tp_bank[:, t * E:(t + 1) * E], xn2T[:, t * P:(t + 1) * P], wr[:, :],
                                           start=True, stop=True)
                    else:
                        pe.wait_ge(oh_done, b + 1)
                        pe.wait_ge(e_done, b * 5 + 4)
                        for t in range(TB):
                            c = slice(t * 16, (t + 1) * 16)
                            pe.matmul(tp_bank[:, c], trib[:, :], ohb[:, 2 * t:2 * t + 2, :].rearrange("p k e -> p (k e)"),
                                      start=True, stop=False)
                            mm = pe.matmul(tp_bank[:, c], onesb[:, :], seenb[:, t, :], start=False, stop=True)
                    mm.then_inc(e_full, 1)
                return piece

            def slot_of(b, use):
                pe.wait_ge(rs_free, b * NG * RSU + use + 1)
                return use % 2

            def project(b, g):
                s = slot_of(b, g * RSU)
                x = xnT[:, bass.ts(b, SEQ)]
                pe.matmul(ps[:, 2 * s, :], WQS[:, 4 * g:4 * g + 4, :, :].rearrange("p h c k -> p (h c k)"), x,
                          start=True, stop=True)
                pe.matmul(ps[:, 2 * s + 1, :], WKS[:, 4 * g:4 * g + 4, :, :].rearrange("p h c k -> p (h c k)"), x,
                          start=True, stop=True).then_inc(rs_full, 1)

            def row_scores(b, g, n):
                t, hp = n // 2, n % 2
                s = slot_of(b, g * RSU + 1 + n)
                if n == 0:
                    pe.wait_ge(rs_free, b * NG * RSU + g * RSU + 3)
                if n == 4:
                    pe.wait_ge(padded, (b * NG + g) * 2 + 2)
                for a in range(2):
                    i = 2 * hp + a
                    if n < 4:
                        pe.matmul(ps[:, 2 * s + a, 0:(t + 1) * P], QS[32 * i:32 * i + 32, g % 2, t * P:(t + 1) * P],
                                  KS[32 * i:32 * i + 32, g % 2, 0:(t + 1) * P], start=True, stop=False)
                    else:
                        pe.matmul(ps[:, 2 * s + a, 0:(t + 1) * P], QS[:, g % 2, t * P:(t + 1) * P],
                                  KP[:, g % 2, i, 0:(t + 1) * P], start=True, stop=False)
                    mm = pe.matmul(ps[:, 2 * s + a, t * P:(t + 1) * P], identb[:, :], maskb[:, :],
                                   start=False, stop=True)
                mm.then_inc(rs_full, 1)

            def attention(b, tail, following):
                def claim(m, e):
                    pe.wait_ge(m_done, b * NM + m)
                    if tail:
                        pe.wait_ge(e_done, (b - 1) * 5 + e)

                def turn_max(g):
                    claim(MXU[g], (0, 2, 4, 5)[g])
                    pe.wait_ge(mx_done, b * NG + g + 1)
                    for t in range(TB):
                        mm = pe.transpose(tp_bank[:, t * P:(t + 1) * P],
                                          MX[:, t, :, :].rearrange("p i c -> p (i c)").bitcast(F32), ident)
                    mm.then_inc(m_full, 1)

                def key_scores(g, i, js):
                    for j in js:
                        n = (g * 4 + i) * TB + j
                        pe.wait_ge(exp_done, b * H * TB + n + 1)
                        pe.matmul(ps[:, 4 + n % 2, 0:SEQ - j * P], KP[:, g % 2, i, j * P:(j + 1) * P],
                                  QM[:, g % 2, j * P:SEQ], start=True, stop=False)
                        pe.matmul(ps[:, 4 + n % 2, 0:P], identb[:, :], maskTb[:, :],
                                  start=False, stop=True).then_inc(ts_full, 1)

                def values(g, p, js):
                    if 0 in js:
                        pe.wait_ge(exp_done, b * H * TB + (4 * g + 2 * p + 2) * TB + 2)
                        if p == 0:
                            pe.wait_ge(v_ready, b + 1)
                            pe.wait_ge(og_done, b * NG + g)
                    for j in js:
                        for i in (2 * p, 2 * p + 1):
                            mm = pe.matmul(bank[6][32 * i:32 * i + 32, j * P:SEQ], V[:, j * H + g * 4 + i, :],
                                           PT[:, i, j, j * P:SEQ], start=(j == 0), stop=(j == TB - 1),
                                           skip_group_check=True)
                    if TB - 1 in js:
                        mm.then_inc(pv_done, 1)

                def turn_out(g):
                    claim(OU[g], (3, 5, 5, 5)[g])
                    pe.wait_ge(og_done, b * NG + g + 1)
                    for t in range(TB):
                        mm = pe.transpose(tp_bank[:, t * P:(t + 1) * P], OG[:, t * P:(t + 1) * P], ident)
                    mm.then_inc(m_full, 1)

                def piece(m, e, name):
                    if tail:
                        claim(m, e)
                        tail(name)

                for g in range(NG):
                    unit = (b, g + 1) if g < NG - 1 else (b + 1, 0) if following else None
                    if unit:
                        project(*unit)
                    turn_max(g)
                    pe.wait_ge(m_done, b * NM + MXU[g] + 1)
                    for i in range(4):
                        before = (g, 0) if i >= 2 else (g - 1, 1) if g else None
                        if i == 1 and g < 3:
                            piece((1, 2, 4)[g], (0, 2, 4)[g], ("turn", "turn2", "ranks")[g])
                        if i == 3:
                            if g:
                                turn_out(g - 1)
                            if g < 2:
                                piece((1, 3)[g], (1, 3)[g], ("wo", "logits")[g])
                        for half in range(2):
                            key_scores(g, i, (2 * half, 2 * half + 1))
                            if unit:
                                row_scores(*unit, 2 * i + half)
                        if before:
                            values(*before, (0,) if i % 2 == 0 else (1, 2, 3))
                values(NG - 1, 1, range(TB))
                turn_out(NG - 1)

            first_turn(0)
            first_turn(1)
            pe.wait_ge(setup, 13)
            project(0, 0)
            first_turn(2)
            first_turn(3)
            pe.wait_ge(bfc, 4)
            for n in range(8):
                row_scores(0, 0, n)
            pe.wait_ge(vc0, NB)
            attention(0, None, True)
            with pe.Fori(1, NB - 1) as b:
                attention(b, tail_of(b - 1), True)
            attention(NB - 1, tail_of(NB - 2), False)
            last = tail_of(NB - 1)
            pe.wait_ge(m_done, NB * NM)
            for name in ("turn", "wo", "turn2", "logits", "ranks"):
                last(name)

            pe.wait_ge(m_done, NB * NM)
            pe.wait_ge(e_done, NB * 5)

            def turn_rows(x, s, n):
                pe.wait_ge(xs_in[s], n * 16)
                pe.wait_ge(xt_done, x + 1)
                for j in range(ST):
                    mm = pe.transpose(bank[6 + j // 4][:, (j % 4) * P:(j % 4 + 1) * P], XS[:, s, j, :], ident)
                mm.then_inc(xt_full, 1)

            def expert(x, s, n, following):
                pe.wait_ge(xt_done, x + 2)
                pe.wait_ge(ew_in[s], n * 32)
                for f in range(FF):
                    pe.wait_ge(h_done, x * FF + f + 1)
                    for a in range(2):
                        mm = pe.matmul(ps[:, 2 * (f % 2) + a, 0:HALF], W1[:, s, f * P:(f + 1) * P],
                                       XST[:, s, a * HALF:(a + 1) * HALF], start=True, stop=True)
                    mm.then_inc(h_full, 1)
                if following:
                    turn_rows(x + 1, 1 - s, n + s)
                pe.wait_ge(h_done, x * FF + FF + 2)
                pe.wait_ge(y_done, x + 1)
                for j in range(ST):
                    for f in range(FF):
                        mm = pe.matmul(bank[4 + j // 4][:, (j % 4) * P:(j % 4 + 1) * P], HT[:, s, f, j * P:(j + 1) * P],
                                       W2[:, s, f, :], start=(f == 0), stop=(f == FF - 1))
                mm.then_inc(y_full, 1)

            turn_rows(0, 0, 1)
            with pe.Fori(0, E // 2 - 1) as it:
                expert(it * 2, 0, it + 1, True)
                expert(it * 2 + 1, 1, it + 1, True)
            expert(E - 2, 0, E // 2, True)
            expert(E - 1, 1, E // 2, False)

            pe.wait_ge(w1_in, 16 * 23)
            pe.wait_ge(y_done, E + 1)

            def turn(n, src):
                pe.wait_ge(lnC, n)
                pe.wait_ge(t_done, n - 1)
                for t in range(TB):
                    mm = pe.transpose(bank[4][:, t * P:(t + 1) * P], src[:, t, :], ident)
                mm.then_inc(t_full, 1)

            def to_rows(row, src, w, n):
                pe.wait_ge(row_done, row - 1)
                for t in range(TB):
                    for f in range(n):
                        mm = pe.matmul(bank[5][:, t * P:(t + 1) * P], src[:, f, t * P:(t + 1) * P], w[:, f, :],
                                       start=(f == 0), stop=(f == n - 1))
                mm.then_inc(row_full, 1)

            def project1(c, f):
                for m, (n, done) in enumerate((("Wv", v_done), ("Wk", k_done), ("Wg", g_done), ("Wq", q_done))):
                    pe.wait_ge(done, c * LF + f)
                    pe.matmul(bank[m], lw[n][:, f * P:(f + 1) * P], aT[:, :], start=True, stop=True).then_inc(qkvg, 1)

            def layer1(b, attn, prep):
                def hidden(n, products):
                    pe.wait_ge(hid_done, b * 12 + n)
                    for i, (w, x) in enumerate(products):
                        mm = pe.matmul(bank[6 + n % 2], w, x, start=(i == 0), stop=(i == len(products) - 1))
                    mm.then_inc(hid_full, 1)

                if attn:
                    pe.wait_ge(t_done, TURN(b) - 1)
                    project1(b + 1, 0)
                for f in range(FF):
                    hidden(f, [(lw1[:, f * P:(f + 1) * P], aT2)])
                if attn:
                    project1(b + 1, 1)
                pe.wait_ge(hid_done, b * 12 + 5)
                to_rows(b * 3 + 2, hA, lw2, FF)
                if attn:
                    for f in range(2, TURN2_AT):
                        project1(b + 1, f)
                turn(TURN(b), xn)
                if attn:
                    for f in range(TURN2_AT, LF):
                        project1(b + 1, f)
                pe.wait_ge(t_done, TURN(b))
                for f in range(FF):
                    if f >= 2:
                        pe.wait_ge(sl_done, b * FF + f - 1)
                        pe.wait_ge(a_done, b * FF + f - 1)
                    elif attn:
                        pe.wait_ge((v_done, k_done)[f], (b + 2) * LF)
                        pe.wait_ge((g_done, q_done)[f], (b + 2) * LF)
                    pe.matmul(bank[f % 2], fw1[:, f * P:(f + 1) * P], aT2, start=True, stop=True).then_inc(a_full, 1)
                    pe.matmul(bank[2 + f % 2], fw2[:, f * P:(f + 1) * P], aT2, start=True, stop=True).then_inc(a_full, 1)
                if attn:
                    pe.wait_ge(o_ready, (b + 2) * LF)
                    to_rows(b * 3 + 3, oT, lwo, LF)
                pe.wait_ge(a_done, b * FF + FF)
                for f in range(FF):
                    hidden(4 + f, [(fh1[:, c, f * P:(f + 1) * P], hA[:, c, :]) for c in range(FF)])
                if attn:
                    turn(TURN(b) + 1, xn)
                pe.wait_ge(hid_done, b * 12 + 9)
                for f in range(FF):
                    hidden(8 + f, [(fh2[:, c, f * P:(f + 1) * P], hB[:, c, :]) for c in range(FF)])
                if prep:
                    turn(TURN(b) + 2, xp)
                pe.wait_ge(hid_done, b * 12 + 13)
                to_rows(b * 3 + (4 if attn else 3), hA, fw3, FF)

            turn(1, xp)
            pe.wait_ge(t_done, 1)
            for f in range(LF):
                project1(0, f)
            turn(2, xp)
            pe.wait_ge(o_ready, LF)
            to_rows(1, oT, lwo, LF)
            turn(3, xn)
            pe.wait_ge(t_done, 3)
            with pe.Fori(0, NB - 2) as b:
                layer1(b, True, True)
            layer1(NB - 2, True, False)
            layer1(NB - 1, False, False)


def shape_constants():
    import numpy as np
    i = np.arange(P)
    later = i[None, :] > i[:, None]
    c = np.zeros((P, N_CONST), np.float32)
    c[:, 0:P] = np.eye(P)
    c[:, P:2 * P] = np.where(later, NEG, 0.0)
    c[:, 2 * P:3 * P] = np.where(later.T, NEG, 0.0)
    c[:, 3 * P:4 * P] = i[:, None] <= i[None, :]
    at = 4 * P
    for k in range(TOPK):
        for e in range(E):
            c[:, at + k * E + e] = e * SLOTS + k * CAP - 1
    at += 16
    for t in range(NT):
        for k in range(TOPK):
            c[:, at + 2 * t + k] = DUMP + k * NT * P + t * P + i
    at += 2 * NT
    c[:, at:at + 8] = np.arange(8)
    at += 8
    part = (i % 32) // 8
    c[:, at] = np.where(part == 2, -1.0, 0.0)
    c[:, at + 1] = np.where(part == 1, -1.0, np.where(part == 3, 1.0, 0.0))
    c[:, at + 2] = np.where(part == 3, 1.0, 0.0)
    return c


def kernel(**inputs):
    import numpy as np
    import concourse.bacc as _bacc
    from concourse.bass_utils import run_bass_kernel_spmd as _run

    a = {k: np.asarray(v) for k, v in inputs.items()}
    col = lambda x: x.reshape(-1, P).T
    dec = np.repeat(a["L1_attn_decay_logit"], LF * P // H)
    parts = [a["L1_attn_ln1_g"], a["L1_attn_ln1_b"], a["L1_attn_ln2_g"], a["L1_attn_ln2_b"], a["L1_attn_bq"],
             a["L1_attn_bk"], a["L1_attn_bv"], a["L1_attn_bg"], dec, a["L1_attn_b1"], a["L1_ffn_w1_s"],
             a["L1_ffn_w2_s"], a["L1_ffn_h1_s"], a["L1_ffn_h2_s"], a["L0_ffn_b1"]]
    arrays = {
        "x": a["L0_attn_x"].reshape(NT * P, P),
        "const": shape_constants(),
        "cols": np.concatenate([col(p) for p in parts], axis=1),
        "WQ": a["L0_attn_WQ"], "WK": a["L0_attn_WK"], "WV": a["L0_attn_WV"], "WO": a["L0_attn_WO"],
        "Wr": a["L0_ffn_Wr"], "eW1": a["L0_ffn_W1"].reshape(E * P, FF * P), "eW2": a["L0_ffn_W2"].reshape(E * FF * P, P),
        "eb2": a["L0_ffn_b2"], "bo": a["L1_attn_bo"], "b2": a["L1_attn_b2"], "w3_s": a["L1_ffn_w3_s"],
        "Wq": a["L1_attn_Wq"], "Wk": a["L1_attn_Wk"], "Wv": a["L1_attn_Wv"], "Wg": a["L1_attn_Wg"],
        "Wo": a["L1_attn_Wo"], "W1": a["L1_attn_W1"], "W2": a["L1_attn_W2"],
        "w1_w": a["L1_ffn_w1_w"].T, "w2_w": a["L1_ffn_w2_w"].T, "h1_w": a["L1_ffn_h1_w"].T,
        "h2_w": a["L1_ffn_h2_w"].T, "w3_w": a["L1_ffn_w3_w"].T,
    }
    arrays = {f"in_{k}": np.ascontiguousarray(v) for k, v in arrays.items()}
    nc = _bacc.Bacc("TRN2", target_bir_lowering=False, num_devices=1)
    d = {k[3:]: nc.dram_tensor(k, v.shape, mybir.dt.from_np(v.dtype), kind="ExternalInput").ap() for k, v in arrays.items()}
    d["out"] = nc.dram_tensor("out_dram", (NT * P, P), F32, kind="ExternalOutput").ap()
    build(nc, d)
    res = _run(nc, [arrays], core_ids=[0])
    return res.results[0]["out_dram"].reshape(NB, SEQ, P)
```

```python
from contextlib import ExitStack

import concourse.bass as bass
from concourse import mybir

ALU = mybir.AluOpType
ACT = mybir.ActivationFunctionType
AXX = mybir.AxisListType.X
F32 = mybir.dt.float32
F32R = mybir.dt.float32r
BF16 = mybir.dt.bfloat16
U32 = mybir.dt.uint32

P = 128
NB = 4
TB = 4
SEQ = TB * P
NT = NB * TB
H = 16
DK = P // H
NG = 4
E = 8
TOPK = 2
CAP = int(NB * SEQ * 1.25 / E)
SLOTS = TOPK * CAP
ST = SLOTS // P
HALF = SLOTS // 2
FF = 4
LF = 8
EPS = 1e-5
DUMP = E * SLOTS
NEG = -1e30
NM = 2 * NG
MXU = (0, 1, 3, 5)
OU = (2, 4, 6, 7)
ROWN = [(2, (0, 1)), (3, (0, 1)), (2, (2, 3)), (3, (2, 3)), (1, (0, 1, 2, 3)), (0, (0, 1, 2, 3))]
RSU = 1 + len(ROWN)
KC = [(0,), (1,), (2, 3)]
NK = len(KC)
OFF = [sum(SEQ - i * P for i in range(j)) for j in range(TB + 1)]
N_CONST = 4 * P + 16 + 2 * NT + 8 + 3

TURN2_AT = 5

COLS = [("ln1_g", 1), ("ln1_b", 1), ("ln2_g", 1), ("ln2_b", 1), ("bq", LF), ("bk", LF), ("bv", LF), ("bg", LF),
        ("decay_logit", LF), ("b1", FF), ("w1_s", FF), ("w2_s", FF), ("h1_s", FF), ("h2_s", FF), ("eb1", E * FF)]
COL = {}
_at = 0
for _name, _n in COLS:
    COL[_name] = _at
    _at += _n
N_COLS = _at
ROWS = ["bo", "b2", "w3_s"] + [f"eb2_{e}" for e in range(E)]
ROW = {n: i for i, n in enumerate(ROWS)}


def TURN(b):
    return b * 3 + 3 if isinstance(b, int) and b == NB - 1 else b * 3 + 4


def VAR(b):
    return b * 4 + 4 if isinstance(b, int) and b == NB - 1 else b * 4 + 6


def ROWS_OUT(b):
    if isinstance(b, int) and b >= NB - 2:
        return 3 * NB - (NB - 1 - b)
    return b * 3 + 4


def build(nc, d):
    ctx = ExitStack()
    with ctx:
        def sb(name, shape, dt=F32):
            return ctx.enter_context(nc.sbuf_tensor(name, shape, dt))

        def sem(name):
            return ctx.enter_context(nc.semaphore(name))

        ps = ctx.enter_context(nc.psum_tensor("ps", [P, 8, 512], F32))

        X = sb("X", [P, NT, P])
        const = sb("const", [P, N_CONST])
        cols = sb("cols", [P, N_COLS])
        rows = sb("rows", [P, len(ROWS), P])
        ident = const[:, 0:P]
        tri_f = const[:, 3 * P:4 * P]
        slot_base = const[:, 4 * P:4 * P + 16]
        dump_row = const[:, 4 * P + 16:4 * P + 16 + 2 * NT]
        iota8 = const[:, 4 * P + 16 + 2 * NT:4 * P + 24 + 2 * NT]
        c0 = 4 * P + 24 + 2 * NT
        q_part, k_part, k_one = const[:, c0:c0 + 1], const[:, c0 + 1:c0 + 2], const[:, c0 + 2:c0 + 3]
        identb = sb("identb", [P, P], BF16)
        maskb = sb("maskb", [P, P], BF16)
        maskTb = sb("maskTb", [P, P], BF16)
        trib = sb("trib", [P, P], BF16)
        onesb = sb("onesb", [P, P], BF16)
        mhalf = sb("mhalf", [P, NT])
        decay = sb("decay", [P, LF])

        wq = sb("wq", [P, P])
        wk = sb("wk", [P, P])
        wv = sb("wv", [P, P])
        wo = sb("wo", [P, P])
        WQS = sb("WQS", [P, H, 4, DK])
        WKS = sb("WKS", [P, H, 4, DK])
        xnT = sb("xnT", [P, NB * SEQ])
        V = sb("V", [P, TB * H, 32])
        rq = sb("rq", [P, SEQ], F32R)
        rk = sb("rk", [P, SEQ], F32R)
        QS = sb("QS", [P, 2, SEQ], F32R)
        KS = sb("KS", [P, 2, SEQ], F32R)
        QM = sb("QM", [P, 2, SEQ], F32R)
        KP = sb("KP", [P, 2, 4, SEQ], F32R)
        mx = sb("mx", [P, TB, 4])
        MX = sb("MX", [P, TB, 4, 32], F32R)
        PTflat = sb("PT", [P, 4 * TB * SEQ])[:, :]
        PT = PTflat[:, 0:4 * OFF[TB]].rearrange("p (i n) -> p i n", i=4)
        rden = sb("rden", [P, TB * 4])
        O = sb("O", [P, TB, P])
        VR = sb("VR", [P, NT, P])
        OG = sb("OG", [P, SEQ])
        OT = sb("OT", [P, SEQ])

        stats = sb("stats", [P, 4, 6])
        mv = sb("mv", [P, 4, 2])
        veps = sb("veps", [P, 4])
        rstd = sb("rstd", [P, 4])
        xn = sb("xn", [P, TB, P])

        stats0 = sb("stats0", [P, NT, 6])
        mv0 = sb("mv0", [P, NT, 2])
        veps0 = sb("veps0", [P, NT])
        rstd0 = sb("rstd0", [P, NT])

        wr = sb("wr", [P, E])
        xn2T = sb("xn2T", [P, SEQ])
        lg = sb("lg", [P, TB, E])
        top = sb("top", [P, TB, 8])
        topi = sb("topi", [P, TB, 8], U32)
        topf = sb("topf", [P, 8])
        oh = sb("oh", [P, 8, 8])
        ohb = sb("ohb", [P, 8, 8], BF16)
        here = sb("here", [P, 16])
        seen = sb("seen", [P, 16])
        seenb = sb("seenb", [P, 16], BF16)
        rank = sb("rank", [P, 8, 8])
        sel = sb("sel", [P, 8, 8])
        keep = sb("keep", [P, 8])
        pos = sb("pos", [P, 8])
        pos2 = sb("pos2", [P, 8])
        posS = sb("posS", [P, 8], U32)
        posG = sb("posG", [P, 2 * NT], U32)
        dl = sb("dl", [P, TB])
        ex = sb("ex", [P, TB])
        w1t = sb("w1t", [P, TB])
        wts = sb("wts", [P, 2 * NT])

        zero = sb("zero", [P, 10 * P])
        _w, _x = 2 * FF * P, 2 * SLOTS
        W1 = PTflat[:, 0:_w].rearrange("p (s n) -> p s n", s=2)
        W2 = PTflat[:, _w:2 * _w].rearrange("p (s f n) -> p s f n", s=2, f=FF)
        XS = PTflat[:, 2 * _w:2 * _w + _x].rearrange("p (s j n) -> p s j n", s=2, j=ST)
        XST = PTflat[:, 2 * _w + _x:2 * _w + 2 * _x].rearrange("p (s n) -> p s n", s=2)
        HT = sb("HT", [P, 2, FF, SLOTS])
        HTflat = HT[:, :, :, :].rearrange("p s f n -> p (s f n)")
        YS = zero[:, :].rearrange("p (s j n) -> p s j n", s=2, n=P)
        G = HTflat[:, 0:2 * NT * P].rearrange("p (n c) -> p n c", c=P)

        lw = {n: sb("lw_" + n, [P, LF * P]) for n in ("Wq", "Wk", "Wv", "Wg")}
        lwo = sb("lwo", [P, LF, P])
        lw1 = sb("lw1", [P, FF * P])
        lw2 = sb("lw2", [P, FF, P])
        fw1 = sb("fw1", [P, FF * P])
        fw2 = sb("fw2", [P, FF * P])
        fh1 = sb("fh1", [P, FF, FF * P])
        fh2 = sb("fh2", [P, FF, FF * P])
        fw3 = sb("fw3", [P, FF, P])
        u = VR[:, 0 * TB:1 * TB, :]
        ubo = VR[:, 1 * TB:2 * TB, :]
        r = VR[:, 2 * TB:3 * TB, :]
        rx = VR[:, 3 * TB:4 * TB, :]
        aT = sb("aT", [P, SEQ])
        vs = xnT[:, 0:0 + 2 * SEQ].rearrange("p (a n) -> p a n", a=2)
        gs = xnT[:, 2 * SEQ:2 * SEQ + 2 * SEQ].rearrange("p (a n) -> p a n", a=2)
        Vflat = V[:, :, :].rearrange("p n k -> p (n k)")
        kv = OG[:, :]
        st = Vflat[:, 0:0 + 2 * SEQ].rearrange("p (a n) -> p a n", a=2)
        qg = Vflat[:, 2 * SEQ:2 * SEQ + 2 * SEQ].rearrange("p (a n) -> p a n", a=2)
        xp = O[:, :, :]
        aT2 = xn2T[:, :]
        sl = HTflat[:, 2 * NT * P:2 * NT * P + 2 * SEQ].rearrange("p (a n) -> p a n", a=2)
        oT = PTflat[:, 0:LF * SEQ].rearrange("p (f n) -> p f n", f=LF)
        hA = PTflat[:, LF * SEQ:(LF + FF) * SEQ].rearrange("p (f n) -> p f n", f=FF)
        hB = PTflat[:, (LF + FF) * SEQ:(LF + 2 * FF) * SEQ].rearrange("p (f n) -> p f n", f=FF)
        yo = sb("yo", [P, TB, P])

        xs_dram = nc.dram_tensor("xs_dram", [DUMP + TOPK * NB * SEQ, P], F32, kind="Internal").ap()
        ys_dram = nc.dram_tensor("ys_dram", [DUMP, P], F32, kind="Internal").ap()

        x_in = [sem(f"x_in{b}") for b in range(NB)]
        par_in = sem("par_in")
        w0_in = sem("w0_in")
        w1_in = sem("w1_in")
        setup = sem("setup")
        bfc = sem("bfc")
        var0, rs0, xn0, tp0, tc0, vp0, vc0 = (sem(n) for n in ("var0", "rs0", "xn0", "tp0", "tc0", "vp0", "vc0"))
        l0, lA, lT, lP, lC, lE = (sem(n) for n in ("l0", "lA", "lT", "lP", "lC", "lE"))
        rs_full, rs_free = sem("rs_full"), sem("rs_free")
        parts = sem("parts")
        padded = sem("padded")
        mx_done = sem("mx_done")
        m_full, m_done = sem("m_full"), sem("m_done")
        ts_full, exp_done = sem("ts_full"), sem("exp_done")
        pv_done, v_ready = sem("pv_done"), sem("v_ready")
        varA, rsA, xnA = sem("varA"), sem("rsA"), sem("xnA")
        og_done = sem("og_done")
        e_full, e_done = sem("e_full"), sem("e_done")
        oh_done, dl_done, ex_done, pos_done = sem("oh_done"), sem("dl_done"), sem("ex_done"), sem("pos_done")
        zeroed, scattered = sem("zeroed"), sem("scattered")
        ew_in = [sem(f"ew_in{s}") for s in range(2)]
        xs_in = [sem(f"xs_in{s}") for s in range(2)]
        xt_full, xt_done = sem("xt_full"), sem("xt_done")
        h_full, h_done = sem("h_full"), sem("h_done")
        y_full, y_done = sem("y_full"), sem("y_done")
        ys_out = [sem(f"ys_out{s}") for s in range(2)]
        rows_in = [sem(f"rows_in{t}") for t in range(TB)]
        gathered, rows_here = sem("gathered"), sem("rows_here")
        v_paced, g_paced = sem("v_paced"), sem("g_paced")
        varC, rsC, lnC = sem("varC"), sem("rsC"), sem("lnC")
        t_full, t_done = sem("t_full"), sem("t_done")
        qkvg = sem("qkvg")
        v_done, k_done, g_done, q_done = sem("v_done"), sem("k_done"), sem("g_done"), sem("q_done")
        o_ready = sem("o_ready")
        row_full, row_done = sem("row_full"), sem("row_done")
        u_in, ubo_done, rx_in, rx_done = sem("u_in"), sem("ubo_done"), sem("rx_in"), sem("rx_done")
        hid_full, hid_done = sem("hid_full"), sem("hid_done")
        a_full, sl_done, a_done = sem("a_full"), sem("sl_done"), sem("a_done")
        y_out, out_done = sem("y_out"), sem("out_done")

        bank = [ps[:, i, :] for i in range(8)]
        tp_bank = bank[7]

        def tiles(ap):
            return ap.rearrange("p (t n) -> p t n", n=P)

        block = ctx.enter_context(nc.Block())

        @block.sync
        def _(sp):
            x_v = d["x"].rearrange("(b t p) n -> b p t n", t=TB, p=P)
            for b in range(NB):
                sp.dma_start(X[:, b * TB:(b + 1) * TB, :], x_v[b]).then_inc(x_in[b], 16)
                if b == 0:
                    sp.dma_start(const[:, :], d["const"]).then_inc(par_in, 16)
                    sp.dma_start(cols[:, :], d["cols"]).then_inc(par_in, 16)
                    for t, n in ((wq, "WQ"), (wk, "WK"), (wv, "WV"), (wo, "WO"), (wr, "Wr")):
                        sp.dma_start(t[:, :], d[n]).then_inc(w0_in, 16)
            for i, n in enumerate(("bo", "b2", "w3_s")):
                sp.dma_start(rows[:, i, :], d[n].partition_broadcast(P)).then_inc(w1_in, 16)
            for e in range(E):
                sp.dma_start(rows[:, 3 + e, :], d["eb2"][e].partition_broadcast(P)).then_inc(w1_in, 16)
            sp.wait_ge(setup, 3)
            zv = xs_dram[0:DUMP, :].rearrange("(p r) n -> p (r n)", p=P)
            for i in range(4):
                sp.dma_start(zv[:, i * 10 * P:(i + 1) * 10 * P], zero[:, :]).then_inc(zeroed, 16)
            for n in ("Wq", "Wk", "Wv", "Wg"):
                sp.dma_start(lw[n][:, :], d[n]).then_inc(w1_in, 16)
            sp.dma_start(lwo[:, :, :], d["Wo"].rearrange("(f p) n -> p f n", p=P)).then_inc(w1_in, 16)
            for t, n in ((lw1, "W1"), (fw1, "w1_w"), (fw2, "w2_w")):
                sp.dma_start(t[:, :], d[n]).then_inc(w1_in, 16)
            for t, n in ((lw2, "W2"), (fh1, "h1_w"), (fh2, "h2_w"), (fw3, "w3_w")):
                sp.dma_start(t[:, :, :], d[n].rearrange("(f p) n -> p f n", p=P)).then_inc(w1_in, 16)

            def load_weights(x, s):
                sp.wait_ge(y_full, x + 1)
                sp.dma_start(W1[:, s, :], d["eW1"][bass.ts(x, P), :]).then_inc(ew_in[s], 16)
                sp.dma_start(W2[:, s, :, :], d["eW2"][bass.ts(x, FF * P), :]
                             .rearrange("(f p) n -> p f n", p=P)).then_inc(ew_in[s], 16)

            def load_rows(x, s):
                sp.wait_ge(xt_full, x + 1)
                sp.dma_start(XS[:, s, :, :], xs_dram[bass.ts(x, SLOTS), :]
                             .rearrange("(j p) n -> p j n", p=P)).then_inc(xs_in[s], 16)

            def send(x, s):
                sp.wait_ge(y_done, x + 2)
                sp.dma_start(ys_dram[bass.ts(x, SLOTS), :].rearrange("(j p) n -> p j n", p=P),
                             YS[:, s, :, :]).then_inc(ys_out[s], 16)

            sp.wait_ge(pv_done, NB * 2 * NG + 2)
            load_weights(0, 0)
            load_weights(1, 1)
            sp.wait_ge(scattered, 16 * TOPK * NT)
            load_rows(0, 0)
            load_rows(1, 1)
            with sp.Fori(0, E // 2 - 1) as it:
                for s in range(2):
                    load_rows(it * 2 + (s + 2), s)
                    send(it * 2 + s, s)
                    load_weights(it * 2 + (s + 2), s)
            send(E - 2, 0)
            send(E - 1, 1)
            with sp.Fori(0, NB) as b:
                sp.wait_ge(y_out, b + 1)
                sp.dma_start(d["out"][bass.ts(b, SEQ), :].rearrange("(t p) n -> p t n", p=P),
                             yo[:, :, :]).then_inc(out_done, 16)
            sp.wait_ge(out_done, 16 * NB)

        @block.gpsimd
        def _(g):
            g.memset(zero[:, :], 0.0).then_inc(setup, 1)
            g.memset(mhalf[:, :], -0.5).then_inc(setup, 1)
            g.memset(V[:, :, :], 0.0).then_inc(setup, 1)
            g.memset(WQS[:, :, 3:4, :], 0.0).then_inc(setup, 1)
            g.memset(WKS[:, :, 3:4, :], 0.0).then_inc(setup, 1)
            g.memset(onesb[:, :], 1.0).then_inc(setup, 1)
            g.memset(seen[:, :], 0.0)
            g.memset(seenb[:, :], 0.0).then_inc(setup, 1)
            g.wait_ge(setup, 7)
            def first_rsqrt(i, c):
                g.wait_ge(var0, i + 1)
                g.tensor_tensor(rstd0[:, c], veps0[:, c], mhalf[:, c], ALU.pow).then_inc(rs0, 1)

            first_rsqrt(0, slice(0, TB))
            g.wait_ge(w0_in, 80)
            for c in range(3):
                g.tensor_copy(WQS[:, :, c, :], wq[:, :].rearrange("p (h k) -> p h k", k=DK)).then_inc(setup, 1)
                g.tensor_copy(WKS[:, :, c, :], wk[:, :].rearrange("p (h k) -> p h k", k=DK)).then_inc(setup, 1)

            g.wait_ge(setup, 13)
            first_rsqrt(1, slice(TB, NT))
            g.memset(V[:, :, DK:DK + 1], 1.0).then_inc(setup, 1)
            g.wait_ge(setup, 14)

            def rsqrt(seen_sem, done_sem, value):
                g.wait_ge(seen_sem, value)
                g.tensor_tensor(rstd[:, :], veps[:, :], mhalf[:, 0:4], ALU.pow).then_inc(done_sem, 1)

            def scatter(b):
                g.wait_ge(pos_done, b + 1)
                g.sem_inc(g_paced, 1)
                for t in range(TB):
                    for k in range(TOPK):
                        g.indirect_dma_start(
                            out=xs_dram, out_offset=bass.IndirectOffsetOnAxis(ap=posS[:, 2 * t + k:2 * t + k + 1], axis=0),
                            in_=xn[:, t, :], in_offset=None).then_inc(scattered, 16)

            g.wait_ge(zeroed, 64)
            with g.Fori(0, NB) as b:
                rsqrt(varA, rsA, b + 1)
                scatter(b)
            g.wait_ge(ys_out[0], 16 * E // 2)
            g.wait_ge(ys_out[1], 16 * E // 2)

            def gather(b):
                for i in range(2 * TB):
                    c = b * 2 * TB + i
                    g.indirect_dma_start(
                        out=G[:, c, :], out_offset=None, in_=ys_dram,
                        in_offset=bass.IndirectOffsetOnAxis(ap=posG[:, c:c + 1], axis=0)).then_inc(gathered, 16)

            def gather_end(b):
                g.wait_ge(gathered, 16 * 2 * TB * b)
                g.sem_inc(rows_here, 1)

            def add_bo(c):
                g.wait_ge(u_in, c + 1)
                g.tensor_tensor(ubo[:, :, :], u[:, :, :],
                                rows[:, ROW["bo"]:ROW["bo"] + 1, :].to_broadcast([P, TB, P]), ALU.add).then_inc(ubo_done, 1)

            def add_b2(c):
                g.wait_ge(rx_in, c + 1)
                g.tensor_tensor(rx[:, :, :], rx[:, :, :],
                                rows[:, ROW["b2"]:ROW["b2"] + 1, :].to_broadcast([P, TB, P]), ALU.add).then_inc(rx_done, 1)

            for t in range(TB):
                for c in (2 * t, 2 * t + 1):
                    g.indirect_dma_start(
                        out=G[:, c, :], out_offset=None, in_=ys_dram,
                        in_offset=bass.IndirectOffsetOnAxis(ap=posG[:, c:c + 1], axis=0)).then_inc(rows_in[t], 16)
            rsqrt(varC, rsC, 1)
            rsqrt(varC, rsC, 2)
            add_bo(0)
            gather(1)
            gather_end(1)
            rsqrt(varC, rsC, 3)
            rsqrt(varC, rsC, 4)
            gather(2)
            rsqrt(varC, rsC, 5)
            add_b2(0)
            add_bo(1)
            gather_end(2)
            gather(3)
            gather_end(3)

            def layer1(b, attn, prep):
                rsqrt(varC, rsC, VAR(b))
                if attn:
                    rsqrt(varC, rsC, VAR(b) + 1)
                    add_b2(b + 1)
                if prep:
                    rsqrt(varC, rsC, VAR(b) + 2)
                    rsqrt(varC, rsC, VAR(b) + 3)
                    add_bo(b + 2)

            with g.Fori(0, NB - 2) as b:
                layer1(b, True, True)
            layer1(NB - 2, True, False)
            layer1(NB - 1, False, False)

        @block.scalar
        def _(act):
            act.wait_ge(par_in, 32)
            act.activation(identb[:, :], const[:, 0:P], ACT.Copy).then_inc(bfc, 1)
            act.activation(maskb[:, :], const[:, P:2 * P], ACT.Copy).then_inc(bfc, 1)
            act.activation(maskTb[:, :], const[:, 2 * P:3 * P], ACT.Copy).then_inc(bfc, 1)
            act.activation(trib[:, :], tri_f, ACT.Copy).then_inc(bfc, 1)
            act.activation(decay[:, :], cols[:, COL["decay_logit"]:COL["decay_logit"] + LF], ACT.Sigmoid).then_inc(bfc, 1)

            def keep_turned(b):
                act.wait_ge(tp0, b + 1)
                act.activation(xnT[:, b * SEQ:(b + 1) * SEQ], bank[4 + b % 2], ACT.Copy).then_inc(tc0, 1)
                act.wait_ge(vp0, b + 1)
                act.activation(VR[:, b * TB:(b + 1) * TB, :], tiles(bank[6 + b % 2]), ACT.Copy).then_inc(vc0, 1)


            def round_parts(b, g):
                slot = (g * RSU) % 2
                act.wait_ge(rs_full, b * NG * RSU + g * RSU + 1)
                act.activation(rq[:, :], ps[:, 2 * slot, :], ACT.Identity).then_inc(parts, 1)
                act.activation(rk[:, :], ps[:, 2 * slot + 1, :], ACT.Identity, bias=k_one).then_inc(parts, 1)

            def pad(b, g, i):
                act.wait_ge(rs_free, b * NG * RSU + g * RSU + 3)
                q = slice(32 * i, 32 * i + 32)
                act.activation(KP[q, g % 2, i, :], KS[q, g % 2, :], ACT.Identity).then_inc(padded, 1)

            def gate_exp(tb):
                act.wait_ge(dl_done, tb + 1)
                act.activation(ex[:, :], dl[:, :], ACT.Exp).then_inc(ex_done, 1)

            def store_sums(b, g):
                act.wait_ge(pv_done, b * 2 * NG + 2 * g + 4)
                act.activation(OG[:, :], bank[6], ACT.Identity).then_inc(og_done, 1)

            def attention(b, tail, following):
                act.activation(V[:, :, 0:DK], VR[:, bass.ts(b, TB), :].rearrange("p t (h k) -> p (t h) k", k=DK),
                               ACT.Identity).then_inc(v_ready, 1)
                for g in range(NG):
                    unit = (b, g + 1) if g < NG - 1 else (b + 1, 0) if following else None
                    if unit:
                        round_parts(*unit)
                    for i in range(4):
                        hh = g * 4 + i
                        if i % 2 == 0:
                            act.wait_ge(pv_done, b * 2 * NG + hh // 2 + 1)
                        for c, js in enumerate(KC):
                            n = hh * NK + c
                            a, z = OFF[js[0]], OFF[js[-1] + 1]
                            act.wait_ge(ts_full, b * H * NK + n + 1)
                            act.activation(PT[:, i, a:z], ps[:, 4 + n % 2, 0:z - a], ACT.Exp,
                                           scale=float(DK) ** -0.5).then_inc(exp_done, 1)
                            if unit and i < 2 and c:
                                pad(*unit, 2 * i + c - 1)
                        if g and i == 1:
                            store_sums(b, g - 1)
                    if tail and g == 2:
                        gate_exp(b - 1)
                store_sums(b, NG - 1)

            keep_turned(0)
            keep_turned(1)
            round_parts(0, 0)
            keep_turned(2)
            keep_turned(3)
            act.wait_ge(setup, 14)
            for i in range(4):
                pad(0, 0, i)
            attention(0, False, True)
            with act.Fori(1, NB - 1) as b:
                attention(b, True, True)
            attention(NB - 1, True, False)
            gate_exp(NB - 1)

            with act.Fori(0, E // 4) as it:
                for s in range(4):
                    x = it * 4 + s
                    for f in range(FF):
                        act.wait_ge(h_full, x * FF + f + 1)
                        act.activation(HT[:, s % 2, f, :].rearrange("p (a n) -> p a n", a=2),
                                       ps[:, 2 * (f % 2):2 * (f % 2) + 2, 0:HALF], ACT.Gelu,
                                       bias=cols[:, bass.ds(x * FF + (COL["eb1"] + f), 1)]).then_inc(h_done, 1)

            def col(name, f=0):
                return cols[:, COL[name] + f:COL[name] + f + 1]

            def turned(n, dst, **kw):
                act.wait_ge(t_full, n)
                act.activation(dst, bank[4], ACT.Identity, **kw).then_inc(t_done, 1)

            def attn_in(n):
                turned(n, aT[:, :], scale=col("ln1_g"), bias=col("ln1_b"))

            def ffn_in(n):
                turned(n, aT2, scale=col("ln2_g"), bias=col("ln2_b"))

            def vg(c, f):
                if f >= 2:
                    act.wait_ge(k_done, c * LF + f - 1)
                    act.wait_ge(q_done, c * LF + f - 1)
                act.wait_ge(qkvg, c * 4 * LF + 4 * f + 1)
                act.activation(vs[:, f % 2, :], bank[0], ACT.Identity, bias=col("bv", f)).then_inc(v_done, 1)
                act.wait_ge(qkvg, c * 4 * LF + 4 * f + 3)
                act.activation(gs[:, f % 2, :], bank[2], ACT.Sigmoid, bias=col("bg", f)).then_inc(g_done, 1)

            def layer1(b, attn, prep):
                def hidden(n, dst, **kw):
                    act.wait_ge(hid_full, b * 12 + n + 1)
                    act.activation(dst, bank[6 + n % 2], ACT.Gelu, **kw).then_inc(hid_done, 1)

                last = not attn
                early = attn and not prep
                if not last:
                    for f in range(FF):
                        hidden(f, hA[:, f, :], bias=col("b1", f))
                if attn:
                    for f in range(1, TURN2_AT):
                        vg(b + 1, f)
                if not last:
                    turned(TURN(b), aT2)
                if attn:
                    for f in range(TURN2_AT, LF):
                        vg(b + 1, f)
                for f in range(FF):
                    act.wait_ge(a_full, b * 2 * FF + 2 * f + 1)
                    if f >= 2:
                        act.wait_ge(a_done, b * FF + f - 1)
                    act.activation(sl[:, f % 2, :], bank[f % 2], ACT.Silu, scale=col("w1_s", f)).then_inc(sl_done, 1)
                for f in range(FF):
                    hidden(4 + f, hB[:, f, :], scale=col("h1_s", f))
                if attn:
                    ffn_in(TURN(b) + 1)
                if early:
                    for f in range(FF):
                        hidden(8 + f, oT[:, f, :], bias=col("b1", f))
                for f in range(FF):
                    hidden((12 if early else 8) + f, hA[:, f, :], scale=col("h2_s", f))
                if early:
                    turned(TURN(NB - 1), aT2)
                if prep:
                    attn_in(TURN(b) + 2)
                    vg(b + 2, 0)

            attn_in(1)
            for f in range(LF):
                vg(0, f)
            attn_in(2)
            vg(1, 0)
            ffn_in(3)
            with act.Fori(0, NB - 2) as b:
                layer1(b, True, True)
            layer1(NB - 2, True, False)
            layer1(NB - 1, False, False)

        @block.vector
        def _(v):
            v.sem_inc(rs_free, 2)
            v.sem_inc(exp_done, 2)
            v.sem_inc(pv_done, 2)
            v.sem_inc(hid_done, 1)
            v.sem_inc(xt_done, 1)
            v.sem_inc(h_done, 2)
            v.sem_inc(y_done, 1)
            v.sem_inc(y_full, 2)
            v.sem_inc(xt_full, 2)

            class Order:

                def __init__(self, s, n, it):
                    self.s, self.n, self.it, self.k = s, n, it, 0

                def __call__(self, ins):
                    self.k += 1
                    ins.then_inc(self.s, 1)
                    v.wait_ge(self.s, self.it * self.n + self.k)

            def ln_stats(src, link, var_s):
                v.sem_inc(v_paced, 1)
                for t in range(TB):
                    ins = v.bn_stats(stats[:, t, :], src(t))
                link(ins)
                v.sem_inc(v_paced, 1)
                for t in range(TB):
                    ins = v.bn_aggr(mv[:, t, :], stats[:, t, :])
                link(ins)
                v.tensor_scalar(veps[:, :], mv[:, :, 1], EPS, None, ALU.add).then_inc(var_s, 1)

            def ln_apply(src, dst, rs_s, value, done):
                v.wait_ge(rs_s, value)
                for t in range(TB):
                    ins = v.tensor_scalar(dst(t), src(t), mv[:, t, 0:1], rstd[:, t:t + 1], ALU.subtract, ALU.mult)
                ins.then_inc(done, 1)

            def layernorm(src, dst, link, var_s, rs_s, value, done):
                ln_stats(src, link, var_s)
                ln_apply(src, dst, rs_s, value, done)

            o0 = Order(l0, 0, 0)

            def zero_keys(a, z):
                for i in range(a, z):
                    v.tensor_copy(KP[:, i // 4, i % 4, :], zero[:, 0:SEQ])

            def first_norm(b):
                dst = (xn, O)[b % 2]
                v.wait_ge(rs0, min(b, 1) + 1)
                if b >= 2:
                    v.wait_ge(tp0, b - 1)
                for t in range(b * TB, (b + 1) * TB):
                    ins = v.tensor_scalar(dst[:, t % TB, :], X[:, t, :], mv0[:, t, 0:1], rstd0[:, t:t + 1],
                                          ALU.subtract, ALU.mult)
                ins.then_inc(xn0, 1)

            v.wait_ge(setup, 1)
            zero_keys(0, 3)
            for ts in (range(0, TB), range(TB, NT)):
                if ts[0]:
                    zero_keys(3, 8)
                    v.memset(MX[:, :, :, :].bitcast(F32), 0.0)
                    first_norm(0)
                for t in ts:
                    if t % TB == 0:
                        v.wait_ge(x_in[t // TB], 16)
                        v.sem_inc(v_paced, 1)
                    ins = v.bn_stats(stats0[:, t, :], X[:, t, :])
                o0(ins)
                v.sem_inc(v_paced, 1)
                for t in ts:
                    ins = v.bn_aggr(mv0[:, t, :], stats0[:, t, :])
                o0(ins)
                c = slice(ts[0], ts[-1] + 1)
                v.tensor_scalar(veps0[:, c], mv0[:, c, 1], EPS, None, ALU.add).then_inc(var0, 1)

            NLA = 2 * NG
            NLT = 15

            def make_parts(b, g):
                u0 = g * RSU
                slot = u0 % 2
                v.wait_ge(parts, b * 2 * NG + 2 * g + 2)
                v.scalar_tensor_tensor(out=QS[:, g % 2, :], in0=rq[:, :].bitcast(F32), scalar=q_part,
                                       in1=ps[:, 2 * slot, :], op0=ALU.mult, op1=ALU.add)
                v.scalar_tensor_tensor(out=KS[:, g % 2, :], in0=rk[:, :].bitcast(F32), scalar=k_part,
                                       in1=ps[:, 2 * slot + 1, :], op0=ALU.mult, op1=ALU.add).then_inc(rs_free, 1)

            def row_max(b, g, n):
                t, heads = ROWN[n]
                use = g * RSU + 1 + n
                slot = use % 2
                v.wait_ge(rs_full, b * NG * RSU + use + 1)
                if len(heads) == 2:
                    scores = ps[:, 2 * slot:2 * slot + 2, 0:(t + 1) * P]
                else:
                    scores = ps[:, 2 * slot:2 * slot + 2, :].rearrange("p a n -> p (a n)")[:, 0:4 * (t + 1) * P]
                    scores = scores.rearrange("p (i n) -> p i n", i=4)
                v.tensor_reduce(mx[:, t, heads[0]:heads[-1] + 1], scores, AXX, ALU.max).then_inc(rs_free, 1)

            def minus_max(b, g, link):
                v.wait_ge(rs_free, b * NG * RSU + (g + 1) * RSU + 2)
                link(v.tensor_scalar(MX[:, :, :, 24], mx[:, :, :], -1.0, None, ALU.mult))
                v.scalar_tensor_tensor(out=MX[:, :, :, 25], in0=mx[:, :, :], scalar=-1.0,
                                       in1=MX[:, :, :, 24].bitcast(F32), op0=ALU.mult,
                                       op1=ALU.subtract).then_inc(mx_done, 1)

            def add_max(b, g):
                v.wait_ge(m_full, b * NM + MXU[g] + 1)
                v.tensor_tensor(QM[:, g % 2, :], QS[:, g % 2, :].bitcast(F32), tp_bank, ALU.add).then_inc(m_done, 1)

            def attention(b, tail, following):
                link = Order(lA, NLA, b)

                def normalise(g):
                    v.wait_ge(m_full, b * NM + OU[g] + 1)
                    o = tp_bank.rearrange("p (t i k) -> p t i k", t=TB, i=4)
                    rd = rden[:, :].rearrange("p (t i) -> p t i", t=TB)
                    link(v.reciprocal(rd, o[:, :, :, DK]))
                    for t in range(TB):
                        ins = v.tensor_tensor(
                            O[:, t, g * 32:(g + 1) * 32].rearrange("p (i k) -> p i k", k=DK), o[:, t, :, 0:DK],
                            rd[:, t, :].rearrange("p (i a) -> p i a", a=1).to_broadcast([P, 4, DK]), ALU.mult)
                    ins.then_inc(m_done, 1)

                minus_max(b, 0, link)
                add_max(b, 0)
                for g in range(NG):
                    unit = (b, g + 1) if g < NG - 1 else (b + 1, 0) if following else None
                    if unit:
                        make_parts(*unit)
                    for n in range(-1, len(ROWN)):
                        if unit and n >= 0:
                            row_max(*unit, n)
                        if n == 3 and g:
                            normalise(g - 1)
                        if tail and (g, n) in TAIL_AT:
                            for name in TAIL_AT[g, n]:
                                tail(name)
                    if g < NG - 1:
                        minus_max(b, g + 1, link)
                        add_max(b, g + 1)
                normalise(NG - 1)
                assert link.k == NLA, link.k

            TAIL_AT = {(0, -1): ("turn",), (0, 3): ("add",), (1, -1): ("stats",), (1, 0): ("norm",), (1, 3): ("turn2",),
                       (2, -1): ("choose",), (2, 3): ("rank",), (3, -1): ("place",)}

            def tail_of(b):
                link = Order(lT, NLT, b)

                def xt(t):
                    return X[:, bass.ds(b * TB + t, 1), :].rearrange("p a n -> p (a n)")

                def piece(name):
                    parts_of[name]()

                def turn():
                    v.wait_ge(e_full, b * 5 + 1)
                    v.tensor_copy(OT[:, :], tp_bank).then_inc(e_done, 1)

                def add():
                    v.wait_ge(e_full, b * 5 + 2)
                    xb = X[:, bass.ts(b, TB), :]
                    v.tensor_tensor(xb, tiles(tp_bank), xb, ALU.add).then_inc(e_done, 1)

                def stats_():
                    v.wait_ge(e_done, b * 5 + 2)
                    ln_stats(xt, link, varA)

                def norm():
                    v.wait_ge(scattered, b * 16 * TOPK * TB)
                    ln_apply(xt, lambda t: xn[:, t, :], rsA, b + 1, xnA)

                def turn2():
                    v.wait_ge(e_full, b * 5 + 3)
                    v.tensor_copy(xn2T[:, :], tp_bank).then_inc(e_done, 1)

                def choose():
                    v.wait_ge(e_full, b * 5 + 4)
                    v.tensor_copy(lg[:, :, :], tp_bank[:, 0:TB * E].rearrange("p (t e) -> p t e", e=E)).then_inc(e_done, 1)
                    v.wait_ge(e_done, b * 5 + 4)
                    v.sem_inc(v_paced, 1)
                    for t in range(TB):
                        ins = v.max(top[:, t, :], lg[:, t, :])
                    link(ins)
                    v.sem_inc(v_paced, 1)
                    for t in range(TB):
                        ins = v.max_index(topi[:, t, :], top[:, t, :], lg[:, t, :])
                    link(ins)
                    v.tensor_tensor(dl[:, :], top[:, :, 1], top[:, :, 0], ALU.subtract).then_inc(dl_done, 1)
                    link(v.tensor_copy(topf[:, :].rearrange("p (t k) -> p t k", k=2), topi[:, :, 0:2]))
                    link(v.tensor_tensor(oh[:, :, :],
                                         iota8.rearrange("p (a e) -> p a e", a=1).to_broadcast([P, 8, 8]),
                                         topf[:, :].rearrange("p (n a) -> p n a", a=1).to_broadcast([P, 8, 8]),
                                         ALU.is_equal))
                    v.tensor_copy(ohb[:, :, :], oh[:, :, :]).then_inc(oh_done, 1)

                def ranks():
                    v.wait_ge(e_full, b * 5 + 5)
                    v.scalar_tensor_tensor(out=sel[:, :, :], in0=tp_bank[:, 0:64].rearrange("p (n e) -> p n e", e=8),
                                           scalar=float(CAP), in1=oh[:, :, :], op0=ALU.is_le, op1=ALU.mult)
                    v.tensor_tensor(rank[:, :, :].rearrange("p (t k) e -> p t (k e)", k=2),
                                    tp_bank[:, 0:64].rearrange("p (t n) -> p t n", n=16),
                                    slot_base.rearrange("p (a n) -> p a n", a=1).to_broadcast([P, TB, 16]),
                                    ALU.add).then_inc(e_done, 1)

                def place():
                    v.wait_ge(e_done, b * 5 + 5)
                    v.tensor_reduce(keep[:, :], sel[:, :, :], AXX, ALU.add)
                    link(v.tensor_tensor(rank[:, :, :], rank[:, :, :], oh[:, :, :], ALU.mult))
                    link(v.tensor_reduce(pos[:, :], rank[:, :, :], AXX, ALU.add))
                    db = dump_row[:, bass.ts(b, 2 * TB)]
                    v.tensor_tensor(posG[:, bass.ts(b, 2 * TB)], pos[:, :], keep[:, :], ALU.mult)
                    link(v.tensor_tensor(pos2[:, :], pos[:, :], db, ALU.subtract))
                    link(v.tensor_tensor(pos2[:, :], pos2[:, :], keep[:, :], ALU.mult))
                    v.tensor_tensor(posS[:, :], pos2[:, :], db, ALU.add).then_inc(pos_done, 1)
                    link(v.tensor_reduce(here[:, :], oh[:, :, :].rearrange("p (t k) e -> p (k e) t", k=2), AXX, ALU.add))
                    link(v.tensor_tensor(seen[:, :], seen[:, :], here[:, :], ALU.add))
                    v.tensor_copy(seenb[:, :], seen[:, :])
                    v.wait_ge(ex_done, b + 1)
                    link(v.tensor_scalar(w1t[:, :], ex[:, :], 1.0, None, ALU.add))
                    link(v.reciprocal(w1t[:, :], w1t[:, :]))
                    wb = wts[:, bass.ts(b, 2 * TB)].rearrange("p (t k) -> p t k", k=2)
                    kb = keep[:, :].rearrange("p (t k) -> p t k", k=2)
                    v.tensor_tensor(wb[:, :, 0], w1t[:, :], kb[:, :, 0], ALU.mult)
                    link(v.tensor_tensor(w1t[:, :], w1t[:, :], ex[:, :], ALU.mult))
                    v.tensor_tensor(wb[:, :, 1], w1t[:, :], kb[:, :, 1], ALU.mult)
                    assert link.k == NLT, link.k

                parts_of = {"turn": turn, "add": add, "stats": stats_, "norm": norm, "turn2": turn2, "choose": choose,
                            "rank": ranks, "place": place}
                return piece

            first_norm(1)
            first_norm(2)
            v.wait_ge(par_in, 32)
            make_parts(0, 0)
            first_norm(3)
            for n in range(len(ROWN)):
                row_max(0, 0, n)
            attention(0, None, True)
            with v.Fori(1, NB - 1) as b:
                attention(b, tail_of(b - 1), True)
            attention(NB - 1, tail_of(NB - 2), False)
            last = tail_of(NB - 1)
            for names in TAIL_AT.values():
                for name in names:
                    last(name)

            v.wait_ge(w1_in, 16 * 23)

            def store_rows(x, s):
                v.wait_ge(xt_full, x + 3)
                v.tensor_copy(XST[:, s, 0:512], bank[6])
                v.tensor_copy(XST[:, s, 512:SLOTS], bank[7][:, 0:P]).then_inc(xt_done, 1)

            def add_b2(x, s, n):
                v.wait_ge(y_full, x + 3)
                v.wait_ge(ys_out[s], n * 16)
                b2 = rows[:, bass.ds(x + ROW["eb2_0"], 1), :]
                v.tensor_tensor(YS[:, s, 0:4, :], tiles(bank[4]), b2.to_broadcast([P, 4, P]), ALU.add)
                v.tensor_tensor(YS[:, s, 4:5, :], tiles(bank[5][:, 0:P]), b2, ALU.add).then_inc(y_done, 1)

            store_rows(0, 0)
            with v.Fori(0, E // 2 - 1) as it:
                store_rows(it * 2 + 1, 1)
                add_b2(it * 2, 0, it)
                store_rows(it * 2 + 2, 0)
                add_b2(it * 2 + 1, 1, it)
            store_rows(E - 1, 1)
            add_b2(E - 2, 0, E // 2 - 1)
            add_b2(E - 1, 1, E // 2 - 1)

            def prepare(c, ln, link):
                def tile_x(t):
                    return X[:, bass.ds(c * TB + t, 1), :].rearrange("p a n -> p (a n)")

                def combine():
                    v.wait_ge(rows_here, c)
                    for k in range(2):
                        for t in range(TB):
                            xt = tile_x(t)
                            gt = G[:, bass.ds(c * 2 * TB + (2 * t + k), 1), :].rearrange("p a n -> p (a n)")
                            wt = wts[:, bass.ds(c * 2 * TB + (2 * t + k), 1)]
                            ins = v.scalar_tensor_tensor(out=xt, in0=gt, scalar=wt, in1=xt, op0=ALU.mult, op1=ALU.add)
                        link(ins)

                def stats1():
                    ln_stats(tile_x, link, varC)

                def apply1(first=isinstance(c, int) and c == 0):
                    if not first:
                        v.wait_ge(ubo_done, c)
                    ln_apply(tile_x, lambda t: u[:, t, :], rsC, ln + 1, u_in)

                def stats2():
                    v.wait_ge(u_in, c + 1)
                    ln_stats(lambda t: u[:, t, :], link, varC)

                def apply2():
                    ln_apply(lambda t: u[:, t, :], lambda t: xp[:, t, :], rsC, ln + 2, lnC)

                return [combine, stats1, apply1, stats2, apply2]

            def attend(c, f, link):
                fb = f % 2
                v.wait_ge(qkvg, c * 4 * LF + 4 * f + 2)
                v.wait_ge(v_done, c * LF + f + 1)
                v.scalar_tensor_tensor(out=kv[:, :], in0=bank[1], scalar=cols[:, COL["bk"] + f:COL["bk"] + f + 1],
                                       in1=vs[:, fb, :], op0=ALU.add, op1=ALU.mult).then_inc(k_done, 1)
                v.wait_ge(k_done, c * LF + f + 1)
                link(v.tensor_tensor_scan(st[:, fb, :], decay[:, f:f + 1].to_broadcast([P, SEQ]), kv[:, :], 0.0,
                                          ALU.mult, ALU.add))
                v.wait_ge(qkvg, c * 4 * LF + 4 * f + 4)
                v.wait_ge(g_done, c * LF + f + 1)
                v.scalar_tensor_tensor(out=qg[:, fb, :], in0=bank[3], scalar=cols[:, COL["bq"] + f:COL["bq"] + f + 1],
                                       in1=gs[:, fb, :], op0=ALU.add, op1=ALU.mult).then_inc(q_done, 1)
                v.wait_ge(q_done, c * LF + f + 1)
                v.scalar_tensor_tensor(out=oT[:, f, :], in0=qg[:, fb, :], scalar=0.125, in1=st[:, fb, :],
                                       op0=ALU.mult, op1=ALU.mult).then_inc(o_ready, 1)

            def residual(c, row, ln, link):
                v.wait_ge(row_full, row)
                v.wait_ge(ubo_done, c + 1)
                v.tensor_tensor(r[:, :, :], tiles(bank[5]), ubo[:, :, :], ALU.add).then_inc(row_done, 1)
                v.wait_ge(row_done, row)
                ln_stats(lambda t: r[:, t, :], link, varC)
                v.tensor_tensor(rx[:, :, :], r[:, :, :], X[:, bass.ts(c, TB), :], ALU.add).then_inc(rx_in, 1)
                ln_apply(lambda t: r[:, t, :], lambda t: xn[:, t, :], rsC, ln + 1, lnC)

            def layer1(b, attn, prep, link):
                def second(c, row):
                    xc = X[:, bass.ts(c, TB), :]
                    v.wait_ge(row_full, row)
                    v.wait_ge(rx_done, c + 1)
                    v.tensor_tensor(xc, tiles(bank[5]), rx[:, :, :], ALU.add).then_inc(row_done, 1)
                    v.wait_ge(row_done, row)
                    ln_stats(lambda t: X[:, bass.ds(c * TB + t, 1), :].rearrange("p a n -> p (a n)"), link, varC)

                def second_apply(c):
                    ln_apply(lambda t: X[:, bass.ds(c * TB + t, 1), :].rearrange("p a n -> p (a n)"),
                             lambda t: xn[:, t, :], rsC, VAR(c), lnC)

                last = not attn
                early = attn and not prep
                if attn:
                    attend(b + 1, 1, link)
                if not last:
                    second(b, b * 3 + 2)
                if attn:
                    attend(b + 1, 2, link)
                if not last:
                    second_apply(b)
                if attn:
                    for f in range(3, LF):
                        attend(b + 1, f, link)
                for f in range(FF):
                    v.wait_ge(a_full, b * 2 * FF + 2 * f + 2)
                    v.wait_ge(sl_done, b * FF + f + 1)
                    v.scalar_tensor_tensor(out=hA[:, f, :], in0=bank[2 + f % 2],
                                           scalar=cols[:, COL["w2_s"] + f:COL["w2_s"] + f + 1],
                                           in1=sl[:, f % 2, :], op0=ALU.mult, op1=ALU.mult).then_inc(a_done, 1)
                if attn:
                    residual(b + 1, b * 3 + 3, VAR(b), link)
                if prep:
                    for piece in prepare(b + 2, VAR(b) + 1, link):
                        piece()
                if early:
                    second(NB - 1, ROWS_OUT(b) - 1)
                    second_apply(NB - 1)
                v.wait_ge(row_full, ROWS_OUT(b))
                v.wait_ge(out_done, b * 16)
                v.tensor_tensor(yo[:, :, :], tiles(bank[5]),
                                rows[:, ROW["w3_s"]:ROW["w3_s"] + 1, :].to_broadcast([P, TB, P]),
                                ALU.mult).then_inc(row_done, 1)
                v.wait_ge(row_done, ROWS_OUT(b))
                v.tensor_tensor(yo[:, :, :], yo[:, :, :], X[:, bass.ts(b, TB), :], ALU.add).then_inc(y_out, 1)
                if prep:
                    attend(b + 2, 0, link)

            link = Order(lP, 0, 0)
            for t in range(TB):
                v.wait_ge(rows_in[t], 32)
                for k in range(2):
                    c = 2 * t + k
                    link(v.scalar_tensor_tensor(out=X[:, t, :], in0=G[:, c, :], scalar=wts[:, c:c + 1],
                                                in1=X[:, t, :], op0=ALU.mult, op1=ALU.add))
            for piece in prepare(0, 0, link)[1:]:
                piece()
            pieces = prepare(1, 2, link)
            for f in range(LF):
                attend(0, f, link)
                if f in (3, 5):
                    pieces.pop(0)()
            for piece in pieces:
                piece()
            residual(0, 1, 4, link)
            attend(1, 0, link)
            NLC = LF + 2 + 2 + 2 + 4
            with v.Fori(0, NB - 2) as b:
                link = Order(lC, NLC, b)
                layer1(b, True, True, link)
                assert link.k == NLC, link.k
            link = Order(lE, 0, 0)
            layer1(NB - 2, True, False, link)
            layer1(NB - 1, False, False, link)

        @block.tensor
        def _(pe):
            pe.wait_ge(par_in, 32)
            pe.wait_ge(w0_in, 80)

            def first_turn(b):
                src = (xn, O)[b % 2]
                pe.wait_ge(xn0, b + 1)
                if b >= 2:
                    pe.wait_ge(tc0, b - 1)
                for t in range(TB):
                    mm = pe.transpose(bank[4 + b % 2][:, t * P:(t + 1) * P], src[:, t, :], ident)
                mm.then_inc(tp0, 1)
                pe.wait_ge(tc0, b + 1)
                if b >= 2:
                    pe.wait_ge(vc0, b - 1)
                for t in range(TB):
                    c = (b * TB + t) * P
                    mm = pe.matmul(bank[6 + b % 2][:, t * P:(t + 1) * P], xnT[:, c:c + P], wv[:, :], start=True, stop=True)
                mm.then_inc(vp0, 1)

            def tail_of(b):
                def piece(name):
                    if name == "turn":
                        for t in range(TB):
                            mm = pe.transpose(tp_bank[:, t * P:(t + 1) * P], O[:, t, :], ident)
                    elif name == "wo":
                        pe.wait_ge(e_done, b * 5 + 1)
                        for t in range(TB):
                            mm = pe.matmul(tp_bank[:, t * P:(t + 1) * P], OT[:, t * P:(t + 1) * P], wo[:, :],
                                           start=True, stop=True)
                    elif name == "turn2":
                        pe.wait_ge(xnA, b + 1)
                        for t in range(TB):
                            mm = pe.transpose(tp_bank[:, t * P:(t + 1) * P], xn[:, t, :], ident)
                    elif name == "logits":
                        pe.wait_ge(e_done, b * 5 + 3)
                        for t in range(TB):
                            mm = pe.matmul(tp_bank[:, t * E:(t + 1) * E], xn2T[:, t * P:(t + 1) * P], wr[:, :],
                                           start=True, stop=True)
                    else:
                        pe.wait_ge(oh_done, b + 1)
                        pe.wait_ge(e_done, b * 5 + 4)
                        for t in range(TB):
                            c = slice(t * 16, (t + 1) * 16)
                            for before in range(t + 1):
                                pe.matmul(tp_bank[:, c], (trib if before == t else onesb)[:, :],
                                          ohb[:, 2 * before:2 * before + 2, :].rearrange("p k e -> p (k e)"),
                                          start=(before == 0), stop=False)
                            mm = pe.matmul(tp_bank[:, c], onesb[:, :], seenb[:, :], start=False, stop=True)
                    mm.then_inc(e_full, 1)
                return piece

            def slot_of(b, use):
                pe.wait_ge(rs_free, b * NG * RSU + use + 1)
                return use % 2

            def project(b, g):
                s = slot_of(b, g * RSU)
                x = xnT[:, bass.ts(b, SEQ)]
                pe.matmul(ps[:, 2 * s, :], WQS[:, 4 * g:4 * g + 4, :, :].rearrange("p h c k -> p (h c k)"), x,
                          start=True, stop=True)
                pe.matmul(ps[:, 2 * s + 1, :], WKS[:, 4 * g:4 * g + 4, :, :].rearrange("p h c k -> p (h c k)"), x,
                          start=True, stop=True).then_inc(rs_full, 1)

            def row_scores(b, g, n):
                t, heads = ROWN[n]
                s = slot_of(b, g * RSU + 1 + n)
                if n == 0:
                    pe.wait_ge(rs_free, b * NG * RSU + g * RSU + 3)
                if n in (0, 2):
                    pe.wait_ge(padded, (b * NG + g) * 4 + n + 2)
                both = ps[:, 2 * s:2 * s + 2, :].rearrange("p a n -> p (a n)")
                for a, i in enumerate(heads):
                    at = a * (t + 1) * P if len(heads) == 4 else a * SEQ
                    pe.matmul(both[:, at:at + (t + 1) * P], QS[:, g % 2, t * P:(t + 1) * P],
                              KP[:, g % 2, i, 0:(t + 1) * P], start=True, stop=False)
                    mm = pe.matmul(both[:, at + t * P:at + (t + 1) * P], identb[:, :], maskb[:, :],
                                   start=False, stop=True)
                mm.then_inc(rs_full, 1)

            def attention(b, tail, following):
                def claim(m, e):
                    pe.wait_ge(m_done, b * NM + m)
                    if tail:
                        pe.wait_ge(e_done, (b - 1) * 5 + e)

                def turn_max(g):
                    claim(MXU[g], (0, 2, 3, 5)[g])
                    pe.wait_ge(mx_done, b * NG + g + 1)
                    for t in range(TB):
                        mm = pe.transpose(tp_bank[:, t * P:(t + 1) * P],
                                          MX[:, t, :, :].rearrange("p i c -> p (i c)").bitcast(F32), ident)
                    mm.then_inc(m_full, 1)

                def key_scores(g, i, cs):
                    for c in cs:
                        n = (g * 4 + i) * NK + c
                        pe.wait_ge(exp_done, b * H * NK + n + 1)
                        for j in KC[c]:
                            at = OFF[j] - OFF[KC[c][0]]
                            pe.matmul(ps[:, 4 + n % 2, at:at + SEQ - j * P], KP[:, g % 2, i, j * P:(j + 1) * P],
                                      QM[:, g % 2, j * P:SEQ], start=True, stop=False)
                            mm = pe.matmul(ps[:, 4 + n % 2, at:at + P], identb[:, :], maskTb[:, :],
                                           start=False, stop=True)
                        mm.then_inc(ts_full, 1)

                def values(g, p, js):
                    if 0 in js:
                        pe.wait_ge(exp_done, b * H * NK + (4 * g + 2 * p + 2) * NK + 2)
                        if p == 0:
                            pe.wait_ge(v_ready, b + 1)
                            pe.wait_ge(og_done, b * NG + g)
                    for j in js:
                        for i in (2 * p, 2 * p + 1):
                            mm = pe.matmul(bank[6][32 * i:32 * i + 32, j * P:SEQ], V[:, j * H + g * 4 + i, :],
                                           PT[:, i, OFF[j]:OFF[j + 1]], start=(j == 0), stop=(j == TB - 1),
                                           skip_group_check=True)
                    if TB - 1 in js:
                        mm.then_inc(pv_done, 1)

                def turn_out(g):
                    claim(OU[g], (2, 4, 5, 5)[g])
                    pe.wait_ge(og_done, b * NG + g + 1)
                    for t in range(TB):
                        mm = pe.transpose(tp_bank[:, t * P:(t + 1) * P], OG[:, t * P:(t + 1) * P], ident)
                    mm.then_inc(m_full, 1)

                def piece(m, e, name):
                    if tail:
                        claim(m, e)
                        tail(name)

                def ahead(g):
                    return (b, g + 1) if g < NG - 1 else (b + 1, 0) if following else None

                project(*ahead(0))
                turn_max(0)
                for g in range(NG):
                    unit = ahead(g)
                    pe.wait_ge(m_done, b * NM + MXU[g] + 1)
                    for i in range(4):
                        before = (g, 0) if i >= 2 else (g - 1, 1) if g else None
                        if i == 1 and g in (0, 2):
                            piece(*((1, 0, "turn") if g == 0 else (4, 3, "logits")))
                        if i == 3:
                            if g:
                                turn_out(g - 1)
                            if g < 3:
                                piece(*((1, 1, "wo"), (3, 2, "turn2"), (5, 4, "ranks"))[g])
                        for half in range(2):
                            key_scores(g, i, ((0, 1), (2,))[half])
                            if unit and i:
                                row_scores(*unit, 2 * i + half - 2)
                        if i == 3 and g < NG - 1:
                            if ahead(g + 1):
                                project(*ahead(g + 1))
                            turn_max(g + 1)
                        if before:
                            values(*before, (0,) if i % 2 == 0 else (1, 2, 3))
                values(NG - 1, 1, range(TB))
                turn_out(NG - 1)

            first_turn(0)
            first_turn(1)
            pe.wait_ge(setup, 13)
            project(0, 0)
            first_turn(2)
            first_turn(3)
            pe.wait_ge(bfc, 4)
            for n in range(len(ROWN)):
                row_scores(0, 0, n)
            pe.wait_ge(vc0, NB)
            attention(0, None, True)
            with pe.Fori(1, NB - 1) as b:
                attention(b, tail_of(b - 1), True)
            attention(NB - 1, tail_of(NB - 2), False)
            last = tail_of(NB - 1)
            pe.wait_ge(m_done, NB * NM)
            for name in ("turn", "wo", "turn2", "logits", "ranks"):
                last(name)

            pe.wait_ge(m_done, NB * NM)
            pe.wait_ge(e_done, NB * 5)

            def turn_rows(x, s, n):
                pe.wait_ge(xs_in[s], n * 16)
                pe.wait_ge(xt_done, x + 1)
                for j in range(ST):
                    mm = pe.transpose(bank[6 + j // 4][:, (j % 4) * P:(j % 4 + 1) * P], XS[:, s, j, :], ident)
                mm.then_inc(xt_full, 1)

            def expert(x, s, n, following):
                pe.wait_ge(xt_done, x + 2)
                pe.wait_ge(ew_in[s], n * 32)
                for f in range(FF):
                    pe.wait_ge(h_done, x * FF + f + 1)
                    for a in range(2):
                        mm = pe.matmul(ps[:, 2 * (f % 2) + a, 0:HALF], W1[:, s, f * P:(f + 1) * P],
                                       XST[:, s, a * HALF:(a + 1) * HALF], start=True, stop=True)
                    mm.then_inc(h_full, 1)
                if following:
                    turn_rows(x + 1, 1 - s, n + s)
                pe.wait_ge(h_done, x * FF + FF + 2)
                pe.wait_ge(y_done, x + 1)
                for j in range(ST):
                    for f in range(FF):
                        mm = pe.matmul(bank[4 + j // 4][:, (j % 4) * P:(j % 4 + 1) * P], HT[:, s, f, j * P:(j + 1) * P],
                                       W2[:, s, f, :], start=(f == 0), stop=(f == FF - 1))
                mm.then_inc(y_full, 1)

            turn_rows(0, 0, 1)
            with pe.Fori(0, E // 2 - 1) as it:
                expert(it * 2, 0, it + 1, True)
                expert(it * 2 + 1, 1, it + 1, True)
            expert(E - 2, 0, E // 2, True)
            expert(E - 1, 1, E // 2, False)

            pe.wait_ge(w1_in, 16 * 23)
            pe.wait_ge(y_done, E + 1)

            def turn(n, src):
                pe.wait_ge(lnC, n)
                pe.wait_ge(t_done, n - 1)
                for t in range(TB):
                    mm = pe.transpose(bank[4][:, t * P:(t + 1) * P], src[:, t, :], ident)
                mm.then_inc(t_full, 1)

            def to_rows(row, src, w, n):
                pe.wait_ge(row_done, row - 1)
                for t in range(TB):
                    for f in range(n):
                        mm = pe.matmul(bank[5][:, t * P:(t + 1) * P], src[:, f, t * P:(t + 1) * P], w[:, f, :],
                                       start=(f == 0), stop=(f == n - 1))
                mm.then_inc(row_full, 1)

            def project1(c, f):
                for m, (n, done) in enumerate((("Wv", v_done), ("Wk", k_done), ("Wg", g_done), ("Wq", q_done))):
                    pe.wait_ge(done, c * LF + f)
                    pe.matmul(bank[m], lw[n][:, f * P:(f + 1) * P], aT[:, :], start=True, stop=True).then_inc(qkvg, 1)

            def layer1(b, attn, prep):
                def hidden(n, products):
                    pe.wait_ge(hid_done, b * 12 + n)
                    for i, (w, x) in enumerate(products):
                        mm = pe.matmul(bank[6 + n % 2], w, x, start=(i == 0), stop=(i == len(products) - 1))
                    mm.then_inc(hid_full, 1)

                last = not attn
                early = attn and not prep
                if not last:
                    pe.wait_ge(t_done, TURN(b) - 1)
                    for f in range(FF):
                        hidden(f, [(lw1[:, f * P:(f + 1) * P], aT2)])
                if attn:
                    project1(b + 1, 1)
                if not last:
                    pe.wait_ge(hid_done, b * 12 + 5)
                    to_rows(b * 3 + 2, hA, lw2, FF)
                if attn:
                    for f in range(2, TURN2_AT):
                        project1(b + 1, f)
                if not last:
                    turn(TURN(b), xn)
                if attn:
                    for f in range(TURN2_AT, LF):
                        project1(b + 1, f)
                pe.wait_ge(t_done, TURN(b))
                for f in range(FF):
                    if f >= 2:
                        pe.wait_ge(sl_done, b * FF + f - 1)
                        pe.wait_ge(a_done, b * FF + f - 1)
                    elif attn:
                        pe.wait_ge((v_done, k_done)[f], (b + 2) * LF)
                        pe.wait_ge((g_done, q_done)[f], (b + 2) * LF)
                    pe.matmul(bank[f % 2], fw1[:, f * P:(f + 1) * P], aT2, start=True, stop=True).then_inc(a_full, 1)
                    pe.matmul(bank[2 + f % 2], fw2[:, f * P:(f + 1) * P], aT2, start=True, stop=True).then_inc(a_full, 1)
                if attn:
                    pe.wait_ge(o_ready, (b + 2) * LF)
                    to_rows(b * 3 + 3, oT, lwo, LF)
                pe.wait_ge(a_done, b * FF + FF)
                for f in range(FF):
                    hidden(4 + f, [(fh1[:, c, f * P:(f + 1) * P], hA[:, c, :]) for c in range(FF)])
                if attn:
                    turn(TURN(b) + 1, xn)
                n = 8
                if early:
                    pe.wait_ge(t_done, TURN(b) + 1)
                    for f in range(FF):
                        hidden(8 + f, [(lw1[:, f * P:(f + 1) * P], aT2)])
                    pe.wait_ge(hid_done, b * 12 + 13)
                    to_rows(ROWS_OUT(b) - 1, oT, lw2, FF)
                    n = 12
                pe.wait_ge(hid_done, b * 12 + 9)
                for f in range(FF):
                    hidden(n + f, [(fh2[:, c, f * P:(f + 1) * P], hB[:, c, :]) for c in range(FF)])
                if early:
                    turn(TURN(NB - 1), xn)
                if prep:
                    turn(TURN(b) + 2, xp)
                pe.wait_ge(hid_done, b * 12 + n + 5)
                to_rows(ROWS_OUT(b), hA, fw3, FF)
                if prep:
                    pe.wait_ge(t_done, TURN(b) + 2)
                    project1(b + 2, 0)

            turn(1, xp)
            pe.wait_ge(t_done, 1)
            for f in range(LF):
                project1(0, f)
            pe.wait_ge(o_ready, LF)
            to_rows(1, oT, lwo, LF)
            turn(2, xp)
            pe.wait_ge(t_done, 2)
            project1(1, 0)
            turn(3, xn)
            with pe.Fori(0, NB - 2) as b:
                layer1(b, True, True)
            layer1(NB - 2, True, False)
            layer1(NB - 1, False, False)


def shape_constants():
    import numpy as np
    i = np.arange(P)
    later = i[None, :] > i[:, None]
    c = np.zeros((P, N_CONST), np.float32)
    c[:, 0:P] = np.eye(P)
    c[:, P:2 * P] = np.where(later, NEG, 0.0)
    c[:, 2 * P:3 * P] = np.where(later.T, NEG, 0.0)
    c[:, 3 * P:4 * P] = i[:, None] <= i[None, :]
    at = 4 * P
    for k in range(TOPK):
        for e in range(E):
            c[:, at + k * E + e] = e * SLOTS + k * CAP - 1
    at += 16
    for t in range(NT):
        for k in range(TOPK):
            c[:, at + 2 * t + k] = DUMP + k * NT * P + t * P + i
    at += 2 * NT
    c[:, at:at + 8] = np.arange(8)
    at += 8
    part = (i % 32) // 8
    c[:, at] = np.where(part == 2, -1.0, 0.0)
    c[:, at + 1] = np.where(part == 1, -1.0, np.where(part == 3, 1.0, 0.0))
    c[:, at + 2] = np.where(part == 3, 1.0, 0.0)
    return c


def kernel(**inputs):
    import numpy as np
    import concourse.bacc as _bacc
    from concourse.bass_utils import run_bass_kernel_spmd as _run

    a = {k: np.asarray(v) for k, v in inputs.items()}
    col = lambda x: x.reshape(-1, P).T
    dec = np.repeat(a["L1_attn_decay_logit"], LF * P // H)
    parts = [a["L1_attn_ln1_g"], a["L1_attn_ln1_b"], a["L1_attn_ln2_g"], a["L1_attn_ln2_b"], a["L1_attn_bq"],
             a["L1_attn_bk"], a["L1_attn_bv"], a["L1_attn_bg"], dec, a["L1_attn_b1"], a["L1_ffn_w1_s"],
             a["L1_ffn_w2_s"], a["L1_ffn_h1_s"], a["L1_ffn_h2_s"], a["L0_ffn_b1"]]
    arrays = {
        "x": a["L0_attn_x"].reshape(NT * P, P),
        "const": shape_constants(),
        "cols": np.concatenate([col(p) for p in parts], axis=1),
        "WQ": a["L0_attn_WQ"], "WK": a["L0_attn_WK"], "WV": a["L0_attn_WV"], "WO": a["L0_attn_WO"],
        "Wr": a["L0_ffn_Wr"], "eW1": a["L0_ffn_W1"].reshape(E * P, FF * P), "eW2": a["L0_ffn_W2"].reshape(E * FF * P, P),
        "eb2": a["L0_ffn_b2"], "bo": a["L1_attn_bo"], "b2": a["L1_attn_b2"], "w3_s": a["L1_ffn_w3_s"],
        "Wq": a["L1_attn_Wq"], "Wk": a["L1_attn_Wk"], "Wv": a["L1_attn_Wv"], "Wg": a["L1_attn_Wg"],
        "Wo": a["L1_attn_Wo"], "W1": a["L1_attn_W1"], "W2": a["L1_attn_W2"],
        "w1_w": a["L1_ffn_w1_w"].T, "w2_w": a["L1_ffn_w2_w"].T, "h1_w": a["L1_ffn_h1_w"].T,
        "h2_w": a["L1_ffn_h2_w"].T, "w3_w": a["L1_ffn_w3_w"].T,
    }
    arrays = {f"in_{k}": np.ascontiguousarray(v) for k, v in arrays.items()}
    nc = _bacc.Bacc("TRN2", target_bir_lowering=False, num_devices=1)
    d = {k[3:]: nc.dram_tensor(k, v.shape, mybir.dt.from_np(v.dtype), kind="ExternalInput").ap() for k, v in arrays.items()}
    d["out"] = nc.dram_tensor("out_dram", (NT * P, P), F32, kind="ExternalOutput").ap()
    build(nc, d)
    res = _run(nc, [arrays], core_ids=[0])
    return res.results[0]["out_dram"].reshape(NB, SEQ, P)
```
